# Optimizing a Trainium2 kernel written in Bass

```python
import numpy as np
import jax
import jax.numpy as jnp

def _softmax(x, axis=-1):
    return jax.nn.softmax(x, axis=axis)

def _gelu(x):
    return jax.nn.gelu(x, approximate=True)

def _silu(x):
    return jax.nn.silu(x)

def _sigmoid(x):
    return jax.nn.sigmoid(x)

def _layernorm(x, axis=-1, eps=1e-05):
    m = jnp.mean(x, axis=axis, keepdims=True)
    v = jnp.var(x, axis=axis, keepdims=True)
    return (x - m) / jnp.sqrt(v + eps)

def _scatter_add(tgt, idx, src, axis=0):
    return tgt.at[idx].add(src)

def _segment_sum(src, seg, n):
    return jax.ops.segment_sum(src, seg, n)
kernel_name = 'mk_gnn_preln_d4_gnn_r32_6ed1b3'

def setup_inputs(seed: int=0):
    np.random.seed(seed)
    _w = jnp.asarray

    def _rec_inputs():
        import jax
        import jax.numpy as jnp
        _gk = jax.random.key(seed)
        x = -0.000202 + 1 * jax.random.normal(jax.random.fold_in(_gk, 1), (3125, 128), jnp.float32)
        src = jax.random.randint(jax.random.fold_in(_gk, 2), (50000,), 0, 3125, jnp.int32)
        dst = jax.random.randint(jax.random.fold_in(_gk, 3), (50000,), 0, 3125, jnp.int32)
        _o = jnp.argsort(dst, stable=True)
        src = src[_o]
        dst = dst[_o]
        edge_attr_128 = 2.93046e-05 + 1.00006 * jax.random.normal(jax.random.fold_in(_gk, 12), (50000, 128), jnp.float32)
        edge_attr_16 = 0.000254156 + 0.999948 * jax.random.normal(jax.random.fold_in(_gk, 13), (50000, 16), jnp.float32)
        edge_attr_4 = 0.00132558 + 1.00026 * jax.random.normal(jax.random.fold_in(_gk, 14), (50000, 4), jnp.float32)
        return (x, src, dst, edge_attr_128, edge_attr_16, edge_attr_4)
    x, src, dst, edge_attr_128, edge_attr_16, edge_attr_4 = _rec_inputs()

    def _L0_gnn_setup():
        import jax, jax.numpy as jnp
        import numpy as np
        N, E, D_IN, D_OUT, H = (50000, 25000, 128, 128, 4)
        D_H = D_OUT // H
        key = jax.random.key(seed)
        ks = jax.random.split(key, 8)
        x = jax.random.normal(ks[0], (N, D_IN), dtype=jnp.float32)
        edge_index = jax.random.randint(ks[1], (2, E), 0, N)
        W = jax.random.normal(ks[2], (H, D_IN, D_H), dtype=jnp.float32) * (1.0 / np.sqrt(D_IN))
        att_src = jax.random.normal(ks[3], (H, D_H), dtype=jnp.float32) * 0.1
        att_dst = jax.random.normal(ks[4], (H, D_H), dtype=jnp.float32) * 0.1
        bias = jnp.zeros((H, D_H), dtype=jnp.float32)
        gamma = jnp.ones((D_OUT,), dtype=jnp.float32)
        beta = jnp.zeros((D_OUT,), dtype=jnp.float32)
        return dict(x=x, edge_index=edge_index, W=W, att_src=att_src, att_dst=att_dst, bias=bias, gamma=gamma, beta=beta)
    _L0_gnn_all = _L0_gnn_setup()
    _L0_gnn_in = {k: v for k, v in _L0_gnn_all.items() if k in ('W', 'att_src', 'att_dst', 'bias', 'gamma', 'beta')}
    del _L0_gnn_all

    def _L1_gnn_setup():
        import jax, jax.numpy as jnp
        import numpy as np
        N, E = (10000, 20000)
        IN_DIM, EDGE_DIM, OUT_DIM = (128, 128, 128)
        key = jax.random.key(seed)
        ks = jax.random.split(key, 9)
        s = 0.02
        return {'x': jax.random.normal(ks[0], (N, IN_DIM), dtype=jnp.float32), 'edge_index': jax.random.randint(ks[1], (2, E), 0, N, dtype=jnp.int64), 'edge_attr': jax.random.normal(ks[2], (E, EDGE_DIM), dtype=jnp.float32), 'We': jax.random.normal(ks[3], (EDGE_DIM, IN_DIM), dtype=jnp.float32) * s, 'be': jnp.zeros((IN_DIM,), dtype=jnp.float32), 'W1': jax.random.normal(ks[4], (2 * IN_DIM, OUT_DIM), dtype=jnp.float32) * s, 'b1': jnp.zeros((OUT_DIM,), dtype=jnp.float32), 'W2': jax.random.normal(ks[5], (OUT_DIM, OUT_DIM), dtype=jnp.float32) * s, 'b2': jnp.zeros((OUT_DIM,), dtype=jnp.float32)}
    _L1_gnn_all = _L1_gnn_setup()
    _L1_gnn_in = {k: v for k, v in _L1_gnn_all.items() if k in ('We', 'be', 'W1', 'b1', 'W2', 'b2')}
    del _L1_gnn_all

    def _L2_gnn_setup():
        import jax, jax.numpy as jnp
        import numpy as np
        N, E, D, H, HD, TD, ED, G = (30000, 15000, 128, 8, 16, 512, 4, 8)

        def group_norm(x, gamma, beta, num_groups=G, eps=1e-05):
            n, c = x.shape
            xr = x.reshape(n, num_groups, c // num_groups)
            mu = xr.mean(-1, keepdims=True)
            var = ((xr - mu) ** 2).mean(-1, keepdims=True)
            xn = (xr - mu) * jax.lax.rsqrt(var + eps)
            return xn.reshape(n, c) * gamma + beta

        def mesh_conv(x, src, dst, ea, w1, b1, g, bt, w2, b2):
            m = jnp.concatenate([x[dst], x[src], ea], axis=-1) @ w1 + b1
            m = jax.nn.silu(group_norm(m, g, bt))
            m = m @ w2 + b2
            n = x.shape[0]
            out = jax.ops.segment_sum(m, dst, num_segments=n)
            cnt = jax.ops.segment_sum(jnp.ones((dst.shape[0],), m.dtype), dst, num_segments=n)
            return out / jnp.clip(cnt, 1.0)[:, None]
        key = jax.random.key(seed)
        ks = jax.random.split(key, 32)
        inp = {}
        inp['x'] = jax.random.normal(ks[0], (N, D), jnp.float32)
        inp['edge_src'] = jax.random.randint(ks[1], (E,), 0, N, jnp.int32)
        inp['edge_dst'] = jax.random.randint(ks[2], (E,), 0, N, jnp.int32)
        inp['edge_attr'] = jax.random.normal(ks[3], (E, ED), jnp.float32)
        inp['t_emb'] = jax.random.normal(ks[4], (TD,), jnp.float32)
        s = 0.02
        inp['c1_w1'] = jax.random.normal(ks[5], (2 * D + ED, D)) * s
        inp['c1_b1'] = jnp.zeros((D,))
        inp['c1_g'] = jnp.ones((D,))
        inp['c1_bt'] = jnp.zeros((D,))
        inp['c1_w2'] = jax.random.normal(ks[6], (D, D)) * s
        inp['c1_b2'] = jnp.zeros((D,))
        inp['c2_w1'] = jax.random.normal(ks[7], (2 * D + ED, D)) * s
        inp['c2_b1'] = jnp.zeros((D,))
        inp['c2_g'] = jnp.ones((D,))
        inp['c2_bt'] = jnp.zeros((D,))
        inp['c2_w2'] = jax.random.normal(ks[8], (D, D)) * s
        inp['c2_b2'] = jnp.zeros((D,))
        inp['tm_w'] = jax.random.normal(ks[9], (TD, D)) * s
        inp['tm_b'] = jnp.zeros((D,))
        inp['n1_g'] = jnp.ones((D,))
        inp['n1_b'] = jnp.zeros((D,))
        inp['n2_g'] = jnp.ones((D,))
        inp['n2_b'] = jnp.zeros((D,))
        inp['qw'] = jax.random.normal(ks[10], (D, D)) * s
        inp['qb'] = jnp.zeros((D,))
        inp['kw'] = jax.random.normal(ks[11], (D, D)) * s
        inp['kb'] = jnp.zeros((D,))
        inp['vw'] = jax.random.normal(ks[12], (D, D)) * s
        inp['vb'] = jnp.zeros((D,))
        inp['ew'] = jax.random.normal(ks[13], (ED, H)) * s
        inp['eb'] = jnp.zeros((H,))
        inp['ow'] = jax.random.normal(ks[14], (D, D)) * s
        inp['ob'] = jnp.zeros((D,))
        inp['an_g'] = jnp.ones((D,))
        inp['an_b'] = jnp.zeros((D,))
        return inp
    _L2_gnn_all = _L2_gnn_setup()
    _L2_gnn_in = {k: v for k, v in _L2_gnn_all.items() if k in ('t_emb', 'c1_w1', 'c1_b1', 'c1_g', 'c1_bt', 'c1_w2', 'c1_b2', 'c2_w1', 'c2_b1', 'c2_g', 'c2_bt', 'c2_w2', 'c2_b2', 'tm_w', 'tm_b', 'n1_g', 'n1_b', 'n2_g', 'n2_b', 'qw', 'qb', 'kw', 'kb', 'vw', 'vb', 'ew', 'eb', 'ow', 'ob', 'an_g', 'an_b')}
    del _L2_gnn_all

    def _L3_gnn_setup():
        import jax, jax.numpy as jnp
        import numpy as np
        N_NODES = 3125
        N_EDGES = 25000
        D_IN = 128
        D_OUT = 128
        E_DIM = 16
        key = jax.random.key(seed)
        k1, k2, k3, k4, k5 = jax.random.split(key, 5)
        x = jax.random.normal(k1, (N_NODES, D_IN), dtype=jnp.float32)
        edge_index = jax.random.randint(k2, (2, N_EDGES), 0, N_NODES, dtype=jnp.int64)
        edge_attr = jax.random.normal(k3, (N_EDGES, E_DIM), dtype=jnp.float32)
        W = jax.random.uniform(k4, (D_IN, D_OUT), dtype=jnp.float32, minval=-1.0, maxval=1.0) * float(np.sqrt(6.0 / (D_IN + D_OUT)))
        edge_w = jax.random.uniform(k5, (E_DIM, D_OUT), dtype=jnp.float32, minval=-1.0, maxval=1.0) * float(np.sqrt(6.0 / (E_DIM + D_OUT)))
        b = jnp.zeros((D_OUT,), dtype=jnp.float32)
        return {'x': x, 'edge_index': edge_index, 'edge_attr': edge_attr, 'W': W, 'edge_w': edge_w, 'b': b}
    _L3_gnn_all = _L3_gnn_setup()
    _L3_gnn_in = {k: v for k, v in _L3_gnn_all.items() if k in ('W', 'edge_w', 'b')}
    del _L3_gnn_all
    return {'x': x, 'src': src, 'dst': dst, 'edge_attr_128': edge_attr_128, 'edge_attr_16': edge_attr_16, 'edge_attr_4': edge_attr_4, 'L0_gnn_W': _L0_gnn_in['W'], 'L0_gnn_att_src': _L0_gnn_in['att_src'], 'L0_gnn_att_dst': _L0_gnn_in['att_dst'], 'L0_gnn_bias': _L0_gnn_in['bias'], 'L0_gnn_gamma': _L0_gnn_in['gamma'], 'L0_gnn_beta': _L0_gnn_in['beta'], 'L1_gnn_We': _L1_gnn_in['We'], 'L1_gnn_be': _L1_gnn_in['be'], 'L1_gnn_W1': _L1_gnn_in['W1'], 'L1_gnn_b1': _L1_gnn_in['b1'], 'L1_gnn_W2': _L1_gnn_in['W2'], 'L1_gnn_b2': _L1_gnn_in['b2'], 'L2_gnn_t_emb': _L2_gnn_in['t_emb'], 'L2_gnn_c1_w1': _L2_gnn_in['c1_w1'], 'L2_gnn_c1_b1': _L2_gnn_in['c1_b1'], 'L2_gnn_c1_g': _L2_gnn_in['c1_g'], 'L2_gnn_c1_bt': _L2_gnn_in['c1_bt'], 'L2_gnn_c1_w2': _L2_gnn_in['c1_w2'], 'L2_gnn_c1_b2': _L2_gnn_in['c1_b2'], 'L2_gnn_c2_w1': _L2_gnn_in['c2_w1'], 'L2_gnn_c2_b1': _L2_gnn_in['c2_b1'], 'L2_gnn_c2_g': _L2_gnn_in['c2_g'], 'L2_gnn_c2_bt': _L2_gnn_in['c2_bt'], 'L2_gnn_c2_w2': _L2_gnn_in['c2_w2'], 'L2_gnn_c2_b2': _L2_gnn_in['c2_b2'], 'L2_gnn_tm_w': _L2_gnn_in['tm_w'], 'L2_gnn_tm_b': _L2_gnn_in['tm_b'], 'L2_gnn_n1_g': _L2_gnn_in['n1_g'], 'L2_gnn_n1_b': _L2_gnn_in['n1_b'], 'L2_gnn_n2_g': _L2_gnn_in['n2_g'], 'L2_gnn_n2_b': _L2_gnn_in['n2_b'], 'L2_gnn_qw': _L2_gnn_in['qw'], 'L2_gnn_qb': _L2_gnn_in['qb'], 'L2_gnn_kw': _L2_gnn_in['kw'], 'L2_gnn_kb': _L2_gnn_in['kb'], 'L2_gnn_vw': _L2_gnn_in['vw'], 'L2_gnn_vb': _L2_gnn_in['vb'], 'L2_gnn_ew': _L2_gnn_in['ew'], 'L2_gnn_eb': _L2_gnn_in['eb'], 'L2_gnn_ow': _L2_gnn_in['ow'], 'L2_gnn_ob': _L2_gnn_in['ob'], 'L2_gnn_an_g': _L2_gnn_in['an_g'], 'L2_gnn_an_b': _L2_gnn_in['an_b'], 'L3_gnn_W': _L3_gnn_in['W'], 'L3_gnn_edge_w': _L3_gnn_in['edge_w'], 'L3_gnn_b': _L3_gnn_in['b']}

def reference(x, src, dst, edge_attr_128, edge_attr_16, edge_attr_4, L0_gnn_W, L0_gnn_att_src, L0_gnn_att_dst, L0_gnn_bias, L0_gnn_gamma, L0_gnn_beta, L1_gnn_We, L1_gnn_be, L1_gnn_W1, L1_gnn_b1, L1_gnn_W2, L1_gnn_b2, L2_gnn_t_emb, L2_gnn_c1_w1, L2_gnn_c1_b1, L2_gnn_c1_g, L2_gnn_c1_bt, L2_gnn_c1_w2, L2_gnn_c1_b2, L2_gnn_c2_w1, L2_gnn_c2_b1, L2_gnn_c2_g, L2_gnn_c2_bt, L2_gnn_c2_w2, L2_gnn_c2_b2, L2_gnn_tm_w, L2_gnn_tm_b, L2_gnn_n1_g, L2_gnn_n1_b, L2_gnn_n2_g, L2_gnn_n2_b, L2_gnn_qw, L2_gnn_qb, L2_gnn_kw, L2_gnn_kb, L2_gnn_vw, L2_gnn_vb, L2_gnn_ew, L2_gnn_eb, L2_gnn_ow, L2_gnn_ob, L2_gnn_an_g, L2_gnn_an_b, L3_gnn_W, L3_gnn_edge_w, L3_gnn_b):
    import jax
    import jax.numpy as jnp

    def _L0_gnn_ref(x, edge_index, W, att_src, att_dst, bias, gamma, beta):
        import jax, jax.numpy as jnp
        import numpy as np
        N, E, D_IN, D_OUT, H = (50000, 25000, 128, 128, 4)
        D_H = D_OUT // H
        n = x.shape[0]
        loop = jnp.arange(n, dtype=edge_index.dtype)
        src = jnp.concatenate([edge_index[0], loop])
        dst = jnp.concatenate([edge_index[1], loop])
        h = jnp.einsum('nd,hdf->nhf', x, W)
        a_src = jnp.einsum('nhf,hf->nh', h, att_src)
        a_dst = jnp.einsum('nhf,hf->nh', h, att_dst)
        alpha = jax.nn.leaky_relu(a_src[src] + a_dst[dst], 0.2)
        m = jax.ops.segment_max(alpha, dst, num_segments=n)
        alpha = jnp.exp(alpha - m[dst])
        s = jax.ops.segment_sum(alpha, dst, num_segments=n)
        alpha = alpha / (s[dst] + 1e-16)
        msgs = h[src] * alpha[:, :, None]
        out = jax.ops.segment_sum(msgs, dst, num_segments=n) + bias[None]
        out = out.reshape(n, H * D_H)
        mu = out.mean(axis=0)
        var = out.var(axis=0)
        return (out - mu) / jnp.sqrt(var + 1e-05) * gamma + beta

    def _L1_gnn_ref(x, edge_index, edge_attr, We, be, W1, b1, W2, b2):
        import jax, jax.numpy as jnp
        import numpy as np
        N, E = (10000, 20000)
        IN_DIM, EDGE_DIM, OUT_DIM = (128, 128, 128)
        src, dst = (edge_index[0], edge_index[1])
        num_nodes = x.shape[0]
        edge_emb = edge_attr @ We + be
        edge_agg = jax.ops.segment_sum(edge_emb, dst, num_segments=num_nodes)
        x_comb = jnp.concatenate([x, edge_agg], axis=-1)
        neigh = jax.ops.segment_sum(x_comb[src], dst, num_segments=num_nodes)
        h = x_comb + neigh
        return jax.nn.relu(h @ W1 + b1) @ W2 + b2

    def _L2_gnn_ref(x, edge_src, edge_dst, edge_attr, t_emb, c1_w1, c1_b1, c1_g, c1_bt, c1_w2, c1_b2, c2_w1, c2_b1, c2_g, c2_bt, c2_w2, c2_b2, tm_w, tm_b, n1_g, n1_b, n2_g, n2_b, qw, qb, kw, kb, vw, vb, ew, eb, ow, ob, an_g, an_b):
        import jax, jax.numpy as jnp
        import numpy as np
        N, E, D, H, HD, TD, ED, G = (30000, 15000, 128, 8, 16, 512, 4, 8)

        def group_norm(x, gamma, beta, num_groups=G, eps=1e-05):
            n, c = x.shape
            xr = x.reshape(n, num_groups, c // num_groups)
            mu = xr.mean(-1, keepdims=True)
            var = ((xr - mu) ** 2).mean(-1, keepdims=True)
            xn = (xr - mu) * jax.lax.rsqrt(var + eps)
            return xn.reshape(n, c) * gamma + beta

        def mesh_conv(x, src, dst, ea, w1, b1, g, bt, w2, b2):
            m = jnp.concatenate([x[dst], x[src], ea], axis=-1) @ w1 + b1
            m = jax.nn.silu(group_norm(m, g, bt))
            m = m @ w2 + b2
            n = x.shape[0]
            out = jax.ops.segment_sum(m, dst, num_segments=n)
            cnt = jax.ops.segment_sum(jnp.ones((dst.shape[0],), m.dtype), dst, num_segments=n)
            return out / jnp.clip(cnt, 1.0)[:, None]
        src, dst = (edge_src, edge_dst)
        n = x.shape[0]
        h = mesh_conv(x, src, dst, edge_attr, c1_w1, c1_b1, c1_g, c1_bt, c1_w2, c1_b2)
        h = jax.nn.silu(group_norm(h, n1_g, n1_b))
        h = h + (jax.nn.silu(t_emb) @ tm_w + tm_b)
        h = mesh_conv(h, src, dst, edge_attr, c2_w1, c2_b1, c2_g, c2_bt, c2_w2, c2_b2)
        h = jax.nn.silu(group_norm(h, n2_g, n2_b))
        h = h + x
        q = (h @ qw + qb).reshape(n, H, HD)
        k = (h @ kw + kb).reshape(n, H, HD)
        v = (h @ vw + vb).reshape(n, H, HD)
        scale = HD ** (-0.5)
        logits = (q[dst] * k[src]).sum(-1) * scale + (edge_attr @ ew + eb)
        amax = jax.ops.segment_max(logits, dst, num_segments=n)
        pe = jnp.exp(logits - amax[dst])
        ssum = jax.ops.segment_sum(pe, dst, num_segments=n)
        w = pe / jnp.clip(ssum[dst], 1e-06)
        o = jax.ops.segment_sum(w[:, :, None] * v[src], dst, num_segments=n)
        o = o.reshape(n, D) @ ow + ob
        o = group_norm(o, an_g, an_b)
        return h + o

    def _L3_gnn_ref(x, edge_index, edge_attr, W, edge_w, b):
        import jax, jax.numpy as jnp
        import numpy as np
        N_NODES = 3125
        N_EDGES = 25000
        D_IN = 128
        D_OUT = 128
        E_DIM = 16
        src, dst = (edge_index[0], edge_index[1])
        xw = x @ W
        ew = edge_attr @ edge_w
        msg = xw[src] * ew
        out = jax.ops.segment_sum(msg, dst, num_segments=x.shape[0])
        out = out + b
        return out
    edge_index = jnp.stack([src, dst])
    h = jnp.maximum(_layernorm(x, axis=-1), 0.0)
    x = x + _L0_gnn_ref(h, edge_index, L0_gnn_W, L0_gnn_att_src, L0_gnn_att_dst, L0_gnn_bias, L0_gnn_gamma, L0_gnn_beta)
    h = jnp.maximum(_layernorm(x, axis=-1), 0.0)
    x = x + _L1_gnn_ref(h, edge_index, edge_attr_128, L1_gnn_We, L1_gnn_be, L1_gnn_W1, L1_gnn_b1, L1_gnn_W2, L1_gnn_b2)
    h = jnp.maximum(_layernorm(x, axis=-1), 0.0)
    x = x + _L2_gnn_ref(h, src, dst, edge_attr_4, L2_gnn_t_emb, L2_gnn_c1_w1, L2_gnn_c1_b1, L2_gnn_c1_g, L2_gnn_c1_bt, L2_gnn_c1_w2, L2_gnn_c1_b2, L2_gnn_c2_w1, L2_gnn_c2_b1, L2_gnn_c2_g, L2_gnn_c2_bt, L2_gnn_c2_w2, L2_gnn_c2_b2, L2_gnn_tm_w, L2_gnn_tm_b, L2_gnn_n1_g, L2_gnn_n1_b, L2_gnn_n2_g, L2_gnn_n2_b, L2_gnn_qw, L2_gnn_qb, L2_gnn_kw, L2_gnn_kb, L2_gnn_vw, L2_gnn_vb, L2_gnn_ew, L2_gnn_eb, L2_gnn_ow, L2_gnn_ob, L2_gnn_an_g, L2_gnn_an_b)
    h = jnp.maximum(_layernorm(x, axis=-1), 0.0)
    x = x + _L3_gnn_ref(h, edge_index, edge_attr_16, L3_gnn_W, L3_gnn_edge_w, L3_gnn_b)
    return x

_drawn_inputs = setup_inputs


def setup_inputs(seed=0):
    import zlib

    import numpy as np

    out = dict(_drawn_inputs(seed))
    spreads = {'L0_gnn_bias': (0.0, 2.0),
     'L0_gnn_gamma': (1.0, 0.2),
     'L0_gnn_beta': (0.0, 0.1),
     'L1_gnn_be': (0.0, 0.1),
     'L1_gnn_b1': (0.0, 0.8),
     'L1_gnn_b2': (0.0, 0.1),
     'L2_gnn_c1_b1': (0.0, 0.1),
     'L2_gnn_c1_g': (1.0, 0.2),
     'L2_gnn_c1_bt': (0.0, 0.548),
     'L2_gnn_c1_b2': (0.0, 0.1),
     'L2_gnn_c2_b1': (0.0, 0.1),
     'L2_gnn_c2_g': (1.0, 0.2),
     'L2_gnn_c2_bt': (0.0, 0.333),
     'L2_gnn_c2_b2': (0.0, 0.1),
     'L2_gnn_tm_b': (0.0, 0.364),
     'L2_gnn_n1_g': (1.0, 0.6),
     'L2_gnn_n1_b': (0.0, 0.441),
     'L2_gnn_n2_g': (1.0, 0.2),
     'L2_gnn_n2_b': (0.0, 0.332),
     'L2_gnn_qb': (0.0, 2.0),
     'L2_gnn_kb': (0.0, 2.0),
     'L2_gnn_vb': (0.0, 0.1),
     'L2_gnn_eb': (0.0, 2.0),
     'L2_gnn_ob': (0.0, 0.1),
     'L2_gnn_an_g': (1.0, 0.2),
     'L2_gnn_an_b': (0.0, 0.1),
     'L3_gnn_b': (0.0, 0.1)}
    factors = {'edge_attr_4': 4.656, 'L2_gnn_qw': 8.0, 'L2_gnn_kw': 8.0, 'L2_gnn_ew': 8.0}
    for name, (base, spread) in spreads.items():
        noise = np.random.default_rng([zlib.crc32(name.encode()), seed]).standard_normal(out[name].shape)
        drawn = base * np.exp(spread * noise) if base else spread * noise
        out[name] = jnp.asarray(drawn.astype(out[name].dtype))
    for name, factor in factors.items():
        out[name] = (out[name] * factor).astype(out[name].dtype)
    return out
```

```python
import concourse.bass as bass
from concourse import mybir
from contextlib import ExitStack

F32 = mybir.dt.float32
I32 = mybir.dt.int32
U8 = mybir.dt.uint8
ALU = mybir.AluOpType
ACT = mybir.ActivationFunctionType
AX = mybir.AxisListType

N = 3125
E = 50000
D = 128
P = 128
BN = 32
NBUK = -(-N // BN)
TILES = -(-N // P)
NP = TILES * P
NB = NP // BN
EP = 125
EC = E // EP
RING = 4
GS = 4
SLOTS_MIN = (E + NBUK * (P - 1)) // P
TRIPS = -(-SLOTS_MIN // (RING * GS))
GROUPS = TRIPS * RING
SLOTS = GROUPS * GS
REC = 152
META = 24
TR = 96
CH = 400
NCH = NP // CH
BIG = 1.0e30
EPS = 1e-5


class Chain:

    def __init__(self, eng, sem, base=0):
        self.eng, self.sem, self.base, self.k = eng, sem, base, 0

    def __call__(self, ins):
        self.k += 1
        ins.then_inc(self.sem, 1)
        self.eng.wait_ge(self.sem, self.base + self.k)


class Build:

    def __init__(self, nc, ctx):
        self.nc, self.ctx, self.n = nc, ctx, 0

    def name(self, s):
        self.n += 1
        return f"{s}_{self.n}"

    def sb(self, s, shape, dt=F32, ctx=None):
        return (ctx or self.ctx).enter_context(self.nc.sbuf_tensor(self.name(s), shape, dt))

    def ps(self, s, shape, ctx, dt=F32):
        return ctx.enter_context(self.nc.psum_tensor(self.name(s), shape, dt))

    def sem(self, s):
        self.sems.append(self.nc.alloc_semaphore(self.name(s)))
        return self.sems[-1]

    def dram(self, s, shape, dt=F32):
        return self.nc.dram_tensor(self.name(s), shape, dt, kind="Internal").ap()


def phase(f):
    def run(nc, B, *args, **kw):
        B.sems = []
        f(nc, B, *args, **kw)
        nc.clear_and_free_semaphores(B.sems)
        nc.all_engine_barrier()
    return run


def bc(ap, shape):
    return ap.to_broadcast(shape)



WEIGHTS = ["L1_gnn_We", "L1_gnn_W2", "L2_gnn_c1_w2", "L2_gnn_c2_w2", "L2_gnn_qw", "L2_gnn_kw",
           "L2_gnn_vw", "L2_gnn_ow", "L3_gnn_W"]
COLS = ["L0_gnn_gamma", "L0_gnn_beta", "L1_gnn_be", "L1_gnn_b1", "L1_gnn_b2", "L2_gnn_c1_b2",
        "L2_gnn_c2_b2", "L2_gnn_tm_b", "L2_gnn_n1_g", "L2_gnn_n1_b", "L2_gnn_n2_g", "L2_gnn_n2_b",
        "L2_gnn_ob", "L2_gnn_an_g", "L2_gnn_an_b", "L3_gnn_b"]
ROWS = ["L2_gnn_c1_g", "L2_gnn_c1_bt", "L2_gnn_c2_g", "L2_gnn_c2_bt", "L2_gnn_qb", "L2_gnn_kb",
        "L2_gnn_vb"]


@phase
def constants(nc, B, A, K):
    s_w = B.sem("weights_loaded")
    s_p = B.sem("patterns_made")
    s_z = B.sem("zeroed")
    s_v = B.sem("vector_chain")
    s_a = B.sem("silu_made")
    s_t = B.sem("time_product")
    K.ident = B.sb("ident", [P, P])
    K.tri = B.sb("tri", [P, P])
    K.ones = B.sb("ones", [P, P])
    K.iota = B.sb("iota", [P, P])
    K.part = B.sb("part", [P, 1])
    K.gmean = B.sb("gmean", [P, P])
    K.slotid = B.sb("slotid", [P, 4])
    K.neg = B.sb("neg", [TR, 4, BN])
    K.sel = B.sb("sel", [TR, 64])
    K.hs32 = B.sb("hs32", [8, 2, P])
    K.hs16 = B.sb("hs16", [8, P])
    K.eqm = B.sb("eqm", [64, 1])
    K.eqc = B.sb("eqc", [64, 1])
    K.w = {n: B.sb(n, [D, D]) for n in WEIGHTS}
    K.c = {n: B.sb(n, [D, 1]) for n in COLS}
    K.c["L0_gnn_bias"] = B.sb("L0_bias", [D, 1])
    K.r = {n: B.sb(n, [P, D]) for n in ROWS}
    K.w0 = B.sb("L0_W", [D, 136])
    K.w1a = B.sb("L1_W1a", [D, D])
    K.w1b = B.sb("L1_W1b", [D, D])
    K.ca = [B.sb("conv_dst_w", [D, D]) for _ in range(2)]
    K.cb = [B.sb("conv_src_w", [D, D]) for _ in range(2)]
    K.cs = [B.sb("conv_edge_w", [TR, D]) for _ in range(2)]
    K.ew = B.sb("logit_edge_w", [TR, 8])
    K.w3 = B.sb("L3_edge_w", [TR, D])
    K.tvec = B.sb("time_vector", [D, 1])
    with ExitStack() as ph:
        att = B.sb("att", [P, 2, D], ctx=ph)
        prod = B.sb("prod", [P, 2, D], ctx=ph)
        gm = B.sb("gm", [P, 8, 8], ctx=ph)
        te = B.sb("te", [P, 4], ctx=ph)
        tes = B.sb("tes", [P, 4], ctx=ph)
        tw = B.sb("tw", [P, 4, D], ctx=ph)
        ii = B.sb("ii", [P, P], I32, ctx=ph)
        pi = B.sb("pi", [P, 1], I32, ctx=ph)
        si = B.sb("si", [P, 4], I32, ctx=ph)
        pst = B.ps("pst", [P, 8], ph)
        block = ph.enter_context(nc.Block())
        loads = []

        @block.gpsimd
        def _(po):
            step = Chain(po, s_p)
            step(nc.gpsimd.iota(ii[:, :], [[1, P]], base=0, channel_multiplier=0))
            step(nc.gpsimd.iota(pi[:, :], [[0, 1]], base=0, channel_multiplier=1))
            step(nc.gpsimd.iota(si[:, :], [[P, 4]], base=0, channel_multiplier=1))
            po.wait_ge(s_z, 9)

            def one_where(t, base, pattern, mult, fill=1.0):
                step(nc.gpsimd.affine_select(out=t, in_=t, compare_op=ALU.not_equal, fill=fill, base=base,
                                             pattern=pattern, channel_multiplier=mult))

            def keep_where(t, base, pattern, mult):
                step(nc.gpsimd.affine_select(out=t, in_=t, compare_op=ALU.is_ge, fill=0.0, base=base,
                                             pattern=pattern, channel_multiplier=mult))

            one_where(K.ident[:, :], 0, [[-1, P]], 1)
            keep_where(K.tri[:, :], -1, [[1, P]], -1)
            g3 = K.gmean[:, :].rearrange("p (g k) -> p g k", g=8)
            keep_where(g3, 0, [[-16, 8], [0, 16]], 1)
            keep_where(g3, 15, [[16, 8], [0, 16]], -1)
            one_where(K.neg[:, :, :], -32, [[0, 4], [-1, BN]], 1, BIG)
            one_where(K.sel[:, :], -64, [[0, 64]], 1)
            one_where(K.hs32[:, :, :].rearrange("p a (h n) -> p (a h) n", h=4), 0, [[-1, 8], [0, 32]], 1)
            one_where(K.hs16[:, :].rearrange("p (h n) -> p h n", h=8), 0, [[-1, 8], [0, 16]], 1)

        @block.sync
        def _(sp):
            n = 0

            def load(dst, src):
                nonlocal n
                n += 16
                sp.dma_start(dst, src).then_inc(s_w, 16)

            for name in WEIGHTS:
                load(K.w[name][:, :], A[name])
            load(K.w1a[:, :], A["L1_gnn_W1"][0:D, :])
            load(K.w1b[:, :], A["L1_gnn_W1"][D:2 * D, :])
            for i, c in enumerate(("c1", "c2")):
                w = A[f"L2_gnn_{c}_w1"]
                load(K.ca[i][:, :], w[0:D, :])
                load(K.cb[i][:, :], w[D:2 * D, :])
            for h in range(4):
                load(K.w0[:, 32 * h:32 * h + 32], A["L0_gnn_W"][h, :, :])
            with nc.allow_non_contiguous_dma(reason="vectors as columns"):
                for name in COLS:
                    load(K.c[name][:, :], A[name].rearrange("(d a) -> d a", a=1))
                load(K.c["L0_gnn_bias"][:, :], A["L0_gnn_bias"].rearrange("h (f a) -> (h f) a", a=1))
                load(te[:, :], A["L2_gnn_t_emb"].rearrange("(c p) -> p c", p=P))
            for name in ROWS:
                load(K.r[name][:, :], A[name].partition_broadcast(P))
            load(tw[:, :, :], A["L2_gnn_tm_w"].rearrange("(c p) d -> p c d", p=P))
            for j, name in enumerate(("L0_gnn_att_src", "L0_gnn_att_dst")):
                load(att[:, j, :], A[name].rearrange("h f -> (h f)").partition_broadcast(P))
            sp.wait_ge(s_v, 4)
            for i, c in enumerate(("c1", "c2")):
                load(K.cs[i][66:70, :], A[f"L2_gnn_{c}_w1"][2 * D:2 * D + 4, :])
                load(K.cs[i][65:66, :], A[f"L2_gnn_{c}_b1"].rearrange("(a d) -> a d", a=1))
            load(K.ew[66:70, :], A["L2_gnn_ew"])
            load(K.ew[65:66, :], A["L2_gnn_eb"].rearrange("(a d) -> a d", a=1))
            load(K.w3[70:86, :], A["L3_gnn_edge_w"])
            sp.wait_ge(s_w, n)
            loads.append(n)

        @block.vector
        def _(ve):
            link = Chain(ve, s_v)
            for t in (K.cs[0], K.cs[1], K.ew, K.w3):
                link(nc.vector.memset(t[:, :], 0.0))
            for t, v in ((K.ident, 0.0), (K.tri, 1.0), (K.ones, 1.0), (K.gmean, 1.0 / 16), (K.sel, 0.0), (K.hs16, 0.0)):
                nc.vector.memset(t[:, :], v).then_inc(s_z, 1)
            nc.vector.memset(K.hs32[:, :, :], 0.0).then_inc(s_z, 1)
            nc.vector.memset(K.neg[:, :, :], 0.0).then_inc(s_z, 1)
            link(nc.vector.memset(K.eqc[0:32, :], 0.0))
            nc.vector.memset(K.eqc[32:64, :], 1.0).then_inc(s_z, 1)
            ve.wait_ge(s_p, 3)
            link(nc.vector.tensor_copy(K.iota[:, :], ii[:, :]))
            link(nc.vector.tensor_copy(K.part[:, :], pi[:, :]))
            link(nc.vector.tensor_copy(K.slotid[:, :], si[:, :]))
            link(nc.vector.tensor_copy(K.eqm[0:32, :], K.part[0:32, :]))
            link(nc.vector.tensor_scalar(K.eqm[32:64, :], K.part[32:64, :], 32.0, None, ALU.subtract))
            ve.wait_ge(s_w, loads[0])
            w0 = K.w0[:, 0:D]
            for j in range(2):
                link(nc.vector.tensor_tensor(prod[:, j, :], w0, att[:, j, :], ALU.mult))
                link(nc.vector.tensor_reduce(K.w0[:, D + 4 * j:D + 4 * j + 4],
                                             prod[:, j, :].rearrange("p (h f) -> p h f", h=4),
                                             AX.X, ALU.add))
            for t, rows in [(K.ca[0], D), (K.ca[1], D), (K.cb[0], D), (K.cb[1], D),
                            (K.cs[0], TR), (K.cs[1], TR)]:
                t3 = t[:, :].rearrange("p (g k) -> p g k", g=8)
                link(nc.vector.tensor_reduce(gm[0:rows, 0, :], t3, AX.X, ALU.add))
                link(nc.vector.tensor_scalar(gm[0:rows, 1, :], gm[0:rows, 0, :], 1.0 / 16, None, ALU.mult))
                link(nc.vector.tensor_tensor(t3, t3, bc(gm[0:rows, 1, :].unsqueeze(2), [rows, 8, 16]),
                                             ALU.subtract))
            link(nc.vector.tensor_scalar(K.r["L2_gnn_qb"][:, :], K.r["L2_gnn_qb"][:, :], 0.25, None, ALU.mult))
            ve.wait_ge(s_t, 1)
            link(nc.vector.tensor_tensor(K.tvec[:, :], pst[:, 0:1], K.c["L2_gnn_tm_b"][:, :], ALU.add))

        @block.scalar
        def _(ac):
            ac.wait_ge(s_w, loads[0])
            nc.scalar.activation(tes[:, :], te[:, :], ACT.Silu).then_inc(s_a, 1)

        @block.tensor
        def _(pe):
            pe.wait_ge(s_a, 1)
            for c in range(4):
                m = nc.tensor.matmul(pst[:, 0:1], tw[:, c, :], tes[:, c:c + 1], start=c == 0, stop=c == 3)
            m.then_inc(s_t, 1)



@phase
def rank_edges(nc, B, A, K):
    s_in, s_img, s_fill = B.sem("edges_loaded"), B.sem("padding_made"), B.sem("padding_stored")
    s_v, s_cnt, s_pre, s_out = B.sem("rank_chain"), B.sem("counted"), B.sem("prefix_made"), B.sem("table_stored")
    s_sc, s_cp, s_ld, s_bk = B.sem("scanned"), B.sem("placed"), B.sem("table_loaded"), B.sem("buckets_made")
    K.pos = B.sb("pos", [EP, EC], I32)
    K.dl = B.sb("dl_unsorted", [EP, EC])
    K.bucket = B.sb("slot_bucket", [1, 512], I32)
    rec_v = K.rec.rearrange("(p c k) w -> c p (k w)", p=P, c=8)
    with ExitStack() as ph:
        dst = B.sb("dst", [EP, EC], I32, ph)
        t_i = B.sb("t_i", [EP, EC], I32, ph)
        buk = B.sb("buk", [EP, EC], F32, ph)
        mask = B.sb("mask", [EP, NBUK, EC], U8, ph)
        cnt = B.sb("cnt", [EP, NBUK], F32, ph)
        off = B.sb("off", [EP, NBUK], F32, ph)
        sl_i = B.sb("sl_i", [P, NBUK], I32, ph)
        sl = B.sb("sl", [P, NBUK], F32, ph)
        ends = B.sb("ends", [P, NBUK], F32, ph)
        zero = B.sb("zero", [P, EC], F32, ph)
        cum = B.sb("cum", [EP, 2, EC], F32, ph)
        c0 = B.sb("c0", [EP, 2], F32, ph)
        posf = B.sb("posf", [EP, EC], F32, ph)
        cmp = B.sb("cmp", [P, NBUK], F32, ph)
        sb_f = B.sb("sb_f", [P, 4], F32, ph)
        sb_i = B.sb("sb_i", [P, 4], I32, ph)
        img = B.sb("img", [P, SLOTS // 8, REC], F32, ph)
        pre = B.ps("pre", [P, 2, P], ph)
        block = ph.enter_context(nc.Block())

        @block.sync
        def _(sp):
            sp.dma_start(dst[:, :], A["dst"].rearrange("(p j) -> p j", p=EP)).then_inc(s_in, 16)
            sp.wait_ge(s_img, 2)
            for c in range(8):
                sp.dma_start(rec_v[c], img[:, :, :].rearrange("p k w -> p (k w)")).then_inc(s_fill, 16)
            sp.wait_ge(s_bk, 1)
            with nc.allow_non_contiguous_dma(reason="512 words"):
                sp.dma_start(K.bucket_dram.rearrange("(k p) -> p k", p=P), sb_i[:, :]).then_inc(s_out, 16)
            sp.wait_ge(s_out, 16)
            sp.dma_start(K.bucket[:, :], K.bucket_dram.rearrange("(a n) -> a n", a=1)).then_inc(s_ld, 16)
            sp.wait_ge(s_ld, 16)
            sp.wait_ge(s_fill, 128)

        @block.gpsimd
        def _(po):
            nc.gpsimd.memset(img[:, :, :], 0.0).then_inc(s_img, 1)
            po.wait_ge(s_img, 1)
            nc.gpsimd.memset(img[:, :, D:D + 1], -1.0).then_inc(s_img, 1)

        @block.vector
        def _(ve):
            link = Chain(ve, s_v)
            link(nc.vector.memset(zero[:, :], 0.0))
            link(nc.vector.memset(posf[:, :], 0.0))
            ve.wait_ge(s_in, 16)
            link(nc.vector.tensor_scalar(t_i[:, :], dst[:, :], 5, None, ALU.arith_shift_right))
            link(nc.vector.tensor_copy(buk[:, :], t_i[:, :]))
            link(nc.vector.tensor_scalar(t_i[:, :], dst[:, :], BN - 1, None, ALU.bitwise_and))
            link(nc.vector.tensor_copy(K.dl[:, :], t_i[:, :]))
            link(nc.vector.tensor_tensor(mask[:, :, :], bc(buk[:, :].unsqueeze(1), [EP, NBUK, EC]),
                                         bc(K.iota[0:EP, 0:NBUK].unsqueeze(2), [EP, NBUK, EC]), ALU.is_equal))
            nc.vector.tensor_reduce(cnt[:, :], mask[:, :, :], AX.X, ALU.add).then_inc(s_cnt, 1)
            ve.wait_ge(s_pre, 1)
            link(nc.vector.tensor_scalar(cmp[:, :], pre[:, 1, 0:NBUK], float(P - 1), None, ALU.add))
            link(nc.vector.tensor_copy(sl_i[:, :], cmp[:, :]))
            link(nc.vector.tensor_scalar(sl_i[:, :], sl_i[:, :], 7, None, ALU.arith_shift_right))
            link(nc.vector.tensor_copy(sl[:, :], sl_i[:, :]))
            link(nc.vector.tensor_tensor_scan(ends[:, :], sl[:, :], zero[:, 0:NBUK], 0.0, ALU.add, ALU.add))
            link(nc.vector.tensor_tensor(sl[:, :], ends[:, :], sl[:, :], ALU.subtract))
            link(nc.vector.tensor_scalar(sl[:, :], sl[:, :], float(P), -1.0, ALU.mult, ALU.add))
            link(nc.vector.tensor_tensor(off[:, :], sl[0:EP, :], pre[0:EP, 0, 0:NBUK], ALU.add))
            for k in range(4):
                link(nc.vector.tensor_scalar(cmp[:, :], ends[:, :], K.slotid[:, k:k + 1], None, ALU.is_le))
                link(nc.vector.tensor_reduce(sb_f[:, k:k + 1], cmp[:, :], AX.X, ALU.add))
            link(nc.vector.tensor_scalar(sb_f[:, :], sb_f[:, :], float(NBUK - 1), None, ALU.min))
            nc.vector.tensor_copy(sb_i[:, :], sb_f[:, :]).then_inc(s_bk, 1)
            base = link.k
            with ve.Fori(0, NBUK // 2) as h:
                l2 = Chain(ve, s_v, h * 8 + base)
                for g in range(2):
                    l2(nc.vector.tensor_copy(c0[:, g:g + 1], off[:, bass.ds(h * 2 + g, 1)]))
                    m = mask[:, bass.ds(h * 2 + g, 1), :].rearrange("p a j -> p (a j)")
                    l2(nc.vector.tensor_tensor_scan(cum[:, g, :], m, zero[0:EP, :], c0[:, g:g + 1],
                                                    ALU.add, ALU.add))
                    l2(nc.vector.tensor_tensor(cum[:, g, :], cum[:, g, :], m, ALU.mult))
                    l2(nc.vector.tensor_tensor(posf[:, :], posf[:, :], cum[:, g, :], ALU.add))
                assert l2.k == 8
            nc.vector.tensor_copy(K.pos[:, :], posf[:, :]).then_inc(s_cp, 1)

        @block.tensor
        def _(pe):
            pe.wait_ge(s_cnt, 1)
            nc.tensor.matmul(pre[0:EP, 0, 0:NBUK], K.tri[0:EP, 0:EP], cnt[:, :], start=True, stop=True)
            nc.tensor.matmul(pre[:, 1, 0:NBUK], K.ones[0:EP, :], cnt[:, :], start=True, stop=True).then_inc(s_pre, 1)


@phase
def scatter_records(nc, B, A, K):
    W = 8
    STEPS = EC // W
    s_in, s_meta, s_free = B.sem("meta_loaded"), B.sem("meta_made"), B.sem("stage_free")
    s_attr = [B.sem("attr_staged") for _ in range(2)]
    s_stage = B.sem("meta_staged")
    s_done = [B.sem("rows_scattered") for _ in range(2)]
    s_go = B.sem("pool_go")
    with ExitStack() as ph:
        src = B.sb("src", [EP, EC], I32, ph)
        a4 = B.sb("a4", [EP, EC, 4], F32, ph)
        a16 = B.sb("a16", [EP, EC, 16], F32, ph)
        meta = B.sb("meta", [EP, EC, META], F32, ph)
        stage = B.sb("stage", [EP, 2, W, REC], F32, ph)
        idx = B.sb("idx", [EP, 2, W], I32, ph)
        block = ph.enter_context(nc.Block())
        attr = A["edge_attr_128"].rearrange("(p j) d -> p j d", p=EP)

        @block.sync
        def _(sp):
            sp.dma_start(src[:, :], A["src"].rearrange("(p j) -> p j", p=EP)).then_inc(s_in, 16)
            sp.dma_start(a4[:, :, :], A["edge_attr_4"].rearrange("(p j) k -> p j k", p=EP)).then_inc(s_in, 16)
            sp.dma_start(a16[:, :, :], A["edge_attr_16"].rearrange("(p j) k -> p j k", p=EP)).then_inc(s_in, 16)
            with sp.Fori(0, STEPS // 2) as i:
                for g in range(2):
                    sp.wait_ge(s_free, i * 2 + g + 1)
                    sp.dma_start(stage[:, g, :, 0:D], attr[:, bass.ds(i * (2 * W) + g * W, W), :]).then_inc(s_attr[g], 16)

        @block.gpsimd
        def _(po):
            with po.Fori(0, STEPS // 2) as i:
                for g in range(2):
                    po.wait_ge(s_attr[g], i * 16 + 16)
                    po.wait_ge(s_stage, i * 2 + g + 1)
                    po.sem_inc(s_go, 1)
                    for k in range(W):
                        nc.gpsimd.indirect_dma_start(
                            out=K.rec, out_offset=bass.IndirectOffsetOnAxis(ap=idx[:, g, k:k + 1], axis=0),
                            in_=stage[:, g, k, :], in_offset=None).then_inc(s_done[g], 16)

        @block.scalar
        def _(ac):
            ac.wait_ge(s_meta, 5)
            with ac.Fori(0, STEPS // 2) as i:
                for g in range(2):
                    ac.wait_ge(s_free, i * 2 + g + 1)
                    j = i * (2 * W) + g * W
                    nc.scalar.copy(stage[:, g, :, D:REC], meta[:, bass.ds(j, W), :])
                    nc.scalar.copy(idx[:, g, :], K.pos[:, bass.ds(j, W)]).then_inc(s_stage, 1)

        @block.vector
        def _(ve):
            nc.vector.memset(meta[:, :, 1:2], 1.0).then_inc(s_meta, 1)
            nc.vector.tensor_copy(meta[:, :, 0:1], K.dl[:, :].unsqueeze(2)).then_inc(s_meta, 1)
            nc.vector.memset(meta[:, :, 23:24], 0.0)
            ve.wait_ge(s_in, 48)
            nc.vector.tensor_copy(meta[:, :, 2:6], a4[:, :, :]).then_inc(s_meta, 1)
            nc.vector.tensor_copy(meta[:, :, 6:22], a16[:, :, :]).then_inc(s_meta, 1)
            nc.vector.tensor_copy(meta[:, :, 22:23].bitcast(I32), src[:, :].unsqueeze(2)).then_inc(s_meta, 1)
            ve.sem_inc(s_free, 2)
            with ve.Fori(0, STEPS // 2) as i:
                for g in range(2):
                    ve.wait_ge(s_done[g], i * (16 * W) + 16 * W)
                    ve.sem_inc(s_free, 1)


@phase
def make_operands(nc, B, A, K):
    K.dls = B.sb("dl_sorted", [P, SLOTS])
    s_rec = [B.sem("meta_read") for _ in range(RING)]
    s_tr, s_row, s_dlb = B.sem("transposed"), B.sem("rows_copied"), B.sem("dst_spread")
    s_free, s_t = B.sem("operand_free"), B.sem("operand_made")
    s_st = [B.sem("operand_stored") for _ in range(RING)]
    s_dl = B.sem("destinations_kept")
    s_src, s_so, s_z = B.sem("sources_kept"), B.sem("sources_stored"), B.sem("rows_zeroed")
    with ExitStack() as ph:
        rec = B.sb("rec", [P, RING, GS, META], F32, ph)
        T = B.sb("T", [TR, RING, GS * P], F32, ph)
        srcs = B.sb("srcs", [P, SLOTS], I32, ph)
        ps_t = [B.ps("ps_t", [META, GS * P], ph) for _ in range(2)]
        ps_d = [B.ps("ps_d", [64, GS * P], ph) for _ in range(2)]
        block = ph.enter_context(nc.Block())
        rec_v = K.rec.rearrange("(s p) w -> p s w", p=P)

        @block.sync
        def _(sp):
            with sp.Fori(0, TRIPS) as i:
                for g in range(RING):
                    n = i * RING + g
                    sp.wait_ge(s_free, n + 1)
                    sp.dma_start(rec[:, g, :, :], rec_v[:, bass.ds(n * GS, GS), D:REC]).then_inc(s_rec[g], 16)
            sp.wait_ge(s_src, GROUPS)
            sp.dma_start(K.src_dram, srcs[:, :]).then_inc(s_so, 16)
            sp.wait_ge(s_so, 16)

        @block.tensor
        def _(pe):
            pe.wait_ge(s_z, 1)
            with pe.Fori(0, TRIPS) as i:
                for g in range(RING):
                    n = i * RING + g
                    pe.wait_ge(s_rec[g], i * 16 + 16)
                    for k in range(GS):
                        m = nc.tensor.transpose(ps_t[g % 2][:, k * P:(k + 1) * P], rec[:, g, k, :], K.ident[:, :])
                    m.then_inc(s_tr, 1)
                    pe.wait_ge(s_row, n + 1)
                    nc.tensor.matmul(ps_d[g % 2][:, :], K.sel[64:64 + META, :], T[64:64 + META, g, :],
                                     start=True, stop=True).then_inc(s_dlb, 1)

        @block.scalar
        def _(ac):
            with ac.Fori(0, TRIPS) as i:
                for g in range(RING):
                    n = i * RING + g
                    ac.wait_ge(s_tr, n + 1)
                    nc.scalar.copy(T[64:64 + META, g, :], ps_t[g % 2][:, :]).then_inc(s_row, 1)
                    ac.wait_ge(s_t, n + 1)
                    ac.dma_start(K.t_dram[bass.ds(n, 1), :, :].rearrange("a r c -> (a r) c"),
                                 T[:, g, :]).then_inc(s_st[g], 16)

        @block.vector
        def _(ve):
            nc.vector.memset(T[:, :, :], 0.0).then_inc(s_z, 1)
            ve.wait_ge(s_z, 1)
            ve.sem_inc(s_free, RING)
            with ve.Fori(0, TRIPS) as i:
                for g in range(RING):
                    n = i * RING + g
                    ve.wait_ge(s_dlb, n + 1)
                    nc.vector.tensor_scalar(T[0:64, g, :], ps_d[g % 2][:, :], K.eqm[:, :], K.eqc[:, :],
                                            ALU.is_equal, ALU.subtract).then_inc(s_t, 1)
                    nc.vector.tensor_copy(srcs[:, bass.ds(n * GS, GS)],
                                          rec[:, g, :, 22:23].bitcast(I32).rearrange("p s a -> p (s a)")).then_inc(s_src, 1)
                    nc.vector.tensor_copy(K.dls[:, bass.ds(n * GS, GS)],
                                          rec[:, g, :, 0:1].rearrange("p s a -> p (s a)")).then_inc(s_dl, 1)
                    ve.wait_ge(s_dl, n + 1)
                    ve.wait_ge(s_st[g], i * 16 + 16)
                    ve.sem_inc(s_free, 1)



@phase
def load_x(nc, B, A, K):
    s_in, s_z, s_tr, s_cp = B.sem("x_loaded"), B.sem("x_padded"), B.sem("x_transposed"), B.sem("x_copied")
    with ExitStack() as ph:
        xn = B.sb("xn", [P, TILES, D], F32, ph)
        ps = [B.ps("ps", [P, P], ph) for _ in range(2)]
        block = ph.enter_context(nc.Block())
        full, rest = N // P, N % P

        @block.sync
        def _(sp):
            sp.dma_start(xn[:, 0:full, :], A["x"][0:full * P, :].rearrange("(t p) d -> p t d", p=P)).then_inc(s_in, 16)
            sp.wait_ge(s_z, 1)
            sp.dma_start(xn[0:rest, full, :], A["x"][full * P:N, :]).then_inc(s_in, 16)

        @block.tensor
        def _(pe):
            pe.wait_ge(s_in, 32)
            for t in range(TILES):
                if t >= 2:
                    pe.wait_ge(s_cp, t - 1)
                nc.tensor.transpose(ps[t % 2][:, :], xn[:, t, :], K.ident[:, :]).then_inc(s_tr, 1)

        @block.vector
        def _(ve):
            nc.vector.memset(xn[:, full, :], 0.0).then_inc(s_z, 1)
            for t in range(TILES):
                ve.wait_ge(s_tr, t + 1)
                nc.vector.tensor_copy(K.X[:, t * P:(t + 1) * P], ps[t % 2][:, :]).then_inc(s_cp, 1)


@phase
def norm_nodes(nc, B, A, K):
    s_tr, s_xc, s_v, s_sd = B.sem("x_transposed"), B.sem("x_copied"), B.sem("stat_chain"), B.sem("deviations")
    s_sq, s_h, s_hb, s_hc = B.sem("roots"), B.sem("normed"), B.sem("h_transposed"), B.sem("h_copied")
    with ExitStack() as ph:
        xn = B.sb("xn", [P, TILES, D], F32, ph)
        st = B.sb("st", [P, TILES, 6], F32, ph)
        mv = B.sb("mv", [P, TILES, 2], F32, ph)
        sd = B.sb("sd", [P, TILES], F32, ph)
        nb = B.sb("nb", [P, TILES], F32, ph)
        psx = [B.ps("psx", [P, P], ph) for _ in range(2)]
        psh = [B.ps("psh", [P, P], ph) for _ in range(2)]
        block = ph.enter_context(nc.Block())

        @block.tensor
        def _(pe):
            for t in range(TILES):
                if t >= 2:
                    pe.wait_ge(s_xc, t - 1)
                nc.tensor.transpose(psx[t % 2][:, :], K.X[:, t * P:(t + 1) * P], K.ident[:, :]).then_inc(s_tr, 1)
            for t in range(TILES):
                pe.wait_ge(s_h, t + 1)
                if t >= 2:
                    pe.wait_ge(s_hc, t - 1)
                nc.tensor.transpose(psh[t % 2][:, :], xn[:, t, :], K.ident[:, :]).then_inc(s_hb, 1)

        @block.vector
        def _(ve):
            link = Chain(ve, s_v)
            for t in range(TILES):
                ve.wait_ge(s_tr, t + 1)
                nc.vector.tensor_copy(xn[:, t, :], psx[t % 2][:, :]).then_inc(s_xc, 1)
                ve.wait_ge(s_xc, t + 1)
                link(nc.vector.bn_stats(st[:, t, :], xn[:, t, :]))
                link(nc.vector.bn_aggr(mv[:, t, :], st[:, t, :]))
            nc.vector.tensor_scalar(sd[:, :], mv[:, :, 1], EPS, None, ALU.add).then_inc(s_sd, 1)
            ve.wait_ge(s_sq, 1)
            link(nc.vector.reciprocal(sd[:, :], sd[:, :]))
            nc.vector.scalar_tensor_tensor(out=nb[:, :], in0=mv[:, :, 0], scalar=-1.0, in1=sd[:, :],
                                           op0=ALU.mult, op1=ALU.mult).then_inc(s_sd, 1)
            for t in range(TILES):
                ve.wait_ge(s_hb, t + 1)
                nc.vector.tensor_copy(K.H[:, t * P:(t + 1) * P], psh[t % 2][:, :]).then_inc(s_hc, 1)

        @block.scalar
        def _(ac):
            ac.wait_ge(s_sd, 1)
            nc.scalar.activation(sd[:, :], sd[:, :], ACT.Sqrt).then_inc(s_sq, 1)
            ac.wait_ge(s_sd, 2)
            for t in range(TILES):
                nc.scalar.activation(xn[:, t, :], xn[:, t, :], ACT.Relu, bias=nb[:, t:t + 1],
                                     scale=sd[:, t:t + 1]).then_inc(s_h, 1)


@phase
def project_nodes(nc, B, K, pairs, width, table, row=None, scale=1.0):
    s_mm, s_cp, s_st = B.sem("projected"), B.sem("row_copied"), B.sem("table_stored")
    with ExitStack() as ph:
        out = B.sb("out", [P, TILES, width], F32, ph)
        ps = [B.ps("ps", [P, 512], ph) for _ in range(2)]
        block = ph.enter_context(nc.Block())

        @block.tensor
        def _(pe):
            for t in range(TILES):
                if t >= 2:
                    pe.wait_ge(s_cp, t - 1)
                for j, (x, ws) in enumerate(pairs):
                    at = 0
                    for w in ws:
                        n = w.shape[1]
                        m = nc.tensor.matmul(ps[t % 2][:, at:at + n], x[:, t * P:(t + 1) * P], w,
                                             start=j == 0, stop=j == len(pairs) - 1, skip_group_check=True)
                        at += n
                m.then_inc(s_mm, 1)

        @block.vector
        def _(ve):
            for t in range(TILES):
                ve.wait_ge(s_mm, t + 1)
                if row is None:
                    nc.vector.tensor_copy(out[:, t, :], ps[t % 2][:, 0:width]).then_inc(s_cp, 1)
                else:
                    for j, r in enumerate(row):
                        m = nc.vector.scalar_tensor_tensor(
                            out=out[:, t, j * D:(j + 1) * D], in0=ps[t % 2][:, j * D:(j + 1) * D], scalar=scale,
                            in1=r, op0=ALU.mult, op1=ALU.add)
                    m.then_inc(s_cp, 1)

        @block.sync
        def _(sp):
            sp.wait_ge(s_cp, TILES)
            sp.dma_start(table.rearrange("(t p) w -> p t w", p=P), out[:, :, :]).then_inc(s_st, 16)
            sp.wait_ge(s_st, 16)


@phase
def feature_product(nc, B, K, pairs, consume, steps, act=None):
    s_mm, s_v = B.sem("chunk_product"), B.sem("chunk_chain")
    with ExitStack() as ph:
        ps = [B.ps("ps", [P, 512], ph) for _ in range(2)]
        block = ph.enter_context(nc.Block())

        @block.tensor
        def _(pe):
            for c in range(NCH):
                if c >= 2:
                    pe.wait_ge(s_v, steps * (c - 1))
                for j, (w, x) in enumerate(pairs):
                    m = nc.tensor.matmul(ps[c % 2][:, 0:CH], w, x[:, c * CH:(c + 1) * CH],
                                         start=j == 0, stop=j == len(pairs) - 1)
                m.then_inc(s_mm, 1)

        @block.vector
        def _(ve):
            link = Chain(ve, s_v)
            for c in range(NCH):
                ve.wait_ge(s_mm, c + 1)
                consume(slice(c * CH, (c + 1) * CH), ps[c % 2][:, 0:CH], link)
                assert link.k == steps * (c + 1)


@phase
def group_norm(nc, B, K, X, gamma, beta, func, Y):
    s_mm, s_c, s_sq = B.sem("group_mean"), B.sem("centred"), B.sem("squared")
    s_var, s_rt, s_v, s_n, s_y = B.sem("group_var"), B.sem("root"), B.sem("norm_chain"), B.sem("normed"), B.sem("written")
    with ExitStack() as ph:
        sq = B.sb("sq", [P, 2, CH], F32, ph)
        rs = B.sb("rs", [P, 2, CH], F32, ph)
        ps = [B.ps("ps", [P, 512], ph) for _ in range(2)]
        pv = [B.ps("pv", [P, 512], ph) for _ in range(2)]
        block = ph.enter_context(nc.Block())

        @block.tensor
        def _(pe):
            for c in range(NCH):
                sl = slice(c * CH, (c + 1) * CH)
                if c >= 2:
                    pe.wait_ge(s_c, c - 1)
                nc.tensor.matmul(ps[c % 2][:, 0:CH], K.gmean[:, :], X[:, sl], start=True, stop=True).then_inc(s_mm, 1)
                pe.wait_ge(s_sq, c + 1)
                nc.tensor.matmul(pv[c % 2][:, 0:CH], K.gmean[:, :], sq[:, c % 2, :], start=True, stop=True).then_inc(s_var, 1)

        @block.scalar
        def _(ac):
            for c in range(NCH):
                sl = slice(c * CH, (c + 1) * CH)
                ac.wait_ge(s_c, c + 1)
                nc.scalar.activation(sq[:, c % 2, :], X[:, sl], ACT.Square).then_inc(s_sq, 1)
                ac.wait_ge(s_v, 3 * c + 1)
                nc.scalar.activation(rs[:, c % 2, :], rs[:, c % 2, :], ACT.Sqrt).then_inc(s_rt, 1)
            for c in range(NCH):
                sl = slice(c * CH, (c + 1) * CH)
                ac.wait_ge(s_v, 3 * c + 3)
                nc.scalar.activation(Y[:, sl], X[:, sl], func, bias=beta[:, :], scale=gamma[:, :]).then_inc(s_y, 1)

        @block.vector
        def _(ve):
            link = Chain(ve, s_v)
            for c in range(NCH):
                sl = slice(c * CH, (c + 1) * CH)
                ve.wait_ge(s_mm, c + 1)
                nc.vector.tensor_tensor(X[:, sl], X[:, sl], ps[c % 2][:, 0:CH], ALU.subtract).then_inc(s_c, 1)
                ve.wait_ge(s_var, c + 1)
                link(nc.vector.tensor_scalar(rs[:, c % 2, :], pv[c % 2][:, 0:CH], EPS, None, ALU.add))
                ve.wait_ge(s_rt, c + 1)
                link(nc.vector.reciprocal(rs[:, c % 2, :], rs[:, c % 2, :]))
                link(nc.vector.tensor_tensor(X[:, sl], X[:, sl], rs[:, c % 2, :], ALU.mult))


@phase
def vector_phase(nc, B, body):
    s_v = B.sem("vector_chain")
    with ExitStack() as ph:
        block = ph.enter_context(nc.Block())

        @block.vector
        def _(ve):
            body(Chain(ve, s_v))


@phase
def load_table(nc, B, table, tab):
    s = B.sem("table_loaded")
    with ExitStack() as ph:
        block = ph.enter_context(nc.Block())

        @block.sync
        def _(sp):
            sp.dma_start(tab[:, :, :], table.rearrange("(b p) d -> p b d", p=BN)).then_inc(s, 16)
            sp.wait_ge(s, 16)



@phase
def edge_pass(nc, B, K, kind, gather=None, gw=0, linear=None, lw=0, store=None, tab=None, tw=0,
              static=None, gcol=None, btcol=None, MX=None, heads=0, LG=None):
    uses_T = kind not in ("sum", "attr")
    is_max = kind in ("gatmax", "logits")
    NS = 2 if kind in ("gat", "attr", "attn") else 1
    HG = heads // 4 if heads else 0
    W = gw or lw
    s_idx = [B.sem("indices_read") for _ in range(RING)]
    s_t = [B.sem("operand_read") for _ in range(RING)]
    s_rows = [B.sem("rows_arrived") for _ in range(RING)]
    s_kept = [B.sem("rows_kept") for _ in range(RING)]
    s_free, s_go = B.sem("group_done"), B.sem("pool_go")
    s_exp, s_v, s_val = B.sem("expanded"), B.sem("vector_chain"), B.sem("value_ready")
    s_act, s_sum, s_lk, s_z = B.sem("activated"), B.sem("summed"), B.sem("logits_kept"), B.sem("acc_zeroed")
    row_incs = 64 if gw else 16
    with ExitStack() as ph:
        rows = B.sb("rows", [P, RING, GS, W], F32, ph)
        idx = B.sb("idx", [P, RING, GS], I32, ph) if gw else None
        T = B.sb("T", [TR, RING, GS * P], F32, ph) if uses_T else None
        oh = B.sb("oh", [P, GS, BN], F32, ph)
        m = B.sb("m", [P, GS, D], F32, ph)
        sq = B.sb("sq", [P, GS, D], F32, ph)
        w = B.sb("w", [P, GS, 8], F32, ph)
        z = B.sb("z", [P, GS, 8], F32, ph)
        y = B.sb("y", [P, 4, GS * 8], F32, ph)
        mx = B.sb("mx", [P, 2, GS], F32, ph)
        pe1 = B.ps("expanded", [P, GS, D], ph)
        pl = B.ps("edge_logits", [P, GS, 8], ph)
        pt = B.ps("logits_T", [heads, GS * P], ph) if is_max else None
        wT = B.sb("wT", [heads, GS * P], F32, ph) if is_max else None
        s_tt, s_tc = B.sem("logits_transposed"), B.sem("logits_copied")
        pm = [B.ps("spread", [P, GS, P], ph) for _ in range(2)] if is_max else None
        psum = B.ps("sums", [P, GS, 2, BN], ph)
        block = ph.enter_context(nc.Block())
        hv = {"gat": (4, 32), "attn": (8, 16)}.get(kind)

        @block.sync
        def _(sp):
            with sp.Fori(0, TRIPS) as i:
                for g in range(RING):
                    n = i * RING + g
                    sp.wait_ge(s_free, n + 1)
                    if gw:
                        sp.dma_start(idx[:, g, :], K.src_dram[:, bass.ds(n * GS, GS)]).then_inc(s_idx[g], 16)
                    else:
                        sp.dma_start(rows[:, g, :, :], linear[:, bass.ds(n * GS, GS), 0:W]).then_inc(s_rows[g], 16)
                    if uses_T:
                        sp.dma_start(T[:, g, :], K.t_dram[bass.ds(n, 1), :, :].rearrange("a r c -> (a r) c")).then_inc(s_t[g], 16)

        if gw:
            @block.gpsimd
            def _(po):
                with po.Fori(0, TRIPS) as i:
                    for g in range(RING):
                        po.wait_ge(s_idx[g], i * 16 + 16)
                        po.sem_inc(s_go, 1)
                        for k in range(GS):
                            nc.gpsimd.indirect_dma_start(
                                out=rows[:, g, k, :], out_offset=None, in_=gather,
                                in_offset=bass.IndirectOffsetOnAxis(ap=idx[:, g, k:k + 1], axis=0)).then_inc(s_rows[g], 16)

        @block.tensor
        def _(pe):
            with pe.Fori(0, TRIPS) as i:
                for g in range(RING):
                    n = i * RING + g

                    def bucket(k):
                        return pe.value_load(K.bucket[0:1, bass.ds(n * GS + k, 1)], min_val=0, max_val=NBUK - 1)

                    if uses_T:
                        pe.wait_ge(s_t[g], i * 16 + 16)
                    if kind in ("gat", "attn", "conv", "logits"):
                        wd = tw
                        for k in range(GS):
                            v = bucket(k)
                            o = pe1[:, k, 0:wd] if wd == D else pl[:, k, 0:wd]
                            mm = nc.tensor.matmul(o, T[0:BN, g, k * P:(k + 1) * P], tab[:, bass.ds(v * wd, wd)],
                                                  start=True, stop=kind != "conv", skip_group_check=True)
                            if kind == "conv":
                                mm = nc.tensor.matmul(o, T[:, g, k * P:(k + 1) * P], static[:, :], start=False,
                                                      stop=True, skip_group_check=True)
                            if kind == "logits":
                                mm = nc.tensor.matmul(pl[:, k, :], T[:, g, k * P:(k + 1) * P], static[:, :],
                                                      start=True, stop=True, skip_group_check=True)
                        mm.then_inc(s_exp, 1)
                    if kind == "prod":
                        for k in range(GS):
                            mm = nc.tensor.matmul(pe1[:, k, :], T[:, g, k * P:(k + 1) * P], static[:, :],
                                                  start=True, stop=True, skip_group_check=True)
                        mm.then_inc(s_exp, 1)
                    if is_max:
                        if kind == "gatmax":
                            pe.wait_ge(s_rows[g], i * row_incs + row_incs)
                            pe.wait_ge(s_free, n + RING)
                        else:
                            pe.wait_ge(s_val, n + 1)
                        for k in range(GS):
                            a = rows[:, g, k, D:D + 4] if kind == "gatmax" else w[:, k, :]
                            mm = nc.tensor.transpose(pt[:, k * P:(k + 1) * P], a, K.ident[:, :])
                        mm.then_inc(s_tt, 1)
                        pe.wait_ge(s_tc, n + 1)
                        for hg in range(HG):
                            nc.tensor.matmul(pm[hg][:, :, :].rearrange("p k e -> p (k e)"),
                                             K.neg[:, :, :].rearrange("p h n -> p (h n)"), T[:, g, :],
                                             start=True, stop=False)
                            mm = nc.tensor.matmul(pm[hg][:, :, :].rearrange("p k e -> p (k e)"),
                                                  K.hs32[0:heads, hg, :], wT[:, :], start=False, stop=True)
                        mm.then_inc(s_sum, 1)
                    else:
                        if kind in ("sum", "attr"):
                            pe.wait_ge(s_rows[g], i * row_incs + row_incs)
                        pe.wait_ge(s_val, n + 1)
                        for k in range(GS):
                            src = rows[:, g, k, 0:D] if kind in ("sum", "attr") else m[:, k, :]
                            mm = nc.tensor.matmul(psum[:, k, 0, :], src, oh[:, k, :], start=True, stop=True,
                                                  skip_group_check=True)
                            if NS == 2:
                                second = K.ones[:, :] if kind == "attr" else w[:, k, 0:hv[0]]
                                mm = nc.tensor.matmul(psum[0:second.shape[1], k, 1, :], second, oh[:, k, :], start=True, stop=True,
                                                      skip_group_check=True)
                        mm.then_inc(s_sum, 1)

        @block.scalar
        def _(ac):
            with ac.Fori(0, TRIPS) as i:
                for g in range(RING):
                    n = i * RING + g
                    if store is not None:
                        ac.wait_ge(s_rows[g], i * row_incs + row_incs)
                        s0, s1, dram = store
                        ac.dma_start(dram[:, bass.ds(n * GS, GS), :], rows[:, g, :, s0:s1]).then_inc(s_kept[g], 16)
                    if kind in ("gat", "attn"):
                        ac.wait_ge(s_lk, n + 1)
                        nc.scalar.activation(w[:, :, 0:hv[0]], z[:, :, 0:hv[0]], ACT.Exp).then_inc(s_act, 1)
                    if kind == "conv":
                        ac.wait_ge(s_lk, 2 * n + 1)
                        nc.scalar.activation(sq[:, :, :], m[:, :, :], ACT.Square).then_inc(s_act, 1)
                        ac.wait_ge(s_lk, 2 * n + 2)
                        nc.scalar.activation(m[:, :, :], sq[:, :, :], ACT.Silu).then_inc(s_act, 1)
                    if is_max:
                        ac.wait_ge(s_tt, n + 1)
                        nc.scalar.copy(wT[:, :], pt[:, :]).then_inc(s_tc, 1)
                    if kind == "logits":
                        nc.scalar.copy(LG[:, bass.ds(n * GS * 8, GS * 8)],
                                       w[:, :, :].rearrange("p k h -> p (k h)")).then_inc(s_act, 1)

        per = {"gatmax": 5, "gat": 7, "sum": 4, "attr": 4, "conv": 19, "logits": 7, "attn": 4, "prod": 4}[kind]

        @block.vector
        def _(ve):
            if is_max:
                nc.vector.memset(MX[:, :, :], -BIG).then_inc(s_z, 1)
            else:
                nc.vector.memset(K.acc[:, 0:NS, :], 0.0).then_inc(s_z, 1)
            nc.vector.memset(psum[:, :, :, :], 0.0).then_inc(s_z, 1)
            ve.wait_ge(s_z, 2)
            ve.sem_inc(s_free, RING)
            with ve.Fori(0, TRIPS) as i:
                link = Chain(ve, s_v, i * (per * RING))
                for g in range(RING):
                    n = i * RING + g

                    def bucket(k):
                        return ve.value_load(K.bucket[0:1, bass.ds(n * GS + k, 1)], min_val=0, max_val=NBUK - 1)

                    if not is_max:
                        o = nc.vector.tensor_tensor(oh[:, :, :], bc(K.iota[:, 0:BN].unsqueeze(1), [P, GS, BN]),
                                                    bc(K.dls[:, bass.ds(n * GS, GS)].unsqueeze(2), [P, GS, BN]),
                                                    ALU.is_equal)
                        if kind in ("sum", "attr"):
                            o.then_inc(s_val, 1)
                    if kind in ("gat", "attn", "conv", "prod", "logits"):
                        ve.wait_ge(s_exp, n + 1)
                    if kind not in ("sum", "attr", "gatmax"):
                        ve.wait_ge(s_rows[g], i * row_incs + row_incs)
                    r = rows[:, g, :, 0:D]
                    if kind == "gat":
                        link(nc.vector.tensor_tensor(w[:, :, 4:8], rows[:, g, :, D:D + 4], pl[:, :, 0:4], ALU.add))
                        link(nc.vector.scalar_tensor_tensor(out=z[:, :, 4:8], in0=w[:, :, 4:8], scalar=0.2,
                                                            in1=w[:, :, 4:8], op0=ALU.mult, op1=ALU.max))
                        link(nc.vector.tensor_tensor(z[:, :, 0:4], z[:, :, 4:8], pl[:, :, 4:8], ALU.subtract))
                        ve.sem_inc(s_lk, 1)
                    if kind == "attn":
                        nc.vector.tensor_tensor(z[:, :, :], LG[:, bass.ds(n * GS * 8, GS * 8)].rearrange("p (k h) -> p k h", h=8),
                                                pl[:, :, :], ALU.subtract).then_inc(s_lk, 1)
                    if kind in ("gat", "attn"):
                        ve.wait_ge(s_act, n + 1)
                        h, f = hv
                        for k in range(GS):
                            mm = nc.vector.tensor_tensor(m[:, k, :].rearrange("p (h f) -> p h f", h=h),
                                                         rows[:, g, k, 0:D].rearrange("p (h f) -> p h f", h=h),
                                                         bc(w[:, k, 0:h].unsqueeze(2), [P, h, f]), ALU.mult)
                        mm.then_inc(s_val, 1)
                    if kind == "prod":
                        nc.vector.tensor_tensor(m[:, :, :], r, pe1[:, :, :], ALU.mult).then_inc(s_val, 1)
                    if kind == "logits":
                        link(nc.vector.tensor_tensor(m[:, :, :], r, pe1[:, :, :], ALU.mult))
                        link(nc.vector.tensor_reduce(z[:, :, :].rearrange("p k h -> p (k h)"),
                                                     m[:, :, :].rearrange("p k (h f) -> p (k h) f", h=8), AX.X, ALU.add))
                        nc.vector.tensor_tensor(w[:, :, :], z[:, :, :], pl[:, :, :], ALU.add).then_inc(s_val, 1)
                    if kind == "conv":
                        nc.vector.tensor_tensor(m[:, :, :], r, pe1[:, :, :], ALU.add).then_inc(s_lk, 1)
                        ve.wait_ge(s_act, 2 * n + 1)
                        link(nc.vector.tensor_reduce(y[:, 0, :], sq[:, :, :].rearrange("p k (h f) -> p (k h) f", h=8),
                                                     AX.X, ALU.add))
                        link(nc.vector.tensor_scalar(y[:, 0, :], y[:, 0, :], 1.0 / 16, EPS, ALU.mult, ALU.add))
                        link(nc.vector.tensor_scalar(y[:, 1, :].bitcast(I32), y[:, 0, :].bitcast(I32), -0.5,
                                                     float(0x5f3759df), ALU.mult, ALU.add))
                        for _ in range(3):
                            link(nc.vector.scalar_tensor_tensor(out=y[:, 2, :], in0=y[:, 1, :], scalar=-0.5,
                                                                in1=y[:, 0, :], op0=ALU.mult, op1=ALU.mult))
                            link(nc.vector.tensor_tensor(y[:, 2, :], y[:, 2, :], y[:, 1, :], ALU.mult))
                            link(nc.vector.scalar_tensor_tensor(out=y[:, 1, :], in0=y[:, 2, :], scalar=1.5,
                                                                in1=y[:, 1, :], op0=ALU.add, op1=ALU.mult))
                        link(nc.vector.tensor_tensor(m[:, :, :].rearrange("p k (h f) -> p (k h) f", h=8),
                                                     m[:, :, :].rearrange("p k (h f) -> p (k h) f", h=8),
                                                     bc(y[:, 1, :].unsqueeze(2), [P, GS * 8, 16]), ALU.mult))
                        link(nc.vector.tensor_tensor(m[:, :, :], m[:, :, :], bc(gcol.unsqueeze(1), [P, GS, D]), ALU.mult))
                        link(nc.vector.tensor_tensor(sq[:, :, :], m[:, :, :], bc(btcol.unsqueeze(1), [P, GS, D]), ALU.add))
                        ve.sem_inc(s_lk, 1)
                        ve.wait_ge(s_act, 2 * n + 2)
                        ve.sem_inc(s_val, 1)
                    ve.wait_ge(s_sum, n + 1)
                    if is_max:
                        for hg in range(HG):
                            mm = nc.vector.tensor_reduce(mx[:, hg, :], pm[hg][:, :, :], AX.X, ALU.max)
                        link(mm)
                        for k in range(GS):
                            v = bucket(k)
                            dst = MX[:, :, bass.ds(v, 1)].rearrange("p g a -> p (g a)")
                            link(nc.vector.tensor_tensor(dst, dst, mx[:, 0:HG, k], ALU.max))
                    else:
                        for k in range(GS):
                            v = bucket(k)
                            dst = K.acc[:, 0:NS, bass.ds(v * BN, BN)]
                            link(nc.vector.tensor_tensor(dst, dst, psum[:, k, 0:NS, :], ALU.add))
                    if kind == "logits":
                        ve.wait_ge(s_act, n + 1)
                    if store is not None:
                        ve.wait_ge(s_kept[g], i * 16 + 16)
                    ve.sem_inc(s_free, 1)
                assert link.k == per * RING, (kind, link.k)



def bucket_maxima(nc, B, K, MX, groups, ps, pe):
    for hg in range(groups):
        for h in range(4):
            m = nc.tensor.matmul(ps[hg][:, h * NB:(h + 1) * NB], K.ident[:, 32 * h:32 * h + 32], MX[:, hg, :],
                                 start=True, stop=True, skip_group_check=True)
    return m


@phase
def gat_tables(nc, B, K, T0, MX, tab8, u4):
    s_ld, s_mm, s_v, s_e = B.sem("logits_loaded"), B.sem("maxima_spread"), B.sem("table_chain"), B.sem("own_weight")
    s_ws, s_cp = B.sem("weight_spread"), B.sem("weight_copied")
    per = 512 // BN
    banks = -(-NB // per)
    with ExitStack() as ph:
        a = B.sb("a", [BN, NB, 8], F32, ph)
        t = B.sb("t", [BN, NB, 4], F32, ph)
        u = B.sb("u", [BN, NB, 4], F32, ph)
        ps = [B.ps("ps", [BN, 512], ph)]
        pw = [B.ps("pw", [4, 512], ph) for _ in range(2)]
        block = ph.enter_context(nc.Block())
        tab = tab8[:, :].rearrange("p (b c) -> p b c", c=8)

        @block.sync
        def _(sp):
            sp.dma_start(a[:, :, :], T0.rearrange("(b p) d -> p b d", p=BN)[:, :, D:D + 8]).then_inc(s_ld, 16)

        @block.tensor
        def _(pe):
            bucket_maxima(nc, B, K, MX, 1, ps, pe).then_inc(s_mm, 1)
            pe.wait_ge(s_e, 1)
            for c in range(banks):
                if c >= 2:
                    pe.wait_ge(s_cp, c - 1)
                for b in range(c * per, min(NB, (c + 1) * per)):
                    m = nc.tensor.matmul(pw[c % 2][:, (b - c * per) * BN:(b - c * per + 1) * BN],
                                         u[:, b, :], K.ident[0:BN, 0:BN],
                                         start=True, stop=True, skip_group_check=True)
                m.then_inc(s_ws, 1)

        @block.scalar
        def _(ac):
            ac.wait_ge(s_v, 8)
            nc.scalar.activation(u[:, :, :], u[:, :, :], ACT.Exp).then_inc(s_e, 1)

        @block.vector
        def _(ve):
            link = Chain(ve, s_v)
            ve.wait_ge(s_ld, 16)
            ve.wait_ge(s_mm, 1)
            mxv = ps[0][:, 0:4 * NB].rearrange("p (h b) -> p b h", h=4)
            link(nc.vector.tensor_tensor(t[:, :, :], a[:, :, 0:4], mxv, ALU.max))
            link(nc.vector.tensor_tensor(t[:, :, :], t[:, :, :], a[:, :, 4:8], ALU.add))
            link(nc.vector.scalar_tensor_tensor(out=tab[:, :, 4:8], in0=t[:, :, :], scalar=0.2, in1=t[:, :, :],
                                                op0=ALU.mult, op1=ALU.max))
            link(nc.vector.tensor_copy(tab[:, :, 0:4], a[:, :, 4:8]))
            link(nc.vector.tensor_tensor(t[:, :, :], a[:, :, 0:4], a[:, :, 4:8], ALU.add))
            link(nc.vector.tensor_scalar(u[:, :, :], t[:, :, :], 0.2, None, ALU.mult))
            link(nc.vector.tensor_tensor(u[:, :, :], u[:, :, :], t[:, :, :], ALU.max))
            link(nc.vector.tensor_tensor(u[:, :, :], u[:, :, :], tab[:, :, 4:8], ALU.subtract))
            for c in range(banks):
                w = min(NP, (c + 1) * 512) - c * 512
                ve.wait_ge(s_ws, c + 1)
                nc.vector.tensor_copy(u4[:, c * 512:c * 512 + w], pw[c % 2][:, 0:w]).then_inc(s_cp, 1)


@phase
def attn_table(nc, B, K, MX, tab8):
    s_mm, s_v = B.sem("maxima_spread"), B.sem("table_chain")
    with ExitStack() as ph:
        ps = [B.ps("ps", [BN, 512], ph) for _ in range(2)]
        block = ph.enter_context(nc.Block())

        @block.tensor
        def _(pe):
            bucket_maxima(nc, B, K, MX, 2, ps, pe).then_inc(s_mm, 1)

        @block.vector
        def _(ve):
            ve.wait_ge(s_mm, 1)
            tab = tab8[:, :].rearrange("p (b c) -> p b c", c=8)
            for hg in range(2):
                nc.vector.tensor_copy(tab[:, :, 4 * hg:4 * hg + 4],
                                      ps[hg][:, 0:4 * NB].rearrange("p (h b) -> p b h", h=4)).then_inc(s_v, 1)
            ve.wait_ge(s_v, 2)


@phase
def batch_norm(nc, B, K):
    s_v, s_r = B.sem("stat_chain"), B.sem("root")
    O = K.acc[:, 0, 0:N]
    with ExitStack() as ph:
        st = B.sb("st", [P, 4], F32, ph)
        block = ph.enter_context(nc.Block())

        @block.scalar
        def _(ac):
            ac.wait_ge(s_v, 6)
            nc.scalar.activation(st[:, 2:3], st[:, 1:2], ACT.Sqrt).then_inc(s_r, 1)

        @block.vector
        def _(ve):
            link = Chain(ve, s_v)
            link(nc.vector.tensor_reduce(st[:, 0:1], O, AX.X, ALU.add))
            link(nc.vector.tensor_scalar(st[:, 0:1], st[:, 0:1], 1.0 / N, None, ALU.mult))
            link(nc.vector.tensor_scalar(O, O, st[:, 0:1], None, ALU.subtract))
            link(nc.vector.tensor_tensor(K.acc[:, 1, 0:N], O, O, ALU.mult))
            link(nc.vector.tensor_reduce(st[:, 1:2], K.acc[:, 1, 0:N], AX.X, ALU.add))
            link(nc.vector.tensor_scalar(st[:, 1:2], st[:, 1:2], 1.0 / N, EPS, ALU.mult, ALU.add))
            ve.wait_ge(s_r, 1)
            link(nc.vector.reciprocal(st[:, 3:4], st[:, 2:3]))
            link(nc.vector.tensor_tensor(st[:, 3:4], st[:, 3:4], K.c["L0_gnn_gamma"][:, :], ALU.mult))
            link(nc.vector.tensor_scalar(O, O, st[:, 3:4], K.c["L0_gnn_beta"][:, :], ALU.mult, ALU.add))
            link(nc.vector.tensor_tensor(K.X[:, 0:N], K.X[:, 0:N], O, ALU.add))


@phase
def store_x(nc, B, K, out):
    s_tr, s_cp, s_st = B.sem("transposed"), B.sem("copied"), B.sem("result_stored")
    with ExitStack() as ph:
        xn = B.sb("xn", [P, TILES, D], F32, ph)
        ps = [B.ps("ps", [P, P], ph) for _ in range(2)]
        block = ph.enter_context(nc.Block())
        full, rest = N // P, N % P

        @block.tensor
        def _(pe):
            for t in range(TILES):
                if t >= 2:
                    pe.wait_ge(s_cp, t - 1)
                nc.tensor.transpose(ps[t % 2][:, :], K.X[:, t * P:(t + 1) * P], K.ident[:, :]).then_inc(s_tr, 1)

        @block.vector
        def _(ve):
            for t in range(TILES):
                ve.wait_ge(s_tr, t + 1)
                nc.vector.tensor_copy(xn[:, t, :], ps[t % 2][:, :]).then_inc(s_cp, 1)

        @block.sync
        def _(sp):
            sp.wait_ge(s_cp, TILES)
            sp.dma_start(out[0:full * P, :].rearrange("(t p) d -> p t d", p=P), xn[:, 0:full, :]).then_inc(s_st, 16)
            sp.dma_start(out[full * P:N, :], xn[0:rest, full, :]).then_inc(s_st, 16)
            sp.wait_ge(s_st, 32)


def program(nc, A, out, upto=99):
    with ExitStack() as ctx:
        B = Build(nc, ctx)

        class K:
            pass

        K.rec = B.dram("records", [SLOTS * P, REC])
        K.bucket_dram = B.dram("slot_buckets", [512], I32)
        K.src_dram = B.dram("sources", [P, SLOTS], I32)
        K.t_dram = B.dram("operands", [GROUPS, TR, GS * P])
        K.X = B.sb("X", [P, NP])
        K.H = B.sb("H", [P, NP])
        K.acc = B.sb("acc", [P, 2, NP])
        K.cnt = B.sb("cnt", [P, NP])
        constants(nc, B, A, K)
        rank_edges(nc, B, A, K)
        scatter_records(nc, B, A, K)
        make_operands(nc, B, A, K)
        load_x(nc, B, A, K)
        rec_v = K.rec.rearrange("(s p) w -> p s w", p=P)
        V = nc.vector
        acc0, acc1 = K.acc[:, 0, :], K.acc[:, 1, :]

        norm_nodes(nc, B, A, K)
        T0 = B.dram("gat_rows", [NP, 136])
        gs = B.dram("gat_slot_rows", [P, SLOTS, 132])
        project_nodes(nc, B, K, [(K.H, [K.w0[:, :]])], 136, T0)
        with ExitStack() as l0:
            MX = B.sb("MX", [P, 1, NB], F32, l0)
            tab8 = B.sb("tab8", [BN, NB * 8], F32, l0)
            wsf = B.sb("wsf", [P, NP], F32, l0)
            u4 = B.sb("own_weights", [4, NP], F32, l0)
            r4 = B.sb("inverse_sums", [4, NP], F32, l0)
            edge_pass(nc, B, K, "gatmax", gather=T0, gw=136, store=(0, 132, gs), MX=MX, heads=4)
            gat_tables(nc, B, K, T0, MX, tab8, u4)
            edge_pass(nc, B, K, "gat", linear=gs, lw=132, tab=tab8, tw=8, heads=4)

            def inverse(link):
                link(V.scalar_tensor_tensor(out=r4[:, :], in0=acc1[0:4, :], scalar=1e-16, in1=u4[:, :],
                                            op0=ALU.add, op1=ALU.add))
                link(V.reciprocal(r4[:, :], r4[:, :]))

            def spread(sl, ps, link):
                link(V.tensor_copy(wsf[:, sl], ps))

            def own(sl, ps, link):
                link(V.tensor_tensor(wsf[:, sl], ps, wsf[:, sl], ALU.mult))
                link(V.tensor_tensor(acc0[:, sl], acc0[:, sl], wsf[:, sl], ALU.add))

            def scale(sl, ps, link):
                link(V.tensor_tensor(acc0[:, sl], acc0[:, sl], ps, ALU.mult))
                link(V.tensor_scalar(acc0[:, sl], acc0[:, sl], K.c["L0_gnn_bias"][:, :], None, ALU.add))

            vector_phase(nc, B, inverse)
            feature_product(nc, B, K, [(K.hs32[0:4, 0, :], u4)], spread, 1)
            feature_product(nc, B, K, [(K.w0[:, 0:D], K.H)], own, 2)
            feature_product(nc, B, K, [(K.hs32[0:4, 0, :], r4)], scale, 2)
        batch_norm(nc, B, K)
        if upto <= 0:
            return store_x(nc, B, K, out)

        norm_nodes(nc, B, A, K)
        edge_pass(nc, B, K, "attr", linear=rec_v, lw=D)
        with ExitStack() as l1:
            agg = B.sb("agg", [P, NP], F32, l1)
            Y = B.dram("gin_rows", [NP, D])

            def embed(sl, ps, link):
                link(V.tensor_copy(K.cnt[:, sl], acc1[:, sl]))
                link(V.scalar_tensor_tensor(out=agg[:, sl], in0=acc1[:, sl], scalar=K.c["L1_gnn_be"][:, :], in1=ps,
                                            op0=ALU.mult, op1=ALU.add))

            feature_product(nc, B, K, [(K.w["L1_gnn_We"][:, :], acc0)], embed, 2)
            both = [(K.H, [K.w1a[:, :]]), (agg, [K.w1b[:, :]])]
            project_nodes(nc, B, K, both, D, Y)
            edge_pass(nc, B, K, "sum", gather=Y, gw=D)

            def hidden(sl, ps, link):
                link(V.tensor_tensor(acc0[:, sl], acc0[:, sl], ps, ALU.add))
                link(V.tensor_scalar(acc0[:, sl], acc0[:, sl], K.c["L1_gnn_b1"][:, :], 0.0, ALU.add, ALU.max))

            feature_product(nc, B, K, [(K.w1a[:, :], K.H), (K.w1b[:, :], agg)], hidden, 2)

            def add_out(sl, ps, link):
                link(V.scalar_tensor_tensor(out=K.X[:, sl], in0=ps, scalar=K.c["L1_gnn_b2"][:, :], in1=K.X[:, sl],
                                            op0=ALU.add, op1=ALU.add))

            feature_product(nc, B, K, [(K.w["L1_gnn_W2"][:, :], acc0)], add_out, 1)
        if upto <= 1:
            return store_x(nc, B, K, out)

        norm_nodes(nc, B, A, K)
        rows_a, rows_b = B.dram("dst_rows", [NP, D]), B.dram("src_rows", [NP, D])
        for i, c in enumerate(("c1", "c2")):
            inp = K.H if i == 0 else acc1
            project_nodes(nc, B, K, [(inp, [K.ca[i][:, :]])], D, rows_a)
            project_nodes(nc, B, K, [(inp, [K.cb[i][:, :]])], D, rows_b)
            with ExitStack() as l2:
                tab = B.sb("tab", [BN, NB, D], F32, l2)
                load_table(nc, B, rows_a, tab)
                edge_pass(nc, B, K, "conv", gather=rows_b, gw=D, tab=tab[:, :, :].rearrange("p b d -> p (b d)"),
                          tw=D, static=K.cs[i], gcol=K.r[f"L2_gnn_{c}_g"][:, :], btcol=K.r[f"L2_gnn_{c}_bt"][:, :])

            def mean(sl, ps, link):
                link(V.scalar_tensor_tensor(out=acc1[:, sl], in0=K.cnt[:, sl], scalar=K.c[f"L2_gnn_{c}_b2"][:, :],
                                            in1=ps, op0=ALU.mult, op1=ALU.add))
                link(V.tensor_scalar(acc0[:, sl], K.cnt[:, sl], 1.0, None, ALU.max))
                link(V.reciprocal(acc0[:, sl], acc0[:, sl]))
                link(V.tensor_tensor(acc1[:, sl], acc1[:, sl], acc0[:, sl], ALU.mult))

            feature_product(nc, B, K, [(K.w[f"L2_gnn_{c}_w2"][:, :], acc0)], mean, 4)
            n = f"L2_gnn_n{i + 1}_"
            group_norm(nc, B, K, acc1, K.c[n + "g"], K.c[n + "b"], ACT.Silu, acc1)
            if i == 0:
                vector_phase(nc, B, lambda link: link(
                    V.tensor_scalar(acc1, acc1, K.tvec[:, :], None, ALU.add)))
            else:
                vector_phase(nc, B, lambda link: link(V.tensor_tensor(K.H[:, :], K.H[:, :], acc1, ALU.add)))
        KV, Q = B.dram("kv_rows", [NP, 2 * D]), rows_a
        vs = B.dram("slot_values", [P, SLOTS, D])
        project_nodes(nc, B, K, [(K.H, [K.w["L2_gnn_kw"][:, :], K.w["L2_gnn_vw"][:, :]])], 2 * D, KV,
                      row=[K.r["L2_gnn_kb"][:, :], K.r["L2_gnn_vb"][:, :]])
        project_nodes(nc, B, K, [(K.H, [K.w["L2_gnn_qw"][:, :]])], D, Q, row=[K.r["L2_gnn_qb"][:, :]], scale=0.25)
        with ExitStack() as l2:
            MX = B.sb("MX", [P, 2, NB], F32, l2)
            LG = B.sb("LG", [P, SLOTS * 8], F32, l2)
            with ExitStack() as l3:
                tab = B.sb("tab", [BN, NB, D], F32, l3)
                load_table(nc, B, Q, tab)
                edge_pass(nc, B, K, "logits", gather=KV, gw=2 * D, store=(D, 2 * D, vs), MX=MX, heads=8, LG=LG,
                          tab=tab[:, :, :].rearrange("p b d -> p (b d)"), tw=D, static=K.ew)
            tab8 = B.sb("tab8", [BN, NB * 8], F32, l2)
            attn_table(nc, B, K, MX, tab8)
            edge_pass(nc, B, K, "attn", linear=vs, lw=D, tab=tab8, tw=8, heads=8, LG=LG)

        def divide(link):
            link(V.tensor_scalar(acc1[0:8, :], acc1[0:8, :], 1e-6, None, ALU.max))
            link(V.reciprocal(acc1[0:8, :], acc1[0:8, :]))

        vector_phase(nc, B, divide)

        def scale8(sl, ps, link):
            link(V.tensor_tensor(acc0[:, sl], acc0[:, sl], ps, ALU.mult))

        feature_product(nc, B, K, [(K.hs16[:, :], acc1[0:8, :])], scale8, 1)

        def attn_out(sl, ps, link):
            link(V.tensor_scalar(acc1[:, sl], ps, K.c["L2_gnn_ob"][:, :], None, ALU.add))

        feature_product(nc, B, K, [(K.w["L2_gnn_ow"][:, :], acc0)], attn_out, 1)
        group_norm(nc, B, K, acc1, K.c["L2_gnn_an_g"], K.c["L2_gnn_an_b"], ACT.Identity, acc1)

        def add_layer(link):
            link(V.tensor_tensor(K.X[:, :], K.X[:, :], K.H[:, :], ALU.add))
            link(V.tensor_tensor(K.X[:, :], K.X[:, :], acc1, ALU.add))

        vector_phase(nc, B, add_layer)
        if upto <= 2:
            return store_x(nc, B, K, out)

        norm_nodes(nc, B, A, K)
        project_nodes(nc, B, K, [(K.H, [K.w["L3_gnn_W"][:, :]])], D, rows_a)
        edge_pass(nc, B, K, "prod", gather=rows_a, gw=D, static=K.w3)
        vector_phase(nc, B, lambda link: link(V.scalar_tensor_tensor(
            out=K.X[:, :], in0=acc0, scalar=K.c["L3_gnn_b"][:, :], in1=K.X[:, :], op0=ALU.add, op1=ALU.add)))
        store_x(nc, B, K, out)


def kernel(**inputs):
    import numpy as _np
    import concourse.bacc as _bacc
    from concourse import mybir as _mybir
    from concourse.bass_utils import run_bass_kernel_spmd as _run

    nc = _bacc.Bacc("TRN2", target_bir_lowering=False, num_devices=1)
    arrays, args = {}, {}
    for name, a in inputs.items():
        a = _np.ascontiguousarray(a)
        arrays[f"in_{name}"] = a
        args[name] = nc.dram_tensor(f"in_{name}", a.shape, _mybir.dt.from_np(a.dtype), kind="ExternalInput").ap()
    out = nc.dram_tensor("out_0", (N, D), _mybir.dt.float32, kind="ExternalOutput").ap()
    program(nc, args, out)
    r = _run(nc, [arrays], core_ids=[0])
    return r.results[0]["out_0"]
```

```python
import concourse.bass as bass
from concourse import mybir
from contextlib import ExitStack

F32 = mybir.dt.float32
I32 = mybir.dt.int32
U8 = mybir.dt.uint8
ALU = mybir.AluOpType
ACT = mybir.ActivationFunctionType
AX = mybir.AxisListType

N = 3125
E = 50000
D = 128
P = 128
BN = 32
NBUK = -(-N // BN)
TILES = -(-N // P)
NP = TILES * P
NB = NP // BN
EP = 125
EC = E // EP
RING = 4
GS = 4
CAPS = 5
CAP = CAPS * P
GB = 2
MG = GB * CAPS
MGROUPS = NB // GB
MSLOTS = NB * CAPS
MW = MG * P
OVER = MSLOTS * P
SLOTS_MIN = (E - CAP + NBUK * (P - 1)) // P
TRIPS = -(-SLOTS_MIN // (RING * GS))
GROUPS = TRIPS * RING
SLOTS = GROUPS * GS
REC = 152
META = 24
TR = 96
CH = 400
NCH = NP // CH
BF16 = mybir.dt.bfloat16
BIG = 1.0e30
EPS = 1e-5


class Chain:

    def __init__(self, eng, sem, base=0):
        self.eng, self.sem, self.base, self.k = eng, sem, base, 0

    def __call__(self, ins):
        self.k += 1
        ins.then_inc(self.sem, 1)
        self.eng.wait_ge(self.sem, self.base + self.k)


class Build:

    def __init__(self, nc, ctx):
        self.nc, self.ctx, self.n = nc, ctx, 0

    def name(self, s):
        self.n += 1
        return f"{s}_{self.n}"

    def sb(self, s, shape, dt=F32, ctx=None):
        return (ctx or self.ctx).enter_context(self.nc.sbuf_tensor(self.name(s), shape, dt))

    def ps(self, s, shape, ctx, dt=F32):
        return ctx.enter_context(self.nc.psum_tensor(self.name(s), shape, dt))

    def sem(self, s):
        self.sems.append(self.nc.alloc_semaphore(self.name(s)))
        return self.sems[-1]

    def dram(self, s, shape, dt=F32):
        return self.nc.dram_tensor(self.name(s), shape, dt, kind="Internal").ap()


def phase(f):
    def run(nc, B, *args, **kw):
        B.sems = []
        f(nc, B, *args, **kw)
        nc.clear_and_free_semaphores(B.sems)
        nc.all_engine_barrier()
    return run


def bc(ap, shape):
    return ap.to_broadcast(shape)


def overflowed(eng, K):
    return eng.If(eng.value_load(K.over[0:1, 0:1], min_val=0, max_val=SLOTS) > 0)


def pipelined(eng, first, second):
    half = (MGROUPS - 2) // 2
    first(0, 0, 0)
    with eng.Fori(0, half) as i:
        first(i * 2 + 1, 1, i)
        second(i * 2, 0, i)
        first(i * 2 + 2, 0, i + 1)
        second(i * 2 + 1, 1, i)
    first(MGROUPS - 1, 1, half)
    second(MGROUPS - 2, 0, half)
    second(MGROUPS - 1, 1, half)


def span(n, size):
    return slice(n * size, (n + 1) * size) if isinstance(n, int) else bass.ds(n * size, size)



WEIGHTS = ["L1_gnn_We", "L1_gnn_W2", "L2_gnn_c1_w2", "L2_gnn_c2_w2", "L2_gnn_qw", "L2_gnn_kw",
           "L2_gnn_vw", "L2_gnn_ow", "L3_gnn_W"]
COLS = ["L0_gnn_gamma", "L0_gnn_beta", "L1_gnn_be", "L1_gnn_b1", "L1_gnn_b2", "L2_gnn_c1_b2",
        "L2_gnn_c2_b2", "L2_gnn_tm_b", "L2_gnn_n1_g", "L2_gnn_n1_b", "L2_gnn_n2_g", "L2_gnn_n2_b",
        "L2_gnn_ob", "L2_gnn_an_g", "L2_gnn_an_b", "L3_gnn_b"]
ROWS = ["L2_gnn_c1_g", "L2_gnn_c1_bt", "L2_gnn_c2_g", "L2_gnn_c2_bt", "L2_gnn_qb", "L2_gnn_kb",
        "L2_gnn_vb"]


@phase
def constants(nc, B, A, K):
    s_w = B.sem("weights_loaded")
    s_p = B.sem("patterns_made")
    s_z = B.sem("zeroed")
    s_v = B.sem("vector_chain")
    s_a = B.sem("silu_made")
    s_t = B.sem("time_product")
    K.ident = B.sb("ident", [P, P])
    K.tri = B.sb("tri", [P, P])
    K.ones = B.sb("ones", [P, P])
    K.iota = B.sb("iota", [P, P])
    K.part = B.sb("part", [P, 1])
    K.gmean = B.sb("gmean", [P, P])
    K.slotid = B.sb("slotid", [P, 4])
    K.neg = B.sb("neg", [TR, 4, BN])
    K.sel = B.sb("sel", [TR, 64])
    K.negb = B.sb("negb", [TR, 4 * BN], BF16)
    K.hs32 = B.sb("hs32", [8, 2, P])
    K.hs16 = B.sb("hs16", [8, P])
    K.eqm = B.sb("eqm", [64, 1])
    K.eqc = B.sb("eqc", [64, 1])
    K.w = {n: B.sb(n, [D, D]) for n in WEIGHTS}
    K.c = {n: B.sb(n, [D, 1]) for n in COLS}
    K.c["L0_gnn_bias"] = B.sb("L0_bias", [D, 1])
    K.r = {n: B.sb(n, [P, D]) for n in ROWS}
    K.w0 = B.sb("L0_W", [D, 136])
    K.w1a = B.sb("L1_W1a", [D, D])
    K.w1b = B.sb("L1_W1b", [D, D])
    K.ca = [B.sb("conv_dst_w", [D, D]) for _ in range(2)]
    K.cb = [B.sb("conv_src_w", [D, D]) for _ in range(2)]
    K.cs = [B.sb("conv_edge_w", [TR, D]) for _ in range(2)]
    K.ew = B.sb("logit_edge_w", [TR, 8])
    K.w3 = B.sb("L3_edge_w", [TR, D])
    K.tvec = B.sb("time_vector", [D, 1])
    with ExitStack() as ph:
        att = B.sb("att", [P, 2, D], ctx=ph)
        prod = B.sb("prod", [P, 2, D], ctx=ph)
        gm = B.sb("gm", [P, 8, 8], ctx=ph)
        te = B.sb("te", [P, 4], ctx=ph)
        tes = B.sb("tes", [P, 4], ctx=ph)
        tw = B.sb("tw", [P, 4, D], ctx=ph)
        ii = B.sb("ii", [P, P], I32, ctx=ph)
        pi = B.sb("pi", [P, 1], I32, ctx=ph)
        si = B.sb("si", [P, 4], I32, ctx=ph)
        pst = B.ps("pst", [P, 8], ph)
        block = ph.enter_context(nc.Block())
        loads = []

        @block.gpsimd
        def _(po):
            step = Chain(po, s_p)
            step(nc.gpsimd.iota(ii[:, :], [[1, P]], base=0, channel_multiplier=0))
            step(nc.gpsimd.iota(pi[:, :], [[0, 1]], base=0, channel_multiplier=1))
            step(nc.gpsimd.iota(si[:, :], [[P, 4]], base=0, channel_multiplier=1))
            po.wait_ge(s_z, 9)

            def one_where(t, base, pattern, mult, fill=1.0):
                step(nc.gpsimd.affine_select(out=t, in_=t, compare_op=ALU.not_equal, fill=fill, base=base,
                                             pattern=pattern, channel_multiplier=mult))

            def keep_where(t, base, pattern, mult):
                step(nc.gpsimd.affine_select(out=t, in_=t, compare_op=ALU.is_ge, fill=0.0, base=base,
                                             pattern=pattern, channel_multiplier=mult))

            one_where(K.ident[:, :], 0, [[-1, P]], 1)
            keep_where(K.tri[:, :], -1, [[1, P]], -1)
            g3 = K.gmean[:, :].rearrange("p (g k) -> p g k", g=8)
            keep_where(g3, 0, [[-16, 8], [0, 16]], 1)
            keep_where(g3, 15, [[16, 8], [0, 16]], -1)
            one_where(K.neg[:, :, :], -32, [[0, 4], [-1, BN]], 1, BIG)
            one_where(K.sel[:, :], -64, [[0, 64]], 1)
            one_where(K.hs32[:, :, :].rearrange("p a (h n) -> p (a h) n", h=4), 0, [[-1, 8], [0, 32]], 1)
            one_where(K.hs16[:, :].rearrange("p (h n) -> p h n", h=8), 0, [[-1, 8], [0, 16]], 1)

        @block.sync
        def _(sp):
            n = 0

            def load(dst, src):
                nonlocal n
                n += 16
                sp.dma_start(dst, src).then_inc(s_w, 16)

            for name in WEIGHTS:
                load(K.w[name][:, :], A[name])
            load(K.w1a[:, :], A["L1_gnn_W1"][0:D, :])
            load(K.w1b[:, :], A["L1_gnn_W1"][D:2 * D, :])
            for i, c in enumerate(("c1", "c2")):
                w = A[f"L2_gnn_{c}_w1"]
                load(K.ca[i][:, :], w[0:D, :])
                load(K.cb[i][:, :], w[D:2 * D, :])
            for h in range(4):
                load(K.w0[:, 32 * h:32 * h + 32], A["L0_gnn_W"][h, :, :])
            with nc.allow_non_contiguous_dma(reason="vectors as columns"):
                for name in COLS:
                    load(K.c[name][:, :], A[name].rearrange("(d a) -> d a", a=1))
                load(K.c["L0_gnn_bias"][:, :], A["L0_gnn_bias"].rearrange("h (f a) -> (h f) a", a=1))
                load(te[:, :], A["L2_gnn_t_emb"].rearrange("(c p) -> p c", p=P))
            for name in ROWS:
                load(K.r[name][:, :], A[name].partition_broadcast(P))
            load(tw[:, :, :], A["L2_gnn_tm_w"].rearrange("(c p) d -> p c d", p=P))
            for j, name in enumerate(("L0_gnn_att_src", "L0_gnn_att_dst")):
                load(att[:, j, :], A[name].rearrange("h f -> (h f)").partition_broadcast(P))
            sp.wait_ge(s_v, 4)
            for i, c in enumerate(("c1", "c2")):
                load(K.cs[i][66:70, :], A[f"L2_gnn_{c}_w1"][2 * D:2 * D + 4, :])
                load(K.cs[i][65:66, :], A[f"L2_gnn_{c}_b1"].rearrange("(a d) -> a d", a=1))
            load(K.ew[66:70, :], A["L2_gnn_ew"])
            load(K.ew[65:66, :], A["L2_gnn_eb"].rearrange("(a d) -> a d", a=1))
            load(K.w3[70:86, :], A["L3_gnn_edge_w"])
            sp.wait_ge(s_w, n)
            loads.append(n)

        @block.vector
        def _(ve):
            link = Chain(ve, s_v)
            for t in (K.cs[0], K.cs[1], K.ew, K.w3):
                link(nc.vector.memset(t[:, :], 0.0))
            link(nc.vector.memset(K.acc[:, :, :], 0.0))
            for t, v in ((K.ident, 0.0), (K.tri, 1.0), (K.ones, 1.0), (K.gmean, 1.0 / 16), (K.sel, 0.0), (K.hs16, 0.0)):
                nc.vector.memset(t[:, :], v).then_inc(s_z, 1)
            nc.vector.memset(K.hs32[:, :, :], 0.0).then_inc(s_z, 1)
            nc.vector.memset(K.neg[:, :, :], 0.0).then_inc(s_z, 1)
            link(nc.vector.memset(K.eqc[0:32, :], 0.0))
            nc.vector.memset(K.eqc[32:64, :], 1.0).then_inc(s_z, 1)
            ve.wait_ge(s_p, 3)
            link(nc.vector.tensor_copy(K.iota[:, :], ii[:, :]))
            link(nc.vector.tensor_copy(K.part[:, :], pi[:, :]))
            link(nc.vector.tensor_copy(K.slotid[:, :], si[:, :]))
            link(nc.vector.tensor_copy(K.eqm[0:32, :], K.part[0:32, :]))
            link(nc.vector.tensor_scalar(K.eqm[32:64, :], K.part[32:64, :], 32.0, None, ALU.subtract))
            ve.wait_ge(s_p, 11)
            link(nc.vector.tensor_copy(K.negb[:, :], K.neg[:, :, :].rearrange("p h n -> p (h n)")))
            ve.wait_ge(s_w, loads[0])
            w0 = K.w0[:, 0:D]
            for j in range(2):
                link(nc.vector.tensor_tensor(prod[:, j, :], w0, att[:, j, :], ALU.mult))
                link(nc.vector.tensor_reduce(K.w0[:, D + 4 * j:D + 4 * j + 4],
                                             prod[:, j, :].rearrange("p (h f) -> p h f", h=4),
                                             AX.X, ALU.add))
            for t, rows in [(K.ca[0], D), (K.ca[1], D), (K.cb[0], D), (K.cb[1], D),
                            (K.cs[0], TR), (K.cs[1], TR)]:
                t3 = t[:, :].rearrange("p (g k) -> p g k", g=8)
                link(nc.vector.tensor_reduce(gm[0:rows, 0, :], t3, AX.X, ALU.add))
                link(nc.vector.tensor_scalar(gm[0:rows, 1, :], gm[0:rows, 0, :], 1.0 / 16, None, ALU.mult))
                link(nc.vector.tensor_tensor(t3, t3, bc(gm[0:rows, 1, :].unsqueeze(2), [rows, 8, 16]),
                                             ALU.subtract))
            link(nc.vector.tensor_scalar(K.r["L2_gnn_qb"][:, :], K.r["L2_gnn_qb"][:, :], 0.25, None, ALU.mult))
            ve.wait_ge(s_t, 1)
            link(nc.vector.tensor_tensor(K.tvec[:, :], pst[:, 0:1], K.c["L2_gnn_tm_b"][:, :], ALU.add))

        @block.scalar
        def _(ac):
            ac.wait_ge(s_w, loads[0])
            nc.scalar.activation(tes[:, :], te[:, :], ACT.Silu).then_inc(s_a, 1)

        @block.tensor
        def _(pe):
            pe.wait_ge(s_a, 1)
            for c in range(4):
                m = nc.tensor.matmul(pst[:, 0:1], tw[:, c, :], tes[:, c:c + 1], start=c == 0, stop=c == 3)
            m.then_inc(s_t, 1)



@phase
def rank_edges(nc, B, A, K):
    s_in, s_img, s_fill = B.sem("edges_loaded"), B.sem("padding_made"), B.sem("padding_stored")
    s_v, s_cnt, s_pre, s_out = B.sem("rank_chain"), B.sem("counted"), B.sem("prefix_made"), B.sem("table_stored")
    s_msk, s_add = B.sem("ranks_masked"), B.sem("ranks_added")
    s_sc, s_cp, s_ld, s_bk = B.sem("scanned"), B.sem("placed"), B.sem("table_loaded"), B.sem("buckets_made")
    K.pos = B.sb("pos", [EP, EC], I32)
    K.dl = B.sb("dl_unsorted", [EP, EC])
    K.bucket = B.sb("slot_bucket", [1, 512], I32)
    K.over = B.sb("overflow_slots", [1, 1], I32)
    fill = K.rec[0:OVER, :].rearrange("(p c k) w -> c p (k w)", p=P, c=10)
    fill_over = K.rec[OVER:, :].rearrange("(p c k) w -> c p (k w)", p=P, c=16)
    with ExitStack() as ph:
        dst = B.sb("dst", [EP, EC], I32, ph)
        t_i = B.sb("t_i", [EP, EC], I32, ph)
        buk = B.sb("buk", [EP, EC], F32, ph)
        mask = B.sb("mask", [EP, NBUK, EC], U8, ph)
        cnt = B.sb("cnt", [EP, NBUK], F32, ph)
        off = B.sb("off", [EP, NBUK], F32, ph)
        sl_i = B.sb("sl_i", [P, NBUK], I32, ph)
        sl = B.sb("sl", [P, NBUK], F32, ph)
        ends = B.sb("ends", [P, NBUK], F32, ph)
        zero = B.sb("zero", [P, EC], F32, ph)
        cum = B.sb("cum", [EP, 2, EC], F32, ph)
        c0 = B.sb("c0", [EP, 2], F32, ph)
        posf = B.sb("posf", [EP, EC], F32, ph)
        cmp = B.sb("cmp", [P, NBUK], F32, ph)
        sb_f = B.sb("sb_f", [P, 4], F32, ph)
        sb_i = B.sb("sb_i", [P, 4], I32, ph)
        img = B.sb("img", [P, max(MSLOTS // 10, SLOTS // 16), REC], F32, ph)
        rest = B.sb("rest", [EP, EC], F32, ph)
        delta = B.sb("delta", [EP, NBUK], F32, ph)
        pre = B.ps("pre", [P, 2, P], ph)
        block = ph.enter_context(nc.Block())

        @block.sync
        def _(sp):
            sp.dma_start(dst[:, :], A["dst"].rearrange("(p j) -> p j", p=EP)).then_inc(s_in, 16)
            sp.wait_ge(s_img, 2)
            for c in range(10):
                sp.dma_start(fill[c], img[:, 0:MSLOTS // 10, :].rearrange("p k w -> p (k w)")).then_inc(s_fill, 16)
            sp.wait_ge(s_bk, 1)
            with nc.allow_non_contiguous_dma(reason="512 words"):
                sp.dma_start(K.bucket_dram.rearrange("(k p) -> p k", p=P), sb_i[:, :]).then_inc(s_out, 16)
            sp.wait_ge(s_out, 16)
            sp.dma_start(K.bucket[:, :], K.bucket_dram.rearrange("(a n) -> a n", a=1)).then_inc(s_ld, 16)
            sp.wait_ge(s_ld, 16)
            sp.wait_ge(s_fill, 160)
            with overflowed(sp, K):
                for c in range(16):
                    sp.dma_start(fill_over[c], img[:, 0:SLOTS // 16, :].rearrange("p k w -> p (k w)")).then_inc(s_fill, 16)
                sp.wait_ge(s_fill, 416)

        @block.gpsimd
        def _(po):
            nc.gpsimd.memset(img[:, :, :], 0.0).then_inc(s_img, 1)
            po.wait_ge(s_img, 1)
            nc.gpsimd.memset(img[:, :, D:D + 1], -1.0).then_inc(s_img, 1)
            nc.gpsimd.memset(posf[:, :], 0.0).then_inc(s_add, 1)
            po.wait_ge(s_add, 1)
            po.sem_inc(s_add, 1)
            with po.Fori(0, NBUK // 2) as h:
                for g in range(2):
                    po.wait_ge(s_msk, h * 2 + g + 1)
                    nc.gpsimd.tensor_tensor(posf[:, :], posf[:, :], cum[:, g, :], ALU.add).then_inc(s_add, 1)
                    po.wait_ge(s_add, h * 2 + g + 3)

        @block.vector
        def _(ve):
            link = Chain(ve, s_v)
            link(nc.vector.memset(zero[:, :], 0.0))
            ve.wait_ge(s_in, 16)
            link(nc.vector.tensor_scalar(t_i[:, :], dst[:, :], 5, None, ALU.arith_shift_right))
            link(nc.vector.tensor_copy(buk[:, :], t_i[:, :]))
            link(nc.vector.tensor_scalar(t_i[:, :], dst[:, :], BN - 1, None, ALU.bitwise_and))
            link(nc.vector.tensor_copy(K.dl[:, :], t_i[:, :]))
            link(nc.vector.tensor_tensor(mask[:, :, :], bc(buk[:, :].unsqueeze(1), [EP, NBUK, EC]),
                                         bc(K.iota[0:EP, 0:NBUK].unsqueeze(2), [EP, NBUK, EC]), ALU.is_equal))
            nc.vector.tensor_reduce(cnt[:, :], mask[:, :, :], AX.X, ALU.add).then_inc(s_cnt, 1)
            ve.wait_ge(s_pre, 1)
            link(nc.vector.tensor_copy(off[:, :], pre[0:EP, 0, 0:NBUK]))
            link(nc.vector.tensor_scalar(cmp[:, :], pre[:, 1, 0:NBUK], -float(CAP), 0.0, ALU.add, ALU.max))
            link(nc.vector.tensor_scalar(cmp[:, :], cmp[:, :], float(P - 1), None, ALU.add))
            link(nc.vector.tensor_copy(sl_i[:, :], cmp[:, :]))
            link(nc.vector.tensor_scalar(sl_i[:, :], sl_i[:, :], 7, None, ALU.arith_shift_right))
            link(nc.vector.tensor_copy(sl[:, :], sl_i[:, :]))
            link(nc.vector.tensor_tensor_scan(ends[:, :], sl[:, :], zero[:, 0:NBUK], 0.0, ALU.add, ALU.add))
            link(nc.vector.tensor_tensor(sl[:, :], ends[:, :], sl[:, :], ALU.subtract))
            link(nc.vector.tensor_scalar(sl[:, :], sl[:, :], float(P), float(OVER - CAP), ALU.mult, ALU.add))
            link(nc.vector.scalar_tensor_tensor(out=delta[:, :], in0=K.iota[0:EP, 0:NBUK], scalar=-float(CAP),
                                                in1=sl[0:EP, :], op0=ALU.mult, op1=ALU.add))
            for k in range(4):
                link(nc.vector.tensor_scalar(cmp[:, :], ends[:, :], K.slotid[:, k:k + 1], None, ALU.is_le))
                link(nc.vector.tensor_reduce(sb_f[:, k:k + 1], cmp[:, :], AX.X, ALU.add))
            link(nc.vector.tensor_scalar(sb_f[:, :], sb_f[:, :], float(NBUK - 1), None, ALU.min))
            link(nc.vector.tensor_copy(K.over[:, :], ends[0:1, NBUK - 1:NBUK]))
            nc.vector.tensor_copy(sb_i[:, :], sb_f[:, :]).then_inc(s_bk, 1)
            base = link.k
            with ve.Fori(0, NBUK // 2) as h:
                l2 = Chain(ve, s_v, h * 2 + base)
                for g in range(2):
                    m = mask[:, bass.ds(h * 2 + g, 1), :].rearrange("p a j -> p (a j)")
                    ve.wait_ge(s_add, h * 2 + g + 1)
                    l2(nc.vector.tensor_tensor_scan(cum[:, g, :], m, zero[0:EP, :], off[:, bass.ds(h * 2 + g, 1)],
                                                    ALU.add, ALU.add))
                    nc.vector.tensor_tensor(cum[:, g, :], cum[:, g, :], m, ALU.mult).then_inc(s_msk, 1)
                assert l2.k == 2
            base += NBUK
            ve.wait_ge(s_add, NBUK + 2)
            link = Chain(ve, s_v, base)
            link(nc.vector.tensor_scalar(posf[:, :], posf[:, :], -1.0, None, ALU.add))
            link(nc.vector.tensor_scalar(buk[:, :], buk[:, :], float(CAP), None, ALU.mult))
            link(nc.vector.tensor_tensor(buk[:, :], buk[:, :], posf[:, :], ALU.add))
            base += 3
            with overflowed(ve, K):
                l2 = Chain(ve, s_v, base)
                l2(nc.vector.memset(rest[:, :], 0.0))
                with ve.Fori(0, NBUK // 2) as h:
                    l3 = Chain(ve, s_v, h * 6 + (base + 1))
                    for g in range(2):
                        m = mask[:, bass.ds(h * 2 + g, 1), :].rearrange("p a j -> p (a j)")
                        l3(nc.vector.tensor_copy(c0[:, g:g + 1], delta[:, bass.ds(h * 2 + g, 1)]))
                        l3(nc.vector.tensor_scalar(cum[:, g, :], m, c0[:, g:g + 1], None, ALU.mult))
                        l3(nc.vector.tensor_tensor(rest[:, :], rest[:, :], cum[:, g, :], ALU.add))
                    assert l3.k == 6
                l2 = Chain(ve, s_v, base + 1 + 3 * NBUK)
                l2(nc.vector.tensor_scalar(posf[:, :], posf[:, :], float(CAP), None, ALU.is_ge))
                l2(nc.vector.tensor_tensor(rest[:, :], rest[:, :], posf[:, :], ALU.mult))
                l2(nc.vector.tensor_tensor(buk[:, :], buk[:, :], rest[:, :], ALU.add))
            nc.vector.tensor_copy(K.pos[:, :], buk[:, :]).then_inc(s_cp, 1)

        @block.tensor
        def _(pe):
            pe.wait_ge(s_cnt, 1)
            nc.tensor.matmul(pre[0:EP, 0, 0:NBUK], K.tri[0:EP, 0:EP], cnt[:, :], start=True, stop=True)
            nc.tensor.matmul(pre[:, 1, 0:NBUK], K.ones[0:EP, :], cnt[:, :], start=True, stop=True).then_inc(s_pre, 1)


@phase
def scatter_records(nc, B, A, K):
    W = 8
    STEPS = EC // W
    s_in, s_meta, s_free = B.sem("meta_loaded"), B.sem("meta_made"), B.sem("stage_free")
    s_attr = [B.sem("attr_staged") for _ in range(2)]
    s_stage = B.sem("meta_staged")
    s_done = [B.sem("rows_scattered") for _ in range(2)]
    s_go = B.sem("pool_go")
    with ExitStack() as ph:
        src = B.sb("src", [EP, EC], I32, ph)
        a4 = B.sb("a4", [EP, EC, 4], F32, ph)
        a16 = B.sb("a16", [EP, EC, 16], F32, ph)
        meta = B.sb("meta", [EP, EC, META], F32, ph)
        stage = B.sb("stage", [EP, 2, W, REC], F32, ph)
        idx = B.sb("idx", [EP, 2, W], I32, ph)
        block = ph.enter_context(nc.Block())
        attr = A["edge_attr_128"].rearrange("(p j) d -> p j d", p=EP)

        @block.sync
        def _(sp):
            sp.dma_start(src[:, :], A["src"].rearrange("(p j) -> p j", p=EP)).then_inc(s_in, 16)
            sp.dma_start(a4[:, :, :], A["edge_attr_4"].rearrange("(p j) k -> p j k", p=EP)).then_inc(s_in, 16)
            sp.dma_start(a16[:, :, :], A["edge_attr_16"].rearrange("(p j) k -> p j k", p=EP)).then_inc(s_in, 16)
            with sp.Fori(0, STEPS // 2) as i:
                for g in range(2):
                    sp.wait_ge(s_free, i * 2 + g + 1)
                    sp.dma_start(stage[:, g, :, 0:D], attr[:, bass.ds(i * (2 * W) + g * W, W), :]).then_inc(s_attr[g], 16)

        @block.gpsimd
        def _(po):
            with po.Fori(0, STEPS // 2) as i:
                for g in range(2):
                    po.wait_ge(s_attr[g], i * 16 + 16)
                    po.wait_ge(s_stage, i * 2 + g + 1)
                    po.sem_inc(s_go, 1)
                    for k in range(W):
                        nc.gpsimd.indirect_dma_start(
                            out=K.rec, out_offset=bass.IndirectOffsetOnAxis(ap=idx[:, g, k:k + 1], axis=0),
                            in_=stage[:, g, k, :], in_offset=None).then_inc(s_done[g], 16)

        @block.scalar
        def _(ac):
            ac.wait_ge(s_meta, 5)
            with ac.Fori(0, STEPS // 2) as i:
                for g in range(2):
                    ac.wait_ge(s_free, i * 2 + g + 1)
                    j = i * (2 * W) + g * W
                    nc.scalar.copy(stage[:, g, :, D:REC], meta[:, bass.ds(j, W), :])
                    nc.scalar.copy(idx[:, g, :], K.pos[:, bass.ds(j, W)]).then_inc(s_stage, 1)

        @block.vector
        def _(ve):
            nc.vector.memset(meta[:, :, 1:2], 1.0).then_inc(s_meta, 1)
            nc.vector.tensor_copy(meta[:, :, 0:1], K.dl[:, :].unsqueeze(2)).then_inc(s_meta, 1)
            nc.vector.memset(meta[:, :, 23:24], 0.0)
            ve.wait_ge(s_in, 48)
            nc.vector.tensor_copy(meta[:, :, 2:6], a4[:, :, :]).then_inc(s_meta, 1)
            nc.vector.tensor_copy(meta[:, :, 6:22], a16[:, :, :]).then_inc(s_meta, 1)
            nc.vector.tensor_copy(meta[:, :, 22:23].bitcast(I32), src[:, :].unsqueeze(2)).then_inc(s_meta, 1)
            ve.sem_inc(s_free, 2)
            with ve.Fori(0, STEPS // 2) as i:
                for g in range(2):
                    ve.wait_ge(s_done[g], i * (16 * W) + 16 * W)
                    ve.sem_inc(s_free, 1)


@phase
def make_operands(nc, B, A, K, reg):
    G, ng = reg.slots, reg.groups
    cols = G * P
    pieces = [(c, min(512, cols - c)) for c in range(0, cols, 512)]
    s_rec = [B.sem("meta_read") for _ in range(2)]
    s_tr, s_row, s_dlb = B.sem("transposed"), B.sem("rows_copied"), B.sem("dst_spread")
    s_free, s_t = B.sem("operand_free"), B.sem("operand_made")
    s_st = [B.sem("operand_stored") for _ in range(2)]
    s_src, s_dl, s_so, s_z = B.sem("sources_kept"), B.sem("dst_kept"), B.sem("sources_stored"), B.sem("rows_zeroed")
    with ExitStack() as ph:
        rec = B.sb("rec", [P, 2, G, META], F32, ph)
        T = B.sb("T", [TR, 2, cols], F32, ph)
        srcs = B.sb("srcs", [P, ng * G], I32, ph)
        ps_t = B.ps("ps_t", [META, -(-G // 4) * 512], ph)
        ps_d = B.ps("ps_d", [64, -(-G // 4) * 512], ph)
        block = ph.enter_context(nc.Block())

        def guard(eng):
            return overflowed(eng, K) if reg.over else ExitStack()

        @block.sync
        def _(sp):
            with guard(sp):
                with sp.Fori(0, ng // 2) as i:
                    for g in range(2):
                        sp.wait_ge(s_free, i * 2 + g + 1)
                        sp.dma_start(rec[:, g, :, :], reg.rec[:, bass.ds(i * (2 * G) + g * G, G), D:REC]).then_inc(s_rec[g], 16)
                sp.wait_ge(s_src, ng)
                sp.dma_start(reg.src, srcs[:, :]).then_inc(s_so, 16)
                sp.wait_ge(s_so, 16)

        @block.tensor
        def _(pe):
            with guard(pe):
                pe.wait_ge(s_z, 1)
                with pe.Fori(0, ng // 2) as i:
                    for g in range(2):
                        n = i * 2 + g
                        pe.wait_ge(s_rec[g], i * 16 + 16)
                        for k in range(G):
                            m = nc.tensor.transpose(ps_t[:, k * P:(k + 1) * P], rec[:, g, k, :], K.ident[:, :])
                        m.then_inc(s_tr, 1)
                        pe.wait_ge(s_row, n + 1)
                        for c, w in pieces:
                            m = nc.tensor.matmul(ps_d[:, c:c + w], K.sel[64:64 + META, :],
                                                 T[64:64 + META, g, c:c + w], start=True, stop=True)
                        m.then_inc(s_dlb, 1)

        @block.scalar
        def _(ac):
            with guard(ac):
                with ac.Fori(0, ng // 2) as i:
                    for g in range(2):
                        n = i * 2 + g
                        ac.wait_ge(s_free, n + 1)
                        ac.wait_ge(s_tr, n + 1)
                        nc.scalar.copy(T[64:64 + META, g, :], ps_t[:, 0:cols]).then_inc(s_row, 1)
                        ac.wait_ge(s_t, n + 1)
                        ac.dma_start(reg.t[bass.ds(n, 1), :, :].rearrange("a r c -> (a r) c"),
                                     T[:, g, :]).then_inc(s_st[g], 16)

        @block.vector
        def _(ve):
            with guard(ve):
                nc.vector.memset(T[:, :, :], 0.0).then_inc(s_z, 1)
                ve.wait_ge(s_z, 1)
                ve.sem_inc(s_free, 2)
                with ve.Fori(0, ng // 2) as i:
                    for g in range(2):
                        n = i * 2 + g
                        ve.wait_ge(s_dlb, n + 1)
                        nc.vector.tensor_copy(srcs[:, bass.ds(n * G, G)],
                                              rec[:, g, :, 22:23].bitcast(I32).rearrange("p s a -> p (s a)")).then_inc(s_src, 1)
                        nc.vector.tensor_copy(reg.dls[:, bass.ds(n * G, G)],
                                              rec[:, g, :, 0:1].rearrange("p s a -> p (s a)")).then_inc(s_dl, 1)
                        nc.vector.tensor_scalar(T[0:64, g, :], ps_d[:, 0:cols], K.eqm[:, :], K.eqc[:, :],
                                                ALU.is_equal, ALU.subtract).then_inc(s_t, 1)
                        ve.wait_ge(s_dl, n + 1)
                        ve.wait_ge(s_st[g], i * 16 + 16)
                        ve.sem_inc(s_free, 1)



@phase
def load_x(nc, B, A, K):
    s_in, s_z, s_tr, s_cp = B.sem("x_loaded"), B.sem("x_padded"), B.sem("x_transposed"), B.sem("x_copied")
    with ExitStack() as ph:
        xn = B.sb("xn", [P, TILES, D], F32, ph)
        ps = [B.ps("ps", [P, P], ph) for _ in range(2)]
        block = ph.enter_context(nc.Block())
        full, rest = N // P, N % P

        @block.sync
        def _(sp):
            sp.dma_start(xn[:, 0:full, :], A["x"][0:full * P, :].rearrange("(t p) d -> p t d", p=P)).then_inc(s_in, 16)
            sp.wait_ge(s_z, 1)
            sp.dma_start(xn[0:rest, full, :], A["x"][full * P:N, :]).then_inc(s_in, 16)

        @block.tensor
        def _(pe):
            pe.wait_ge(s_in, 32)
            for t in range(TILES):
                if t >= 2:
                    pe.wait_ge(s_cp, t - 1)
                nc.tensor.transpose(ps[t % 2][:, :], xn[:, t, :], K.ident[:, :]).then_inc(s_tr, 1)

        @block.vector
        def _(ve):
            nc.vector.memset(xn[:, full, :], 0.0).then_inc(s_z, 1)
            for t in range(TILES):
                ve.wait_ge(s_tr, t + 1)
                nc.vector.tensor_copy(K.X[:, t * P:(t + 1) * P], ps[t % 2][:, :]).then_inc(s_cp, 1)


@phase
def norm_nodes(nc, B, A, K):
    s_tr, s_xc, s_v, s_sd = B.sem("x_transposed"), B.sem("x_copied"), B.sem("stat_chain"), B.sem("deviations")
    s_sq, s_h, s_hb, s_hc = B.sem("roots"), B.sem("normed"), B.sem("h_transposed"), B.sem("h_copied")
    with ExitStack() as ph:
        xn = B.sb("xn", [P, TILES, D], F32, ph)
        st = B.sb("st", [P, TILES, 6], F32, ph)
        mv = B.sb("mv", [P, TILES, 2], F32, ph)
        sd = B.sb("sd", [P, TILES], F32, ph)
        nb = B.sb("nb", [P, TILES], F32, ph)
        psx = [B.ps("psx", [P, P], ph) for _ in range(2)]
        psh = [B.ps("psh", [P, P], ph) for _ in range(2)]
        block = ph.enter_context(nc.Block())

        @block.tensor
        def _(pe):
            for t in range(TILES):
                if t >= 2:
                    pe.wait_ge(s_xc, t - 1)
                nc.tensor.transpose(psx[t % 2][:, :], K.X[:, t * P:(t + 1) * P], K.ident[:, :]).then_inc(s_tr, 1)
            for t in range(TILES):
                pe.wait_ge(s_h, t + 1)
                if t >= 2:
                    pe.wait_ge(s_hc, t - 1)
                nc.tensor.transpose(psh[t % 2][:, :], xn[:, t, :], K.ident[:, :]).then_inc(s_hb, 1)

        @block.vector
        def _(ve):
            link = Chain(ve, s_v)
            for t in range(TILES):
                ve.wait_ge(s_tr, t + 1)
                nc.vector.tensor_copy(xn[:, t, :], psx[t % 2][:, :]).then_inc(s_xc, 1)
                ve.wait_ge(s_xc, t + 1)
                link(nc.vector.bn_stats(st[:, t, :], xn[:, t, :]))
                link(nc.vector.bn_aggr(mv[:, t, :], st[:, t, :]))
            nc.vector.tensor_scalar(sd[:, :], mv[:, :, 1], EPS, None, ALU.add).then_inc(s_sd, 1)
            ve.wait_ge(s_sq, 1)
            link(nc.vector.reciprocal(sd[:, :], sd[:, :]))
            nc.vector.scalar_tensor_tensor(out=nb[:, :], in0=mv[:, :, 0], scalar=-1.0, in1=sd[:, :],
                                           op0=ALU.mult, op1=ALU.mult).then_inc(s_sd, 1)
            for t in range(TILES):
                ve.wait_ge(s_hb, t + 1)
                nc.vector.tensor_copy(K.H[:, t * P:(t + 1) * P], psh[t % 2][:, :]).then_inc(s_hc, 1)

        @block.scalar
        def _(ac):
            ac.wait_ge(s_sd, 1)
            nc.scalar.activation(sd[:, :], sd[:, :], ACT.Sqrt).then_inc(s_sq, 1)
            ac.wait_ge(s_sd, 2)
            for t in range(TILES):
                nc.scalar.activation(xn[:, t, :], xn[:, t, :], ACT.Relu, bias=nb[:, t:t + 1],
                                     scale=sd[:, t:t + 1]).then_inc(s_h, 1)


@phase
def project_nodes(nc, B, K, pairs, width, table, row=None, scale=1.0):
    s_mm, s_cp, s_st = B.sem("projected"), B.sem("row_copied"), B.sem("table_stored")
    with ExitStack() as ph:
        out = B.sb("out", [P, TILES, width], F32, ph)
        ps = [B.ps("ps", [P, 512], ph) for _ in range(2)]
        block = ph.enter_context(nc.Block())

        @block.tensor
        def _(pe):
            for t in range(TILES):
                if t >= 2:
                    pe.wait_ge(s_cp, t - 1)
                for j, (x, ws) in enumerate(pairs):
                    at = 0
                    for w in ws:
                        n = w.shape[1]
                        m = nc.tensor.matmul(ps[t % 2][:, at:at + n], x[:, t * P:(t + 1) * P], w,
                                             start=j == 0, stop=j == len(pairs) - 1, skip_group_check=True)
                        at += n
                m.then_inc(s_mm, 1)

        @block.vector
        def _(ve):
            for t in range(TILES):
                ve.wait_ge(s_mm, t + 1)
                if row is None:
                    nc.vector.tensor_copy(out[:, t, :], ps[t % 2][:, 0:width]).then_inc(s_cp, 1)
                else:
                    for j, r in enumerate(row):
                        m = nc.vector.scalar_tensor_tensor(
                            out=out[:, t, j * D:(j + 1) * D], in0=ps[t % 2][:, j * D:(j + 1) * D], scalar=scale,
                            in1=r, op0=ALU.mult, op1=ALU.add)
                    m.then_inc(s_cp, 1)

        @block.sync
        def _(sp):
            sp.wait_ge(s_cp, TILES)
            sp.dma_start(table.rearrange("(t p) w -> p t w", p=P), out[:, :, :]).then_inc(s_st, 16)
            sp.wait_ge(s_st, 16)


@phase
def feature_product(nc, B, K, pairs, consume, steps, act=None):
    s_mm, s_v = B.sem("chunk_product"), B.sem("chunk_chain")
    with ExitStack() as ph:
        ps = [B.ps("ps", [P, 512], ph) for _ in range(2)]
        block = ph.enter_context(nc.Block())

        @block.tensor
        def _(pe):
            for c in range(NCH):
                if c >= 2:
                    pe.wait_ge(s_v, steps * (c - 1))
                for j, (w, x) in enumerate(pairs):
                    m = nc.tensor.matmul(ps[c % 2][:, 0:CH], w, x[:, c * CH:(c + 1) * CH],
                                         start=j == 0, stop=j == len(pairs) - 1)
                m.then_inc(s_mm, 1)

        @block.vector
        def _(ve):
            link = Chain(ve, s_v)
            for c in range(NCH):
                ve.wait_ge(s_mm, c + 1)
                consume(slice(c * CH, (c + 1) * CH), ps[c % 2][:, 0:CH], link)
                assert link.k == steps * (c + 1)


@phase
def group_norm(nc, B, K, X, gamma, beta, func, Y):
    s_mm, s_c, s_sq = B.sem("group_mean"), B.sem("centred"), B.sem("squared")
    s_var, s_rt, s_v, s_n, s_y = B.sem("group_var"), B.sem("root"), B.sem("norm_chain"), B.sem("normed"), B.sem("written")
    with ExitStack() as ph:
        sq = B.sb("sq", [P, 2, CH], F32, ph)
        rs = B.sb("rs", [P, 2, CH], F32, ph)
        ps = [B.ps("ps", [P, 512], ph) for _ in range(2)]
        pv = [B.ps("pv", [P, 512], ph) for _ in range(2)]
        block = ph.enter_context(nc.Block())

        @block.tensor
        def _(pe):
            for c in range(NCH):
                sl = slice(c * CH, (c + 1) * CH)
                if c >= 2:
                    pe.wait_ge(s_c, c - 1)
                nc.tensor.matmul(ps[c % 2][:, 0:CH], K.gmean[:, :], X[:, sl], start=True, stop=True).then_inc(s_mm, 1)
                pe.wait_ge(s_sq, c + 1)
                nc.tensor.matmul(pv[c % 2][:, 0:CH], K.gmean[:, :], sq[:, c % 2, :], start=True, stop=True).then_inc(s_var, 1)

        @block.scalar
        def _(ac):
            for c in range(NCH):
                sl = slice(c * CH, (c + 1) * CH)
                ac.wait_ge(s_c, c + 1)
                nc.scalar.activation(sq[:, c % 2, :], X[:, sl], ACT.Square).then_inc(s_sq, 1)
                ac.wait_ge(s_v, 3 * c + 1)
                nc.scalar.activation(rs[:, c % 2, :], rs[:, c % 2, :], ACT.Sqrt).then_inc(s_rt, 1)
            for c in range(NCH):
                sl = slice(c * CH, (c + 1) * CH)
                ac.wait_ge(s_v, 3 * c + 3)
                nc.scalar.activation(Y[:, sl], X[:, sl], func, bias=beta[:, :], scale=gamma[:, :]).then_inc(s_y, 1)

        @block.vector
        def _(ve):
            link = Chain(ve, s_v)
            for c in range(NCH):
                sl = slice(c * CH, (c + 1) * CH)
                ve.wait_ge(s_mm, c + 1)
                nc.vector.tensor_tensor(X[:, sl], X[:, sl], ps[c % 2][:, 0:CH], ALU.subtract).then_inc(s_c, 1)
                ve.wait_ge(s_var, c + 1)
                link(nc.vector.tensor_scalar(rs[:, c % 2, :], pv[c % 2][:, 0:CH], EPS, None, ALU.add))
                ve.wait_ge(s_rt, c + 1)
                link(nc.vector.reciprocal(rs[:, c % 2, :], rs[:, c % 2, :]))
                link(nc.vector.tensor_tensor(X[:, sl], X[:, sl], rs[:, c % 2, :], ALU.mult))


@phase
def vector_phase(nc, B, body):
    s_v = B.sem("vector_chain")
    with ExitStack() as ph:
        block = ph.enter_context(nc.Block())

        @block.vector
        def _(ve):
            body(Chain(ve, s_v))


@phase
def load_table(nc, B, table, tab):
    s = B.sem("table_loaded")
    with ExitStack() as ph:
        block = ph.enter_context(nc.Block())

        @block.sync
        def _(sp):
            sp.dma_start(tab[:, :, :], table.rearrange("(b p) d -> p b d", p=BN)).then_inc(s, 16)
            sp.wait_ge(s, 16)



@phase
def overflow_pass(nc, B, K, kind, gather=None, gw=0, linear=None, lw=0, store=None, tab=None, tw=0,
              static=None, gcol=None, btcol=None, MX=None, heads=0, LG=None):
    uses_T = kind not in ("sum", "attr")
    is_max = kind in ("gatmax", "logits")
    NS = 2 if kind in ("gat", "attr", "attn") else 1
    HG = heads // 4 if heads else 0
    W = gw or lw
    s_idx = [B.sem("indices_read") for _ in range(RING)]
    s_t = [B.sem("operand_read") for _ in range(RING)]
    s_rows = [B.sem("rows_arrived") for _ in range(RING)]
    s_kept = [B.sem("rows_kept") for _ in range(RING)]
    s_lg = [B.sem("logits_moved") for _ in range(RING)]
    s_free, s_go = B.sem("group_done"), B.sem("pool_go")
    s_exp, s_v, s_val = B.sem("expanded"), B.sem("vector_chain"), B.sem("value_ready")
    s_act, s_sum, s_lk, s_z = B.sem("activated"), B.sem("summed"), B.sem("logits_kept"), B.sem("acc_zeroed")
    row_incs = 64 if gw else 16
    with ExitStack() as ph:
        rows = B.sb("rows", [P, RING, GS, W], F32, ph)
        idx = B.sb("idx", [P, RING, GS], I32, ph) if gw else None
        T = B.sb("T", [TR, RING, GS * P], F32, ph) if uses_T else None
        lg = B.sb("lg", [P, RING, GS, 8], F32, ph) if kind == "attn" else None
        oh = B.sb("oh", [P, GS, BN], F32, ph)
        m = B.sb("m", [P, GS, D], F32, ph)
        sq = B.sb("sq", [P, GS, D], F32, ph)
        w = B.sb("w", [P, GS, 8], F32, ph)
        z = B.sb("z", [P, GS, 8], F32, ph)
        y = B.sb("y", [P, 4, GS * 8], F32, ph)
        mx = B.sb("mx", [P, 2, GS], F32, ph)
        pe1 = B.ps("expanded", [P, GS, D], ph)
        pl = B.ps("edge_logits", [P, GS, 8], ph)
        pt = B.ps("logits_T", [heads, GS * P], ph) if is_max else None
        wT = B.sb("wT", [heads, GS * P], F32, ph) if is_max else None
        s_tt, s_tc = B.sem("logits_transposed"), B.sem("logits_copied")
        pm = [B.ps("spread", [P, GS, P], ph) for _ in range(2)] if is_max else None
        psum = B.ps("sums", [P, GS, 2, BN], ph)
        block = ph.enter_context(nc.Block())
        hv = {"gat": (4, 32), "attn": (8, 16)}.get(kind)

        @block.sync
        def _(sp):
            with overflowed(sp, K):
                with sp.Fori(0, TRIPS) as i:
                    for g in range(RING):
                        n = i * RING + g
                        sp.wait_ge(s_free, n + 1)
                        if gw:
                            sp.dma_start(idx[:, g, :], K.reg_o.src[:, bass.ds(n * GS, GS)]).then_inc(s_idx[g], 16)
                        else:
                            sp.dma_start(rows[:, g, :, :], linear[:, bass.ds(n * GS, GS), 0:W]).then_inc(s_rows[g], 16)
                        if kind == "attn":
                            sp.dma_start(lg[:, g, :, :], LG[:, bass.ds(n * GS, GS), :]).then_inc(s_lg[g], 16)
                        if uses_T:
                            sp.dma_start(T[:, g, :], K.reg_o.t[bass.ds(n, 1), :, :].rearrange("a r c -> (a r) c")).then_inc(s_t[g], 16)

        if gw:
            @block.gpsimd
            def _(po):
                with overflowed(po, K):
                    with po.Fori(0, TRIPS) as i:
                        for g in range(RING):
                            po.wait_ge(s_idx[g], i * 16 + 16)
                            po.sem_inc(s_go, 1)
                            for k in range(GS):
                                nc.gpsimd.indirect_dma_start(
                                    out=rows[:, g, k, :], out_offset=None, in_=gather,
                                    in_offset=bass.IndirectOffsetOnAxis(ap=idx[:, g, k:k + 1], axis=0)).then_inc(s_rows[g], 16)

        @block.tensor
        def _(pe):
            with overflowed(pe, K):
                with pe.Fori(0, TRIPS) as i:
                    for g in range(RING):
                        n = i * RING + g

                        def bucket(k):
                            return pe.value_load(K.bucket[0:1, bass.ds(n * GS + k, 1)], min_val=0, max_val=NBUK - 1)

                        if uses_T:
                            pe.wait_ge(s_t[g], i * 16 + 16)
                        if kind in ("gat", "attn", "conv", "logits"):
                            wd = tw
                            for k in range(GS):
                                v = bucket(k)
                                o = pe1[:, k, 0:wd] if wd == D else pl[:, k, 0:wd]
                                mm = nc.tensor.matmul(o, T[0:BN, g, k * P:(k + 1) * P], tab[:, bass.ds(v * wd, wd)],
                                                      start=True, stop=kind != "conv", skip_group_check=True)
                                if kind == "conv":
                                    mm = nc.tensor.matmul(o, T[:, g, k * P:(k + 1) * P], static[:, :], start=False,
                                                          stop=True, skip_group_check=True)
                                if kind == "logits":
                                    mm = nc.tensor.matmul(pl[:, k, :], T[:, g, k * P:(k + 1) * P], static[:, :],
                                                          start=True, stop=True, skip_group_check=True)
                            mm.then_inc(s_exp, 1)
                        if kind == "prod":
                            for k in range(GS):
                                mm = nc.tensor.matmul(pe1[:, k, :], T[:, g, k * P:(k + 1) * P], static[:, :],
                                                      start=True, stop=True, skip_group_check=True)
                            mm.then_inc(s_exp, 1)
                        if is_max:
                            if kind == "gatmax":
                                pe.wait_ge(s_rows[g], i * row_incs + row_incs)
                                pe.wait_ge(s_free, n + RING)
                            else:
                                pe.wait_ge(s_val, n + 1)
                            for k in range(GS):
                                a = rows[:, g, k, D:D + 4] if kind == "gatmax" else w[:, k, :]
                                mm = nc.tensor.transpose(pt[:, k * P:(k + 1) * P], a, K.ident[:, :])
                            mm.then_inc(s_tt, 1)
                            pe.wait_ge(s_tc, n + 1)
                            for hg in range(HG):
                                nc.tensor.matmul(pm[hg][:, :, :].rearrange("p k e -> p (k e)"),
                                                 K.neg[:, :, :].rearrange("p h n -> p (h n)"), T[:, g, :],
                                                 start=True, stop=False)
                                mm = nc.tensor.matmul(pm[hg][:, :, :].rearrange("p k e -> p (k e)"),
                                                      K.hs32[0:heads, hg, :], wT[:, :], start=False, stop=True)
                            mm.then_inc(s_sum, 1)
                        else:
                            if kind in ("sum", "attr"):
                                pe.wait_ge(s_rows[g], i * row_incs + row_incs)
                            pe.wait_ge(s_val, n + 1)
                            for k in range(GS):
                                src = rows[:, g, k, 0:D] if kind in ("sum", "attr") else m[:, k, :]
                                mm = nc.tensor.matmul(psum[:, k, 0, :], src, oh[:, k, :], start=True, stop=True,
                                                      skip_group_check=True)
                                if NS == 2:
                                    second = K.ones[:, :] if kind == "attr" else w[:, k, 0:hv[0]]
                                    mm = nc.tensor.matmul(psum[0:second.shape[1], k, 1, :], second, oh[:, k, :], start=True, stop=True,
                                                          skip_group_check=True)
                            mm.then_inc(s_sum, 1)

        @block.scalar
        def _(ac):
            with overflowed(ac, K):
                with ac.Fori(0, TRIPS) as i:
                    for g in range(RING):
                        n = i * RING + g
                        if store is not None:
                            ac.wait_ge(s_rows[g], i * row_incs + row_incs)
                            s0, s1, dram = store
                            ac.dma_start(dram[:, bass.ds(n * GS, GS), :], rows[:, g, :, s0:s1]).then_inc(s_kept[g], 16)
                        if kind in ("gat", "attn"):
                            ac.wait_ge(s_lk, n + 1)
                            nc.scalar.activation(w[:, :, 0:hv[0]], z[:, :, 0:hv[0]], ACT.Exp).then_inc(s_act, 1)
                        if kind == "conv":
                            ac.wait_ge(s_lk, 2 * n + 1)
                            nc.scalar.activation(sq[:, :, :], m[:, :, :], ACT.Square).then_inc(s_act, 1)
                            ac.wait_ge(s_lk, 2 * n + 2)
                            nc.scalar.activation(m[:, :, :], sq[:, :, :], ACT.Silu).then_inc(s_act, 1)
                        if is_max:
                            ac.wait_ge(s_tt, n + 1)
                            nc.scalar.copy(wT[:, :], pt[:, :]).then_inc(s_tc, 1)
                        if kind == "logits":
                            ac.wait_ge(s_val, n + 1)
                            ac.dma_start(LG[:, bass.ds(n * GS, GS), :], w[:, :, :]).then_inc(s_lg[g], 16)

        per = {"gatmax": 5, "gat": 7, "sum": 4, "attr": 4, "conv": 19, "logits": 7, "attn": 4, "prod": 4}[kind]

        @block.vector
        def _(ve):
            with overflowed(ve, K):
                nc.vector.memset(psum[:, :, :, :], 0.0).then_inc(s_z, 1)
                ve.wait_ge(s_z, 1)
                ve.sem_inc(s_free, RING)
                with ve.Fori(0, TRIPS) as i:
                    link = Chain(ve, s_v, i * (per * RING))
                    for g in range(RING):
                        n = i * RING + g

                        def bucket(k):
                            return ve.value_load(K.bucket[0:1, bass.ds(n * GS + k, 1)], min_val=0, max_val=NBUK - 1)

                        if not is_max:
                            o = nc.vector.tensor_tensor(oh[:, :, :], bc(K.iota[:, 0:BN].unsqueeze(1), [P, GS, BN]),
                                                        bc(K.reg_o.dls[:, bass.ds(n * GS, GS)].unsqueeze(2), [P, GS, BN]),
                                                        ALU.is_equal)
                            if kind in ("sum", "attr"):
                                o.then_inc(s_val, 1)
                        if kind in ("gat", "attn", "conv", "prod", "logits"):
                            ve.wait_ge(s_exp, n + 1)
                        if kind not in ("sum", "attr", "gatmax"):
                            ve.wait_ge(s_rows[g], i * row_incs + row_incs)
                        r = rows[:, g, :, 0:D]
                        if kind == "gat":
                            link(nc.vector.tensor_tensor(w[:, :, 4:8], rows[:, g, :, D:D + 4], pl[:, :, 0:4], ALU.add))
                            link(nc.vector.scalar_tensor_tensor(out=z[:, :, 4:8], in0=w[:, :, 4:8], scalar=0.2,
                                                                in1=w[:, :, 4:8], op0=ALU.mult, op1=ALU.max))
                            link(nc.vector.tensor_tensor(z[:, :, 0:4], z[:, :, 4:8], pl[:, :, 4:8], ALU.subtract))
                            ve.sem_inc(s_lk, 1)
                        if kind == "attn":
                            ve.wait_ge(s_lg[g], i * 16 + 16)
                            nc.vector.tensor_tensor(z[:, :, :], lg[:, g, :, :],
                                                    pl[:, :, :], ALU.subtract).then_inc(s_lk, 1)
                        if kind in ("gat", "attn"):
                            ve.wait_ge(s_act, n + 1)
                            h, f = hv
                            for k in range(GS):
                                mm = nc.vector.tensor_tensor(m[:, k, :].rearrange("p (h f) -> p h f", h=h),
                                                             rows[:, g, k, 0:D].rearrange("p (h f) -> p h f", h=h),
                                                             bc(w[:, k, 0:h].unsqueeze(2), [P, h, f]), ALU.mult)
                            mm.then_inc(s_val, 1)
                        if kind == "prod":
                            nc.vector.tensor_tensor(m[:, :, :], r, pe1[:, :, :], ALU.mult).then_inc(s_val, 1)
                        if kind == "logits":
                            link(nc.vector.tensor_tensor(m[:, :, :], r, pe1[:, :, :], ALU.mult))
                            link(nc.vector.tensor_reduce(z[:, :, :].rearrange("p k h -> p (k h)"),
                                                         m[:, :, :].rearrange("p k (h f) -> p (k h) f", h=8), AX.X, ALU.add))
                            nc.vector.tensor_tensor(w[:, :, :], z[:, :, :], pl[:, :, :], ALU.add).then_inc(s_val, 1)
                        if kind == "conv":
                            nc.vector.tensor_tensor(m[:, :, :], r, pe1[:, :, :], ALU.add).then_inc(s_lk, 1)
                            ve.wait_ge(s_act, 2 * n + 1)
                            link(nc.vector.tensor_reduce(y[:, 0, :], sq[:, :, :].rearrange("p k (h f) -> p (k h) f", h=8),
                                                         AX.X, ALU.add))
                            link(nc.vector.tensor_scalar(y[:, 0, :], y[:, 0, :], 1.0 / 16, EPS, ALU.mult, ALU.add))
                            link(nc.vector.tensor_scalar(y[:, 1, :].bitcast(I32), y[:, 0, :].bitcast(I32), -0.5,
                                                         float(0x5f3759df), ALU.mult, ALU.add))
                            for _ in range(3):
                                link(nc.vector.scalar_tensor_tensor(out=y[:, 2, :], in0=y[:, 1, :], scalar=-0.5,
                                                                    in1=y[:, 0, :], op0=ALU.mult, op1=ALU.mult))
                                link(nc.vector.tensor_tensor(y[:, 2, :], y[:, 2, :], y[:, 1, :], ALU.mult))
                                link(nc.vector.scalar_tensor_tensor(out=y[:, 1, :], in0=y[:, 2, :], scalar=1.5,
                                                                    in1=y[:, 1, :], op0=ALU.add, op1=ALU.mult))
                            link(nc.vector.tensor_tensor(m[:, :, :].rearrange("p k (h f) -> p (k h) f", h=8),
                                                         m[:, :, :].rearrange("p k (h f) -> p (k h) f", h=8),
                                                         bc(y[:, 1, :].unsqueeze(2), [P, GS * 8, 16]), ALU.mult))
                            link(nc.vector.tensor_tensor(m[:, :, :], m[:, :, :], bc(gcol.unsqueeze(1), [P, GS, D]), ALU.mult))
                            link(nc.vector.tensor_tensor(sq[:, :, :], m[:, :, :], bc(btcol.unsqueeze(1), [P, GS, D]), ALU.add))
                            ve.sem_inc(s_lk, 1)
                            ve.wait_ge(s_act, 2 * n + 2)
                            ve.sem_inc(s_val, 1)
                        ve.wait_ge(s_sum, n + 1)
                        if is_max:
                            for hg in range(HG):
                                mm = nc.vector.tensor_reduce(mx[:, hg, :], pm[hg][:, :, :], AX.X, ALU.max)
                            link(mm)
                            for k in range(GS):
                                v = bucket(k)
                                dst = MX[:, :, bass.ds(v, 1)].rearrange("p g a -> p (g a)")
                                link(nc.vector.tensor_tensor(dst, dst, mx[:, 0:HG, k], ALU.max))
                        else:
                            for k in range(GS):
                                v = bucket(k)
                                dst = K.acc[:, 0:NS, bass.ds(v * BN, BN)]
                                link(nc.vector.tensor_tensor(dst, dst, psum[:, k, 0:NS, :], ALU.add))
                        if kind == "logits":
                            ve.wait_ge(s_lg[g], i * 16 + 16)
                        if store is not None:
                            ve.wait_ge(s_kept[g], i * 16 + 16)
                        ve.sem_inc(s_free, 1)
                    assert link.k == per * RING, (kind, link.k)


@phase
def bucket_pass(nc, B, K, kind, gather=None, gw=0, linear=None, lw=0, store=None, tab=None, tw=0,
                static=None, gcol=None, btcol=None, MX=None, heads=0, LG=None):
    uses_T = kind not in ("sum", "attr")
    is_max = kind in ("gatmax", "logits")
    soft = kind in ("gat", "attn")
    wide = kind in ("conv", "prod", "logits")
    NS = 2 if kind in ("gat", "attr", "attn") else 1
    HG = heads // 4 if heads else 0
    W = gw or lw
    h = {"gat": 4, "attn": 8}.get(kind, 0)
    rowinc = 16 * MG if gw else 16
    s_idx = [B.sem("indices_read") for _ in range(2)]
    s_t = [B.sem("operand_read") for _ in range(2)]
    s_rows = [B.sem("rows_arrived") for _ in range(2)]
    s_kept = [B.sem("rows_kept") for _ in range(2)]
    s_rfree, s_tfree, s_go = B.sem("rows_free"), B.sem("operand_free"), B.sem("pool_go")
    s_exp, s_efree = B.sem("expanded"), B.sem("expanded_free")
    s_va, s_vb = B.sem("vector_chain_a"), B.sem("vector_chain_b")
    s_sq, s_pre, s_val = B.sem("squared"), B.sem("before_activation"), B.sem("values_ready")
    s_w, s_oh, s_sum, s_done = B.sem("weights_made"), B.sem("onehot_made"), B.sem("summed"), B.sem("sums_kept")
    s_tt, s_tc, s_nt = B.sem("logits_transposed"), B.sem("logits_copied"), B.sem("complement_copied")
    s_pm, s_mr, s_lk = B.sem("logits_spread"), B.sem("maxima_taken"), B.sem("logits_kept")
    with ExitStack() as ph:
        rows = B.sb("rows", [P, 2, MG, W], F32, ph)
        idx = B.sb("idx", [P, 2, MG], I32, ph) if gw else None
        T = B.sb("T", [TR, 2, MW], F32, ph) if uses_T else None
        oh = B.sb("oh", [P, 2, MG, BN], F32, ph) if not is_max else None
        nm = 1 if kind == "logits" else 2
        m = B.sb("m", [P, nm, MG, D], F32, ph) if kind in ("gat", "attn", "conv", "prod", "logits") else None
        sq = B.sb("sq", [P, 2, MG, D], F32, ph) if kind == "conv" else None
        y = B.sb("y", [P, 3, MG * 8], F32, ph) if kind == "conv" else None
        w = B.sb("w", [P, 2, MG, 8], F32, ph) if soft or is_max else None
        z = B.sb("z", [P, 2, MG, 8], F32, ph) if soft or kind == "logits" else None
        u = B.sb("u", [P, 2, MG, 4], F32, ph) if kind == "gat" else None
        wT = B.sb("wT", [heads, 2, CAP], F32, ph) if is_max else None
        NT = B.sb("NT", [TR, 2, MW], BF16, ph) if is_max else None
        big = ([B.ps("expanded", [P, 12, D], ph) for _ in range(1 if kind == "logits" else 2)] if wide else None)
        pl = ([B.ps("edge_logits", [P, MG, 8], ph) for _ in range(1 if kind == "logits" else 2)]
              if soft or kind == "logits" else None)
        pt = B.ps("logits_T", [heads, 1024], ph) if is_max else None
        pm = B.ps("spread", [P, 1024], ph) if is_max else None
        psum = [B.ps("sums", [P, NS, GB, BN], ph) for _ in range(2)] if not is_max else None
        block = ph.enter_context(nc.Block())
        ne = 1 if kind == "logits" else 2

        def nothing(n, g, r):
            pass

        @block.sync
        def _(sp):
            def load(n, g, r):
                sp.wait_ge(s_rfree, n + 1)
                if gw:
                    sp.dma_start(idx[:, g, :], K.reg_m.src[:, span(n, MG)]).then_inc(s_idx[g], 16)
                else:
                    sp.dma_start(rows[:, g, :, :], linear[:, span(n, MG), 0:W]).then_inc(s_rows[g], 16)
                if uses_T:
                    sp.wait_ge(s_tfree, n + 1)
                    sp.dma_start(T[:, g, :], K.reg_m.t[span(n, 1), :, :].rearrange("a r c -> (a r) c")).then_inc(s_t[g], 16)

            pipelined(sp, load, nothing)

        if gw:
            @block.gpsimd
            def _(po):
                def fetch(n, g, r):
                    po.wait_ge(s_idx[g], r * 16 + 16)
                    po.sem_inc(s_go, 1)
                    for k in range(MG):
                        nc.gpsimd.indirect_dma_start(
                            out=rows[:, g, k, :], out_offset=None, in_=gather,
                            in_offset=bass.IndirectOffsetOnAxis(ap=idx[:, g, k:k + 1], axis=0)).then_inc(s_rows[g], 16)

                pipelined(po, fetch, nothing)

        @block.tensor
        def _(pe):
            def expand(n, g, r):
                pe.wait_ge(s_t[g], r * 16 + 16)
                pe.wait_ge(s_efree, n + 1)
                if kind == "conv":
                    pe.wait_ge(s_rows[g], r * rowinc + rowinc)
                    for c in range(0, MG, 4):
                        c1 = min(MG, c + 4)
                        nc.tensor.matmul(big[g][:, c:c1, :].rearrange("p k d -> p (k d)"), K.ident[:, :],
                                         rows[:, g, c:c1, :].rearrange("p k d -> p (k d)"), start=True, stop=True,
                                         skip_group_check=True)
                for k in range(MG):
                    t = T[:, g, k * P:(k + 1) * P]
                    o = big[g % ne][:, k, :] if wide else pl[g][:, k, :]
                    if tab is not None:
                        b = n * GB + k // CAPS
                        mm = nc.tensor.matmul(o, t[0:BN, :], tab[:, span(b, tw)], start=kind != "conv",
                                              stop=True, skip_group_check=True)
                    if kind == "logits":
                        mm = nc.tensor.matmul(pl[0][:, k, :], t, static[:, :], start=True, stop=True,
                                              skip_group_check=True)
                    elif static is not None:
                        mm = nc.tensor.matmul(o, t, static[:, :], start=kind != "conv", stop=True,
                                              skip_group_check=True)
                mm.then_inc(s_exp, 1)

            def sums(n, g, r):
                if kind in ("sum", "attr"):
                    pe.wait_ge(s_rows[g], r * rowinc + rowinc)
                    pe.wait_ge(s_oh, n + 1)
                else:
                    pe.wait_ge(s_val, n + 1)
                for b in range(GB):
                    for s in range(NS):
                        for j in range(CAPS):
                            k = b * CAPS + j
                            if s == 0:
                                a = rows[:, g, k, 0:D] if kind in ("sum", "attr") else m[:, g, k, :]
                            else:
                                a = K.ones[:, :] if kind == "attr" else w[:, g, k, 0:h]
                            mm = nc.tensor.matmul(psum[g][0:a.shape[1], s, b, :], a, oh[:, g, k, :],
                                                  start=j == 0, stop=j == CAPS - 1)
                mm.then_inc(s_sum, 1)

            def spread(n, g, r):
                if kind == "gatmax":
                    pe.wait_ge(s_rows[g], r * rowinc + rowinc)
                else:
                    pe.wait_ge(s_val, n + 1)
                for b in range(GB + 1):
                    if b < GB:
                        if not (b == 0 and isinstance(n, int) and n == 0):
                            pe.wait_ge(s_tc, n * GB + b)
                        for j in range(CAPS):
                            k = b * CAPS + j
                            a = rows[:, g, k, D:D + 4] if kind == "gatmax" else w[:, g, k, :]
                            mm = nc.tensor.transpose(pt[:, j * P:(j + 1) * P], a, K.ident[:, :])
                        mm.then_inc(s_tt, 1)
                    if b == 0:
                        continue
                    b1 = b - 1
                    pe.wait_ge(s_tc, n * GB + b1 + 1)
                    pe.wait_ge(s_nt, n + 1)
                    for hg in range(HG):
                        pe.wait_ge(s_mr, n * (GB * HG) + b1 * HG + hg + 1)
                        for c, c1 in [(c, min(CAP, c + 512)) for c in range(0, CAP, 512)]:
                            nc.tensor.matmul(pm[:, c:c1], K.negb[:, :], NT[:, g, b1 * CAP + c:b1 * CAP + c1],
                                             start=True, stop=False)
                            mm = nc.tensor.matmul(pm[:, c:c1], K.hs32[0:heads, hg, :], wT[:, b1, c:c1],
                                                  start=False, stop=True)
                        mm.then_inc(s_pm, 1)

            if kind in ("sum", "attr"):
                pipelined(pe, sums_free(pe, sums, s_done), nothing)
            elif kind == "gatmax":
                pipelined(pe, spread, nothing)
            elif kind == "logits":
                pipelined(pe, expand, spread)
            else:
                pipelined(pe, expand, sums_free(pe, sums, s_done))

        @block.scalar
        def _(ac):
            def keep_rows(n, g, r):
                ac.wait_ge(s_rows[g], r * rowinc + rowinc)
                c0, c1, dram = store
                ac.dma_start(dram[:, span(n, MG), :], rows[:, g, :, c0:c1]).then_inc(s_kept[g], 16)

            def complement(n, g, r):
                ac.wait_ge(s_t[g], r * 16 + 16)
                nc.scalar.copy(NT[:, g, :], T[:, g, :]).then_inc(s_nt, 1)

            def copy_T(n, g, r):
                for b in range(GB):
                    ac.wait_ge(s_tt, n * GB + b + 1)
                    nc.scalar.copy(wT[:, b, :], pt[:, 0:CAP]).then_inc(s_tc, 1)

            def keep_sums(n, g, r):
                ac.wait_ge(s_sum, n + 1)
                if kind in ("gat", "attn"):
                    nc.scalar.copy(K.acc[0:h, 1, span(n, GB * BN)], psum[g][0:h, 1, :, :].rearrange("p b n -> p (b n)"))
                    o = nc.scalar.copy(K.acc[:, 0, span(n, GB * BN)], psum[g][:, 0, :, :].rearrange("p b n -> p (b n)"))
                else:
                    o = nc.scalar.copy(K.acc[:, 0:NS, span(n, GB * BN)],
                                       psum[g][:, :, :, :].rearrange("p s b n -> p s (b n)"))
                o.then_inc(s_done, 1)

            def first(n, g, r):
                if store is not None:
                    keep_rows(n, g, r)
                if kind == "gatmax":
                    complement(n, g, r)
                    copy_T(n, g, r)
                if kind in ("sum", "attr"):
                    keep_sums(n, g, r)
                if kind == "conv":
                    ac.wait_ge(s_exp, n + 1)
                    nc.scalar.activation(sq[:, g, :, :], big[g][:, 0:MG, :], ACT.Square).then_inc(s_sq, 1)
                if soft:
                    ac.wait_ge(s_pre, n + 1)
                    nc.scalar.activation(w[:, g, :, 0:h], z[:, g, :, 0:h], ACT.Exp).then_inc(s_w, 1)

            def second(n, g, r):
                if kind == "conv":
                    ac.wait_ge(s_pre, n + 1)
                    nc.scalar.activation(m[:, g, :, :], m[:, g, :, :], ACT.Silu).then_inc(s_val, 1)
                if kind == "logits":
                    complement(n, g, r)
                    ac.wait_ge(s_val, n + 1)
                    nc.scalar.copy(LG[:, span(n, MG * 8)], w[:, g, :, :].rearrange("p k h -> p (k h)"))
                    copy_T(n, g, r)
                elif kind not in ("gatmax", "sum", "attr"):
                    keep_sums(n, g, r)

            pipelined(ac, first, second)

        per_a = {"conv": 15, "gat": 3, "attn": 1, "prod": 1, "logits": 3}.get(kind, 0)

        @block.vector
        def _(ve):
            ve.sem_inc(s_rfree, 2)
            ve.sem_inc(s_tfree, 2)
            ve.sem_inc(s_done, 2)
            ve.sem_inc(s_efree, ne)
            ve.sem_inc(s_mr, 1)

            def onehot(n, g):
                ve.wait_ge(s_done, n + 1)
                return nc.vector.tensor_tensor(oh[:, g, :, :], bc(K.iota[:, 0:BN].unsqueeze(1), [P, MG, BN]),
                                               bc(K.reg_m.dls[:, span(n, MG)].unsqueeze(2), [P, MG, BN]), ALU.is_equal)

            def maxima(n, g):
                for b in range(GB):
                    for hg in range(HG):
                        u0 = n * (GB * HG) + b * HG + hg
                        ve.wait_ge(s_pm, u0 + 1)
                        nc.vector.tensor_reduce(MX[:, hg, span(n * GB + b, 1)], pm[:, 0:CAP], AX.X, ALU.max).then_inc(s_mr, 1)
                ve.wait_ge(s_mr, n * (GB * HG) + GB * HG + 1)

            def first(n, g, r):
                link = Chain(ve, s_va, n * per_a)
                groups = lambda t: t.rearrange("p k (h f) -> p (k h) f", h=8)
                if kind in ("sum", "attr"):
                    onehot(n, g).then_inc(s_oh, 1)
                    ve.wait_ge(s_sum, n + 1)
                    ve.sem_inc(s_rfree, 1)
                if kind == "gatmax":
                    maxima(n, g)
                    ve.wait_ge(s_kept[g], r * 16 + 16)
                    ve.sem_inc(s_rfree, 1)
                    ve.sem_inc(s_tfree, 1)
                if soft:
                    onehot(n, g)
                    ve.wait_ge(s_exp, n + 1)
                    ve.wait_ge(s_rows[g], r * rowinc + rowinc)
                    if kind == "gat":
                        link(nc.vector.tensor_tensor(u[:, g, :, :], rows[:, g, :, D:D + 4], pl[g][:, :, 0:4], ALU.add))
                        link(nc.vector.scalar_tensor_tensor(out=u[:, g, :, :], in0=u[:, g, :, :], scalar=0.2,
                                                            in1=u[:, g, :, :], op0=ALU.mult, op1=ALU.max))
                        link(nc.vector.tensor_tensor(z[:, g, :, 0:4], u[:, g, :, :], pl[g][:, :, 4:8], ALU.subtract))
                    else:
                        link(nc.vector.tensor_tensor(z[:, g, :, :],
                                                     LG[:, span(n, MG * 8)].rearrange("p (k h) -> p k h", h=8),
                                                     pl[g][:, :, :], ALU.subtract))
                    ve.sem_inc(s_pre, 1)
                    ve.sem_inc(s_efree, 1)
                    ve.sem_inc(s_tfree, 1)
                if kind == "prod":
                    onehot(n, g)
                    ve.wait_ge(s_exp, n + 1)
                    ve.wait_ge(s_rows[g], r * rowinc + rowinc)
                    link(nc.vector.tensor_tensor(m[:, g, :, :], rows[:, g, :, :], big[g][:, 0:MG, :], ALU.mult))
                    for s in (s_val, s_efree, s_tfree, s_rfree):
                        ve.sem_inc(s, 1)
                if kind == "logits":
                    ve.wait_ge(s_exp, n + 1)
                    ve.wait_ge(s_rows[g], r * rowinc + rowinc)
                    link(nc.vector.tensor_tensor(m[:, 0, :, :], rows[:, g, :, 0:D], big[0][:, 0:MG, :], ALU.mult))
                    link(nc.vector.tensor_reduce(z[:, g, :, :].rearrange("p k h -> p (k h)"), groups(m[:, 0, :, :]),
                                                 AX.X, ALU.add))
                    link(nc.vector.tensor_tensor(w[:, g, :, :], z[:, g, :, :], pl[0][:, :, :], ALU.add))
                    ve.sem_inc(s_val, 1)
                    ve.sem_inc(s_efree, 1)
                    ve.wait_ge(s_kept[g], r * 16 + 16)
                    ve.sem_inc(s_rfree, 1)
                if kind == "conv":
                    onehot(n, g)
                    ve.wait_ge(s_sq, n + 1)
                    ve.sem_inc(s_rfree, 1)
                    ve.sem_inc(s_tfree, 1)
                    link(nc.vector.tensor_reduce(y[:, 0, :], groups(sq[:, g, :, :]), AX.X, ALU.add))
                    link(nc.vector.tensor_scalar(y[:, 0, :], y[:, 0, :], 1.0 / 16, EPS, ALU.mult, ALU.add))
                    link(nc.vector.tensor_scalar(y[:, 1, :].bitcast(I32), y[:, 0, :].bitcast(I32), -0.5,
                                                 float(0x5f3759df), ALU.mult, ALU.add))
                    for _ in range(3):
                        link(nc.vector.scalar_tensor_tensor(out=y[:, 2, :], in0=y[:, 1, :], scalar=-0.5,
                                                            in1=y[:, 0, :], op0=ALU.mult, op1=ALU.mult))
                        link(nc.vector.tensor_tensor(y[:, 2, :], y[:, 2, :], y[:, 1, :], ALU.mult))
                        link(nc.vector.scalar_tensor_tensor(out=y[:, 1, :], in0=y[:, 2, :], scalar=1.5,
                                                            in1=y[:, 1, :], op0=ALU.add, op1=ALU.mult))
                    link(nc.vector.tensor_tensor(groups(m[:, g, :, :]), groups(big[g][:, 0:MG, :]),
                                                 bc(y[:, 1, :].unsqueeze(2), [P, MG * 8, 16]), ALU.mult))
                    ve.sem_inc(s_efree, 1)
                    link(nc.vector.tensor_tensor(m[:, g, :, :], m[:, g, :, :], bc(gcol.unsqueeze(1), [P, MG, D]), ALU.mult))
                    link(nc.vector.tensor_tensor(m[:, g, :, :], m[:, g, :, :], bc(btcol.unsqueeze(1), [P, MG, D]), ALU.add))
                    ve.sem_inc(s_pre, 1)
                assert link.k == per_a, (kind, link.k)

            def second(n, g, r):
                if soft:
                    link = Chain(ve, s_vb, n)
                    ve.wait_ge(s_w, n + 1)
                    link(nc.vector.tensor_tensor(m[:, g, :, :].rearrange("p k (h f) -> p k h f", h=h),
                                                 rows[:, g, :, 0:D].rearrange("p k (h f) -> p k h f", h=h),
                                                 bc(w[:, g, :, 0:h].unsqueeze(3), [P, MG, h, D // h]), ALU.mult))
                    ve.sem_inc(s_val, 1)
                    ve.sem_inc(s_rfree, 1)
                if kind == "logits":
                    maxima(n, g)
                    ve.sem_inc(s_tfree, 1)

            pipelined(ve, first, second)


def sums_free(eng, sums, s_done):
    def step(n, g, r):
        eng.wait_ge(s_done, n + 1)
        sums(n, g, r)
    return step



def bucket_maxima(nc, B, K, MX, groups, ps, pe):
    for hg in range(groups):
        for h in range(4):
            m = nc.tensor.matmul(ps[hg][:, h * NB:(h + 1) * NB], K.ident[:, 32 * h:32 * h + 32], MX[:, hg, :],
                                 start=True, stop=True, skip_group_check=True)
    return m


@phase
def gat_tables(nc, B, K, T0, MX, tab8, u4):
    s_ld, s_mm, s_v, s_e = B.sem("logits_loaded"), B.sem("maxima_spread"), B.sem("table_chain"), B.sem("own_weight")
    s_ws, s_cp = B.sem("weight_spread"), B.sem("weight_copied")
    per = 512 // BN
    banks = -(-NB // per)
    with ExitStack() as ph:
        a = B.sb("a", [BN, NB, 8], F32, ph)
        t = B.sb("t", [BN, NB, 4], F32, ph)
        u = B.sb("u", [BN, NB, 4], F32, ph)
        ps = [B.ps("ps", [BN, 512], ph)]
        pw = [B.ps("pw", [4, 512], ph) for _ in range(2)]
        block = ph.enter_context(nc.Block())
        tab = tab8[:, :].rearrange("p (b c) -> p b c", c=8)

        @block.sync
        def _(sp):
            sp.dma_start(a[:, :, :], T0.rearrange("(b p) d -> p b d", p=BN)[:, :, D:D + 8]).then_inc(s_ld, 16)

        @block.tensor
        def _(pe):
            bucket_maxima(nc, B, K, MX, 1, ps, pe).then_inc(s_mm, 1)
            pe.wait_ge(s_e, 1)
            for c in range(banks):
                if c >= 2:
                    pe.wait_ge(s_cp, c - 1)
                for b in range(c * per, min(NB, (c + 1) * per)):
                    m = nc.tensor.matmul(pw[c % 2][:, (b - c * per) * BN:(b - c * per + 1) * BN],
                                         u[:, b, :], K.ident[0:BN, 0:BN],
                                         start=True, stop=True, skip_group_check=True)
                m.then_inc(s_ws, 1)

        @block.scalar
        def _(ac):
            ac.wait_ge(s_v, 8)
            nc.scalar.activation(u[:, :, :], u[:, :, :], ACT.Exp).then_inc(s_e, 1)

        @block.vector
        def _(ve):
            link = Chain(ve, s_v)
            ve.wait_ge(s_ld, 16)
            ve.wait_ge(s_mm, 1)
            mxv = ps[0][:, 0:4 * NB].rearrange("p (h b) -> p b h", h=4)
            link(nc.vector.tensor_tensor(t[:, :, :], a[:, :, 0:4], mxv, ALU.max))
            link(nc.vector.tensor_tensor(t[:, :, :], t[:, :, :], a[:, :, 4:8], ALU.add))
            link(nc.vector.scalar_tensor_tensor(out=tab[:, :, 4:8], in0=t[:, :, :], scalar=0.2, in1=t[:, :, :],
                                                op0=ALU.mult, op1=ALU.max))
            link(nc.vector.tensor_copy(tab[:, :, 0:4], a[:, :, 4:8]))
            link(nc.vector.tensor_tensor(t[:, :, :], a[:, :, 0:4], a[:, :, 4:8], ALU.add))
            link(nc.vector.tensor_scalar(u[:, :, :], t[:, :, :], 0.2, None, ALU.mult))
            link(nc.vector.tensor_tensor(u[:, :, :], u[:, :, :], t[:, :, :], ALU.max))
            link(nc.vector.tensor_tensor(u[:, :, :], u[:, :, :], tab[:, :, 4:8], ALU.subtract))
            for c in range(banks):
                w = min(NP, (c + 1) * 512) - c * 512
                ve.wait_ge(s_ws, c + 1)
                nc.vector.tensor_copy(u4[:, c * 512:c * 512 + w], pw[c % 2][:, 0:w]).then_inc(s_cp, 1)


@phase
def attn_table(nc, B, K, MX, tab8):
    s_mm, s_v = B.sem("maxima_spread"), B.sem("table_chain")
    with ExitStack() as ph:
        ps = [B.ps("ps", [BN, 512], ph) for _ in range(2)]
        block = ph.enter_context(nc.Block())

        @block.tensor
        def _(pe):
            bucket_maxima(nc, B, K, MX, 2, ps, pe).then_inc(s_mm, 1)

        @block.vector
        def _(ve):
            ve.wait_ge(s_mm, 1)
            tab = tab8[:, :].rearrange("p (b c) -> p b c", c=8)
            for hg in range(2):
                nc.vector.tensor_copy(tab[:, :, 4 * hg:4 * hg + 4],
                                      ps[hg][:, 0:4 * NB].rearrange("p (h b) -> p b h", h=4)).then_inc(s_v, 1)
            ve.wait_ge(s_v, 2)


@phase
def batch_norm(nc, B, K):
    s_v, s_r = B.sem("stat_chain"), B.sem("root")
    O = K.acc[:, 0, 0:N]
    with ExitStack() as ph:
        st = B.sb("st", [P, 4], F32, ph)
        block = ph.enter_context(nc.Block())

        @block.scalar
        def _(ac):
            ac.wait_ge(s_v, 6)
            nc.scalar.activation(st[:, 2:3], st[:, 1:2], ACT.Sqrt).then_inc(s_r, 1)

        @block.vector
        def _(ve):
            link = Chain(ve, s_v)
            link(nc.vector.tensor_reduce(st[:, 0:1], O, AX.X, ALU.add))
            link(nc.vector.tensor_scalar(st[:, 0:1], st[:, 0:1], 1.0 / N, None, ALU.mult))
            link(nc.vector.tensor_scalar(O, O, st[:, 0:1], None, ALU.subtract))
            link(nc.vector.tensor_tensor(K.acc[:, 1, 0:N], O, O, ALU.mult))
            link(nc.vector.tensor_reduce(st[:, 1:2], K.acc[:, 1, 0:N], AX.X, ALU.add))
            link(nc.vector.tensor_scalar(st[:, 1:2], st[:, 1:2], 1.0 / N, EPS, ALU.mult, ALU.add))
            ve.wait_ge(s_r, 1)
            link(nc.vector.reciprocal(st[:, 3:4], st[:, 2:3]))
            link(nc.vector.tensor_tensor(st[:, 3:4], st[:, 3:4], K.c["L0_gnn_gamma"][:, :], ALU.mult))
            link(nc.vector.tensor_scalar(O, O, st[:, 3:4], K.c["L0_gnn_beta"][:, :], ALU.mult, ALU.add))
            link(nc.vector.tensor_tensor(K.X[:, 0:N], K.X[:, 0:N], O, ALU.add))


@phase
def store_x(nc, B, K, out):
    s_tr, s_cp, s_st = B.sem("transposed"), B.sem("copied"), B.sem("result_stored")
    with ExitStack() as ph:
        xn = B.sb("xn", [P, TILES, D], F32, ph)
        ps = [B.ps("ps", [P, P], ph) for _ in range(2)]
        block = ph.enter_context(nc.Block())
        full, rest = N // P, N % P

        @block.tensor
        def _(pe):
            for t in range(TILES):
                if t >= 2:
                    pe.wait_ge(s_cp, t - 1)
                nc.tensor.transpose(ps[t % 2][:, :], K.X[:, t * P:(t + 1) * P], K.ident[:, :]).then_inc(s_tr, 1)

        @block.vector
        def _(ve):
            for t in range(TILES):
                ve.wait_ge(s_tr, t + 1)
                nc.vector.tensor_copy(xn[:, t, :], ps[t % 2][:, :]).then_inc(s_cp, 1)

        @block.sync
        def _(sp):
            sp.wait_ge(s_cp, TILES)
            sp.dma_start(out[0:full * P, :].rearrange("(t p) d -> p t d", p=P), xn[:, 0:full, :]).then_inc(s_st, 16)
            sp.dma_start(out[full * P:N, :], xn[0:rest, full, :]).then_inc(s_st, 16)
            sp.wait_ge(s_st, 32)


def program(nc, A, out, upto=99):
    with ExitStack() as ctx:
        B = Build(nc, ctx)

        class K:
            pass

        K.rec = B.dram("records", [(MSLOTS + SLOTS) * P, REC])
        K.bucket_dram = B.dram("slot_buckets", [512], I32)
        K.X = B.sb("X", [P, NP])
        K.H = B.sb("H", [P, NP])
        K.acc = B.sb("acc", [P, 2, NP])
        K.cnt = B.sb("cnt", [P, NP])
        constants(nc, B, A, K)
        rank_edges(nc, B, A, K)
        scatter_records(nc, B, A, K)

        class Region:
            def __init__(self, over, slots, groups, rec):
                self.over, self.slots, self.groups = over, slots, groups
                self.rec = rec.rearrange("(s p) w -> p s w", p=P)
                self.src = B.dram("sources", [P, slots * groups], I32)
                self.t = B.dram("operands", [groups, TR, slots * P])
                self.dls = B.sb("dst_local", [P, slots * groups])

            def rows(self, width):
                return B.dram("slot_rows", [P, self.slots * self.groups, width])

        K.reg_m = Region(False, MG, MGROUPS, K.rec[0:OVER, :])
        K.reg_o = Region(True, GS, GROUPS, K.rec[OVER:, :])
        make_operands(nc, B, A, K, K.reg_m)
        make_operands(nc, B, A, K, K.reg_o)
        load_x(nc, B, A, K)

        def edge_pass(kind, kept=None, LG=None, **kw):
            for f, j in ((bucket_pass, 0), (overflow_pass, 1)):
                args = dict(kw)
                if kept:
                    name, c0, c1, arrays = kept
                    args[name] = arrays[j] if name == "linear" else (c0, c1, arrays[j])
                f(nc, B, K, kind, LG=LG[j] if LG else None, **args)

        V = nc.vector
        acc0, acc1 = K.acc[:, 0, :], K.acc[:, 1, :]

        norm_nodes(nc, B, A, K)
        T0 = B.dram("gat_rows", [NP, 136])
        gs = [r.rows(132) for r in (K.reg_m, K.reg_o)]
        project_nodes(nc, B, K, [(K.H, [K.w0[:, :]])], 136, T0)
        with ExitStack() as l0:
            MX = B.sb("MX", [P, 1, NB], F32, l0)
            tab8 = B.sb("tab8", [BN, NB * 8], F32, l0)
            wsf = B.sb("wsf", [P, NP], F32, l0)
            u4 = B.sb("own_weights", [4, NP], F32, l0)
            r4 = B.sb("inverse_sums", [4, NP], F32, l0)
            edge_pass("gatmax", gather=T0, gw=136, kept=("store", 0, 132, gs), MX=MX, heads=4)
            gat_tables(nc, B, K, T0, MX, tab8, u4)
            edge_pass("gat", kept=("linear", 0, 132, gs), lw=132, tab=tab8, tw=8, heads=4)

            def inverse(link):
                link(V.scalar_tensor_tensor(out=r4[:, :], in0=acc1[0:4, :], scalar=1e-16, in1=u4[:, :],
                                            op0=ALU.add, op1=ALU.add))
                link(V.reciprocal(r4[:, :], r4[:, :]))

            def spread(sl, ps, link):
                link(V.tensor_copy(wsf[:, sl], ps))

            def own(sl, ps, link):
                link(V.tensor_tensor(wsf[:, sl], ps, wsf[:, sl], ALU.mult))
                link(V.tensor_tensor(acc0[:, sl], acc0[:, sl], wsf[:, sl], ALU.add))

            def scale(sl, ps, link):
                link(V.tensor_tensor(acc0[:, sl], acc0[:, sl], ps, ALU.mult))
                link(V.tensor_scalar(acc0[:, sl], acc0[:, sl], K.c["L0_gnn_bias"][:, :], None, ALU.add))

            vector_phase(nc, B, inverse)
            feature_product(nc, B, K, [(K.hs32[0:4, 0, :], u4)], spread, 1)
            feature_product(nc, B, K, [(K.w0[:, 0:D], K.H)], own, 2)
            feature_product(nc, B, K, [(K.hs32[0:4, 0, :], r4)], scale, 2)
        batch_norm(nc, B, K)
        if upto <= 0:
            return store_x(nc, B, K, out)

        norm_nodes(nc, B, A, K)
        edge_pass("attr", kept=("linear", 0, D, (K.reg_m.rec, K.reg_o.rec)), lw=D)
        with ExitStack() as l1:
            agg = B.sb("agg", [P, NP], F32, l1)
            Y = B.dram("gin_rows", [NP, D])

            def embed(sl, ps, link):
                link(V.tensor_copy(K.cnt[:, sl], acc1[:, sl]))
                link(V.scalar_tensor_tensor(out=agg[:, sl], in0=acc1[:, sl], scalar=K.c["L1_gnn_be"][:, :], in1=ps,
                                            op0=ALU.mult, op1=ALU.add))

            feature_product(nc, B, K, [(K.w["L1_gnn_We"][:, :], acc0)], embed, 2)
            both = [(K.H, [K.w1a[:, :]]), (agg, [K.w1b[:, :]])]
            project_nodes(nc, B, K, both, D, Y)
            edge_pass("sum", gather=Y, gw=D)

            def hidden(sl, ps, link):
                link(V.tensor_tensor(acc0[:, sl], acc0[:, sl], ps, ALU.add))
                link(V.tensor_scalar(acc0[:, sl], acc0[:, sl], K.c["L1_gnn_b1"][:, :], 0.0, ALU.add, ALU.max))

            feature_product(nc, B, K, [(K.w1a[:, :], K.H), (K.w1b[:, :], agg)], hidden, 2)

            def add_out(sl, ps, link):
                link(V.scalar_tensor_tensor(out=K.X[:, sl], in0=ps, scalar=K.c["L1_gnn_b2"][:, :], in1=K.X[:, sl],
                                            op0=ALU.add, op1=ALU.add))

            feature_product(nc, B, K, [(K.w["L1_gnn_W2"][:, :], acc0)], add_out, 1)
        if upto <= 1:
            return store_x(nc, B, K, out)

        norm_nodes(nc, B, A, K)
        rows_a, rows_b = B.dram("dst_rows", [NP, D]), B.dram("src_rows", [NP, D])
        for i, c in enumerate(("c1", "c2")):
            inp = K.H if i == 0 else acc1
            project_nodes(nc, B, K, [(inp, [K.ca[i][:, :]])], D, rows_a)
            project_nodes(nc, B, K, [(inp, [K.cb[i][:, :]])], D, rows_b)
            with ExitStack() as l2:
                tab = B.sb("tab", [BN, NB, D], F32, l2)
                load_table(nc, B, rows_a, tab)
                edge_pass("conv", gather=rows_b, gw=D, tab=tab[:, :, :].rearrange("p b d -> p (b d)"),
                          tw=D, static=K.cs[i], gcol=K.r[f"L2_gnn_{c}_g"][:, :], btcol=K.r[f"L2_gnn_{c}_bt"][:, :])

            def mean(sl, ps, link):
                link(V.scalar_tensor_tensor(out=acc1[:, sl], in0=K.cnt[:, sl], scalar=K.c[f"L2_gnn_{c}_b2"][:, :],
                                            in1=ps, op0=ALU.mult, op1=ALU.add))
                link(V.tensor_scalar(acc0[:, sl], K.cnt[:, sl], 1.0, None, ALU.max))
                link(V.reciprocal(acc0[:, sl], acc0[:, sl]))
                link(V.tensor_tensor(acc1[:, sl], acc1[:, sl], acc0[:, sl], ALU.mult))

            feature_product(nc, B, K, [(K.w[f"L2_gnn_{c}_w2"][:, :], acc0)], mean, 4)
            n = f"L2_gnn_n{i + 1}_"
            group_norm(nc, B, K, acc1, K.c[n + "g"], K.c[n + "b"], ACT.Silu, acc1)
            if i == 0:
                vector_phase(nc, B, lambda link: link(
                    V.tensor_scalar(acc1, acc1, K.tvec[:, :], None, ALU.add)))
            else:
                vector_phase(nc, B, lambda link: link(V.tensor_tensor(K.H[:, :], K.H[:, :], acc1, ALU.add)))
        KV, Q = B.dram("kv_rows", [NP, 2 * D]), rows_a
        vs = [r.rows(D) for r in (K.reg_m, K.reg_o)]
        project_nodes(nc, B, K, [(K.H, [K.w["L2_gnn_kw"][:, :], K.w["L2_gnn_vw"][:, :]])], 2 * D, KV,
                      row=[K.r["L2_gnn_kb"][:, :], K.r["L2_gnn_vb"][:, :]])
        project_nodes(nc, B, K, [(K.H, [K.w["L2_gnn_qw"][:, :]])], D, Q, row=[K.r["L2_gnn_qb"][:, :]], scale=0.25)
        with ExitStack() as l2:
            MX = B.sb("MX", [P, 2, NB], F32, l2)
            LG = (B.sb("logits", [P, MSLOTS * 8], F32, l2), K.reg_o.rows(8))
            with ExitStack() as l3:
                tab = B.sb("tab", [BN, NB, D], F32, l3)
                load_table(nc, B, Q, tab)
                edge_pass("logits", gather=KV, gw=2 * D, kept=("store", D, 2 * D, vs), MX=MX, heads=8, LG=LG,
                          tab=tab[:, :, :].rearrange("p b d -> p (b d)"), tw=D, static=K.ew)
            tab8 = B.sb("tab8", [BN, NB * 8], F32, l2)
            attn_table(nc, B, K, MX, tab8)
            edge_pass("attn", kept=("linear", 0, D, vs), lw=D, tab=tab8, tw=8, heads=8, LG=LG)

        def divide(link):
            link(V.tensor_scalar(acc1[0:8, :], acc1[0:8, :], 1e-6, None, ALU.max))
            link(V.reciprocal(acc1[0:8, :], acc1[0:8, :]))

        vector_phase(nc, B, divide)

        def scale8(sl, ps, link):
            link(V.tensor_tensor(acc0[:, sl], acc0[:, sl], ps, ALU.mult))

        feature_product(nc, B, K, [(K.hs16[:, :], acc1[0:8, :])], scale8, 1)

        def attn_out(sl, ps, link):
            link(V.tensor_scalar(acc1[:, sl], ps, K.c["L2_gnn_ob"][:, :], None, ALU.add))

        feature_product(nc, B, K, [(K.w["L2_gnn_ow"][:, :], acc0)], attn_out, 1)
        group_norm(nc, B, K, acc1, K.c["L2_gnn_an_g"], K.c["L2_gnn_an_b"], ACT.Identity, acc1)

        def add_layer(link):
            link(V.tensor_tensor(K.X[:, :], K.X[:, :], K.H[:, :], ALU.add))
            link(V.tensor_tensor(K.X[:, :], K.X[:, :], acc1, ALU.add))

        vector_phase(nc, B, add_layer)
        if upto <= 2:
            return store_x(nc, B, K, out)

        norm_nodes(nc, B, A, K)
        project_nodes(nc, B, K, [(K.H, [K.w["L3_gnn_W"][:, :]])], D, rows_a)
        edge_pass("prod", gather=rows_a, gw=D, static=K.w3)
        vector_phase(nc, B, lambda link: link(V.scalar_tensor_tensor(
            out=K.X[:, :], in0=acc0, scalar=K.c["L3_gnn_b"][:, :], in1=K.X[:, :], op0=ALU.add, op1=ALU.add)))
        store_x(nc, B, K, out)


def kernel(**inputs):
    import numpy as _np
    import concourse.bacc as _bacc
    from concourse import mybir as _mybir
    from concourse.bass_utils import run_bass_kernel_spmd as _run

    nc = _bacc.Bacc("TRN2", target_bir_lowering=False, num_devices=1)
    arrays, args = {}, {}
    for name, a in inputs.items():
        a = _np.ascontiguousarray(a)
        arrays[f"in_{name}"] = a
        args[name] = nc.dram_tensor(f"in_{name}", a.shape, _mybir.dt.from_np(a.dtype), kind="ExternalInput").ap()
    out = nc.dram_tensor("out_0", (N, D), _mybir.dt.float32, kind="ExternalOutput").ap()
    program(nc, args, out)
    r = _run(nc, [arrays], core_ids=[0])
    return r.results[0]["out_0"]
```

```python
import concourse.bass as bass
from concourse import mybir
from contextlib import ExitStack

F32 = mybir.dt.float32
I32 = mybir.dt.int32
U8 = mybir.dt.uint8
ALU = mybir.AluOpType
ACT = mybir.ActivationFunctionType
AX = mybir.AxisListType

N = 3125
E = 50000
D = 128
P = 128
BN = 32
NBUK = -(-N // BN)
TILES = -(-N // P)
NP = TILES * P
NB = NP // BN
EP = 125
EC = E // EP
RING = 4
GS = 4
CAPS = 5
CAP = CAPS * P
GB = 2
MG = GB * CAPS
MGROUPS = NB // GB
MSLOTS = NB * CAPS
MW = MG * P
OVER = MSLOTS * P
SLOTS_MIN = (E - CAP + NBUK * (P - 1)) // P
TRIPS = -(-SLOTS_MIN // (RING * GS))
GROUPS = TRIPS * RING
SLOTS = GROUPS * GS
REC = 152
META = 24
TR = 96
CH = 400
NCH = NP // CH
BF16 = mybir.dt.bfloat16
BIG = 1.0e30
EPS = 1e-5


class Chain:

    def __init__(self, eng, sem, base=0):
        self.eng, self.sem, self.base, self.k = eng, sem, base, 0

    def __call__(self, ins):
        self.k += 1
        ins.then_inc(self.sem, 1)
        self.eng.wait_ge(self.sem, self.base + self.k)


class Build:

    def __init__(self, nc, ctx):
        self.nc, self.ctx, self.n = nc, ctx, 0

    def name(self, s):
        self.n += 1
        return f"{s}_{self.n}"

    def sb(self, s, shape, dt=F32, ctx=None):
        return (ctx or self.ctx).enter_context(self.nc.sbuf_tensor(self.name(s), shape, dt))

    def ps(self, s, shape, ctx, dt=F32):
        return ctx.enter_context(self.nc.psum_tensor(self.name(s), shape, dt))

    def sem(self, s):
        self.sems.append(self.nc.alloc_semaphore(self.name(s)))
        return self.sems[-1]

    def dram(self, s, shape, dt=F32):
        return self.nc.dram_tensor(self.name(s), shape, dt, kind="Internal").ap()


def phase(f):
    def run(nc, B, *args, **kw):
        B.sems = []
        f(nc, B, *args, **kw)
        nc.clear_and_free_semaphores(B.sems)
        nc.all_engine_barrier()
    return run


def bc(ap, shape):
    return ap.to_broadcast(shape)


def overflowed(eng, K):
    return eng.If(eng.value_load(K.over[0:1, 0:1], min_val=0, max_val=SLOTS) > 0)


def pipelined(eng, first, second, lag=1):
    if lag == 2:
        first(0, 0, 0)
        first(1, 1, 0)
        with eng.Fori(0, MGROUPS // 2 - 1) as i:
            first(i * 2 + 2, 0, i + 1)
            second(i * 2, 0, i)
            first(i * 2 + 3, 1, i + 1)
            second(i * 2 + 1, 1, i)
        second(MGROUPS - 2, 0, MGROUPS // 2 - 1)
        second(MGROUPS - 1, 1, MGROUPS // 2 - 1)
        return
    half = (MGROUPS - 2) // 2
    first(0, 0, 0)
    with eng.Fori(0, half) as i:
        first(i * 2 + 1, 1, i)
        second(i * 2, 0, i)
        first(i * 2 + 2, 0, i + 1)
        second(i * 2 + 1, 1, i)
    first(MGROUPS - 1, 1, half)
    second(MGROUPS - 2, 0, half)
    second(MGROUPS - 1, 1, half)


def in_pairs(eng, groups, step):
    step(0, 0, 0)
    step(1, 1, 0)
    with eng.Fori(0, groups // 2 - 1) as i:
        step(i * 2 + 2, 0, i + 1)
        step(i * 2 + 3, 1, i + 1)


def span(n, size):
    return slice(n * size, (n + 1) * size) if isinstance(n, int) else bass.ds(n * size, size)


def at(start, size):
    return slice(start, start + size) if isinstance(start, int) else bass.ds(start, size)



WEIGHTS = ["L1_gnn_We", "L1_gnn_W2", "L2_gnn_c1_w2", "L2_gnn_c2_w2", "L2_gnn_qw", "L2_gnn_kw",
           "L2_gnn_vw", "L2_gnn_ow", "L3_gnn_W"]
COLS = ["L0_gnn_gamma", "L0_gnn_beta", "L1_gnn_be", "L1_gnn_b1", "L1_gnn_b2", "L2_gnn_c1_b2",
        "L2_gnn_c2_b2", "L2_gnn_tm_b", "L2_gnn_n1_g", "L2_gnn_n1_b", "L2_gnn_n2_g", "L2_gnn_n2_b",
        "L2_gnn_ob", "L2_gnn_an_g", "L2_gnn_an_b", "L3_gnn_b"]
ROWS = ["L2_gnn_c1_g", "L2_gnn_c1_bt", "L2_gnn_c2_g", "L2_gnn_c2_bt", "L2_gnn_qb", "L2_gnn_kb",
        "L2_gnn_vb"]


@phase
def constants(nc, B, A, K):
    s_w = B.sem("weights_loaded")
    s_p = B.sem("patterns_made")
    s_z = B.sem("zeroed")
    s_v = B.sem("vector_chain")
    s_a = B.sem("silu_made")
    s_t = B.sem("time_product")
    K.ident = B.sb("ident", [P, P])
    K.tri = B.sb("tri", [P, P])
    K.ones = B.sb("ones", [P, P])
    K.iota = B.sb("iota", [P, P])
    K.part = B.sb("part", [P, 1])
    K.gmean = B.sb("gmean", [P, P])
    K.slotid = B.sb("slotid", [P, 4])
    K.neg = B.sb("neg", [TR, 4, BN])
    K.identb = B.sb("identb", [P, P], BF16)
    K.spread = {4: B.sb("spread4", [TR, P], BF16), 8: B.sb("spread8", [TR, 2 * P], BF16)}
    K.hs32 = B.sb("hs32", [8, 2, P])
    K.hs16 = B.sb("hs16", [8, P])
    K.eqm = B.sb("eqm", [64, 1])
    K.eqc = B.sb("eqc", [64, 1])
    K.w = {n: B.sb(n, [D, D]) for n in WEIGHTS}
    K.c = {n: B.sb(n, [D, 1]) for n in COLS}
    K.c["L0_gnn_bias"] = B.sb("L0_bias", [D, 1])
    K.r = {n: B.sb(n, [P, D]) for n in ROWS}
    K.w0 = B.sb("L0_W", [D, 136])
    K.w1a = B.sb("L1_W1a", [D, D])
    K.w1b = B.sb("L1_W1b", [D, D])
    K.ca = [B.sb("conv_dst_w", [D, D]) for _ in range(2)]
    K.cb = [B.sb("conv_src_w", [D, D]) for _ in range(2)]
    K.cs = [B.sb("conv_edge_w", [TR, D]) for _ in range(2)]
    K.ew = B.sb("logit_edge_w", [TR, 8])
    K.w3 = B.sb("L3_edge_w", [TR, D])
    K.tvec = B.sb("time_vector", [D, 1])
    with ExitStack() as ph:
        att = B.sb("att", [P, 2, D], ctx=ph)
        prod = B.sb("prod", [P, 2, D], ctx=ph)
        gm = B.sb("gm", [P, 8, 8], ctx=ph)
        sp4 = B.sb("sp4", [TR, 4, BN], ctx=ph)
        sp8 = B.sb("sp8", [TR, 8, BN], ctx=ph)
        te = B.sb("te", [P, 4], ctx=ph)
        tes = B.sb("tes", [P, 4], ctx=ph)
        tw = B.sb("tw", [P, 4, D], ctx=ph)
        ii = B.sb("ii", [P, P], I32, ctx=ph)
        pi = B.sb("pi", [P, 1], I32, ctx=ph)
        si = B.sb("si", [P, 4], I32, ctx=ph)
        pst = B.ps("pst", [P, 8], ph)
        block = ph.enter_context(nc.Block())
        loads = []

        @block.gpsimd
        def _(po):
            step = Chain(po, s_p)
            step(nc.gpsimd.iota(ii[:, :], [[1, P]], base=0, channel_multiplier=0))
            step(nc.gpsimd.iota(pi[:, :], [[0, 1]], base=0, channel_multiplier=1))
            step(nc.gpsimd.iota(si[:, :], [[P, 4]], base=0, channel_multiplier=1))
            po.wait_ge(s_z, 10)

            def one_where(t, base, pattern, mult, fill=1.0):
                step(nc.gpsimd.affine_select(out=t, in_=t, compare_op=ALU.not_equal, fill=fill, base=base,
                                             pattern=pattern, channel_multiplier=mult))

            def keep_where(t, base, pattern, mult):
                step(nc.gpsimd.affine_select(out=t, in_=t, compare_op=ALU.is_ge, fill=0.0, base=base,
                                             pattern=pattern, channel_multiplier=mult))

            one_where(K.ident[:, :], 0, [[-1, P]], 1)
            keep_where(K.tri[:, :], -1, [[1, P]], -1)
            g3 = K.gmean[:, :].rearrange("p (g k) -> p g k", g=8)
            keep_where(g3, 0, [[-16, 8], [0, 16]], 1)
            keep_where(g3, 15, [[16, 8], [0, 16]], -1)
            one_where(K.neg[:, :, :], -32, [[0, 4], [-1, BN]], 1, BIG)
            one_where(K.hs32[:, :, :].rearrange("p a (h n) -> p (a h) n", h=4), 0, [[-1, 8], [0, 32]], 1)
            for t, heads in ((sp4, 4), (sp8, 8)):
                for j in range(3):
                    one_where(t[:, :, :], -64 - heads * j, [[-1, heads], [0, BN]], 1)
                one_where(t[:, :, :], -32, [[0, heads], [-1, BN]], 1, BIG)
            one_where(K.hs16[:, :].rearrange("p (h n) -> p h n", h=8), 0, [[-1, 8], [0, 16]], 1)

        @block.sync
        def _(sp):
            n = 0

            def load(dst, src):
                nonlocal n
                n += 16
                sp.dma_start(dst, src).then_inc(s_w, 16)

            for name in WEIGHTS:
                load(K.w[name][:, :], A[name])
            load(K.w1a[:, :], A["L1_gnn_W1"][0:D, :])
            load(K.w1b[:, :], A["L1_gnn_W1"][D:2 * D, :])
            for i, c in enumerate(("c1", "c2")):
                w = A[f"L2_gnn_{c}_w1"]
                load(K.ca[i][:, :], w[0:D, :])
                load(K.cb[i][:, :], w[D:2 * D, :])
            for h in range(4):
                load(K.w0[:, 32 * h:32 * h + 32], A["L0_gnn_W"][h, :, :])
            with nc.allow_non_contiguous_dma(reason="vectors as columns"):
                for name in COLS:
                    load(K.c[name][:, :], A[name].rearrange("(d a) -> d a", a=1))
                load(K.c["L0_gnn_bias"][:, :], A["L0_gnn_bias"].rearrange("h (f a) -> (h f) a", a=1))
                load(te[:, :], A["L2_gnn_t_emb"].rearrange("(c p) -> p c", p=P))
            for name in ROWS:
                load(K.r[name][:, :], A[name].partition_broadcast(P))
            load(tw[:, :, :], A["L2_gnn_tm_w"].rearrange("(c p) d -> p c d", p=P))
            for j, name in enumerate(("L0_gnn_att_src", "L0_gnn_att_dst")):
                load(att[:, j, :], A[name].rearrange("h f -> (h f)").partition_broadcast(P))
            sp.wait_ge(s_v, 4)
            for i, c in enumerate(("c1", "c2")):
                load(K.cs[i][66:70, :], A[f"L2_gnn_{c}_w1"][2 * D:2 * D + 4, :])
                load(K.cs[i][65:66, :], A[f"L2_gnn_{c}_b1"].rearrange("(a d) -> a d", a=1))
            load(K.ew[66:70, :], A["L2_gnn_ew"])
            load(K.ew[65:66, :], A["L2_gnn_eb"].rearrange("(a d) -> a d", a=1))
            load(K.w3[70:86, :], A["L3_gnn_edge_w"])
            sp.wait_ge(s_w, n)
            loads.append(n)

        @block.vector
        def _(ve):
            link = Chain(ve, s_v)
            for t in (K.cs[0], K.cs[1], K.ew, K.w3):
                link(nc.vector.memset(t[:, :], 0.0))
            link(nc.vector.memset(K.acc[:, :, :], 0.0))
            for t, v in ((K.ident, 0.0), (K.tri, 1.0), (K.ones, 1.0), (K.gmean, 1.0 / 16), (K.hs16, 0.0)):
                nc.vector.memset(t[:, :], v).then_inc(s_z, 1)
            nc.vector.memset(K.hs32[:, :, :], 0.0).then_inc(s_z, 1)
            for t in (K.neg, sp4, sp8):
                nc.vector.memset(t[:, :, :], 0.0).then_inc(s_z, 1)
            link(nc.vector.memset(K.eqc[0:32, :], 0.0))
            nc.vector.memset(K.eqc[32:64, :], 1.0).then_inc(s_z, 1)
            ve.wait_ge(s_p, 3)
            link(nc.vector.tensor_copy(K.iota[:, :], ii[:, :]))
            link(nc.vector.tensor_copy(K.part[:, :], pi[:, :]))
            link(nc.vector.tensor_copy(K.slotid[:, :], si[:, :]))
            link(nc.vector.tensor_copy(K.eqm[0:32, :], K.part[0:32, :]))
            link(nc.vector.tensor_scalar(K.eqm[32:64, :], K.part[32:64, :], 32.0, None, ALU.subtract))
            ve.wait_ge(s_p, 18)
            link(nc.vector.tensor_copy(K.identb[:, :], K.ident[:, :]))
            for heads, t in ((4, sp4), (8, sp8)):
                link(nc.vector.tensor_copy(K.spread[heads][:, :], t[:, :, :].rearrange("p h n -> p (h n)")))
            ve.wait_ge(s_w, loads[0])
            w0 = K.w0[:, 0:D]
            for j in range(2):
                link(nc.vector.tensor_tensor(prod[:, j, :], w0, att[:, j, :], ALU.mult))
                link(nc.vector.tensor_reduce(K.w0[:, D + 4 * j:D + 4 * j + 4],
                                             prod[:, j, :].rearrange("p (h f) -> p h f", h=4),
                                             AX.X, ALU.add))
            for t, rows in [(K.ca[0], D), (K.ca[1], D), (K.cb[0], D), (K.cb[1], D),
                            (K.cs[0], TR), (K.cs[1], TR)]:
                t3 = t[:, :].rearrange("p (g k) -> p g k", g=8)
                link(nc.vector.tensor_reduce(gm[0:rows, 0, :], t3, AX.X, ALU.add))
                link(nc.vector.tensor_scalar(gm[0:rows, 1, :], gm[0:rows, 0, :], 1.0 / 16, None, ALU.mult))
                link(nc.vector.tensor_tensor(t3, t3, bc(gm[0:rows, 1, :].unsqueeze(2), [rows, 8, 16]),
                                             ALU.subtract))
            link(nc.vector.tensor_scalar(K.r["L2_gnn_qb"][:, :], K.r["L2_gnn_qb"][:, :], 0.25, None, ALU.mult))
            ve.wait_ge(s_t, 1)
            link(nc.vector.tensor_tensor(K.tvec[:, :], pst[:, 0:1], K.c["L2_gnn_tm_b"][:, :], ALU.add))

        @block.scalar
        def _(ac):
            ac.wait_ge(s_w, loads[0])
            nc.scalar.activation(tes[:, :], te[:, :], ACT.Silu).then_inc(s_a, 1)

        @block.tensor
        def _(pe):
            pe.wait_ge(s_a, 1)
            for c in range(4):
                m = nc.tensor.matmul(pst[:, 0:1], tw[:, c, :], tes[:, c:c + 1], start=c == 0, stop=c == 3)
            m.then_inc(s_t, 1)



@phase
def rank_edges(nc, B, A, K):
    s_in, s_img, s_fill = B.sem("edges_loaded"), B.sem("padding_made"), B.sem("padding_stored")
    s_v, s_cnt, s_pre, s_out = B.sem("rank_chain"), B.sem("counted"), B.sem("prefix_made"), B.sem("table_stored")
    s_msk, s_add = B.sem("ranks_masked"), B.sem("ranks_added")
    s_sc, s_cp, s_ld, s_bk = B.sem("scanned"), B.sem("placed"), B.sem("table_loaded"), B.sem("buckets_made")
    K.pos = B.sb("pos", [EP, EC], I32)
    K.dl = B.sb("dl_unsorted", [EP, EC])
    K.bucket = B.sb("slot_bucket", [1, 512], I32)
    K.over = B.sb("overflow_slots", [1, 1], I32)
    fill = K.rec[0:OVER, :].rearrange("(p c k) w -> c p (k w)", p=P, c=10)
    fill_over = K.rec[OVER:, :].rearrange("(p c k) w -> c p (k w)", p=P, c=16)
    with ExitStack() as ph:
        dst = B.sb("dst", [EP, EC], I32, ph)
        t_i = B.sb("t_i", [EP, EC], I32, ph)
        buk = B.sb("buk", [EP, EC], F32, ph)
        mask = B.sb("mask", [EP, NBUK, EC], U8, ph)
        cnt = B.sb("cnt", [EP, NBUK], F32, ph)
        off = B.sb("off", [EP, NBUK], F32, ph)
        sl_i = B.sb("sl_i", [P, NBUK], I32, ph)
        sl = B.sb("sl", [P, NBUK], F32, ph)
        ends = B.sb("ends", [P, NBUK], F32, ph)
        zero = B.sb("zero", [P, EC], F32, ph)
        cum = B.sb("cum", [EP, 2, EC], F32, ph)
        c0 = B.sb("c0", [EP, 2], F32, ph)
        posf = B.sb("posf", [EP, EC], F32, ph)
        cmp = B.sb("cmp", [P, NBUK], F32, ph)
        sb_f = B.sb("sb_f", [P, 4], F32, ph)
        sb_i = B.sb("sb_i", [P, 4], I32, ph)
        img = B.sb("img", [P, max(MSLOTS // 10, SLOTS // 16), REC], F32, ph)
        rest = B.sb("rest", [EP, EC], F32, ph)
        delta = B.sb("delta", [EP, NBUK], F32, ph)
        pre = B.ps("pre", [P, 2, P], ph)
        block = ph.enter_context(nc.Block())

        @block.sync
        def _(sp):
            sp.dma_start(dst[:, :], A["dst"].rearrange("(p j) -> p j", p=EP)).then_inc(s_in, 16)
            sp.wait_ge(s_img, 2)
            for c in range(10):
                sp.dma_start(fill[c], img[:, 0:MSLOTS // 10, :].rearrange("p k w -> p (k w)")).then_inc(s_fill, 16)
            sp.wait_ge(s_bk, 1)
            with nc.allow_non_contiguous_dma(reason="512 words"):
                sp.dma_start(K.bucket_dram.rearrange("(k p) -> p k", p=P), sb_i[:, :]).then_inc(s_out, 16)
            sp.wait_ge(s_out, 16)
            sp.dma_start(K.bucket[:, :], K.bucket_dram.rearrange("(a n) -> a n", a=1)).then_inc(s_ld, 16)
            sp.wait_ge(s_ld, 16)
            sp.wait_ge(s_fill, 160)
            with overflowed(sp, K):
                for c in range(16):
                    sp.dma_start(fill_over[c], img[:, 0:SLOTS // 16, :].rearrange("p k w -> p (k w)")).then_inc(s_fill, 16)
                sp.wait_ge(s_fill, 416)

        @block.gpsimd
        def _(po):
            nc.gpsimd.memset(img[:, :, :], 0.0).then_inc(s_img, 1)
            po.wait_ge(s_img, 1)
            nc.gpsimd.memset(img[:, :, D:D + 1], -1.0).then_inc(s_img, 1)
            nc.gpsimd.memset(posf[:, :], 0.0).then_inc(s_add, 1)
            po.wait_ge(s_add, 1)
            po.sem_inc(s_add, 1)
            with po.Fori(0, NBUK // 2) as h:
                for g in range(2):
                    po.wait_ge(s_msk, h * 2 + g + 1)
                    nc.gpsimd.tensor_tensor(posf[:, :], posf[:, :], cum[:, g, :], ALU.add).then_inc(s_add, 1)
                    po.wait_ge(s_add, h * 2 + g + 3)

        @block.vector
        def _(ve):
            link = Chain(ve, s_v)
            link(nc.vector.memset(zero[:, :], 0.0))
            ve.wait_ge(s_in, 16)
            link(nc.vector.tensor_scalar(t_i[:, :], dst[:, :], 5, None, ALU.arith_shift_right))
            link(nc.vector.tensor_copy(buk[:, :], t_i[:, :]))
            link(nc.vector.tensor_scalar(t_i[:, :], dst[:, :], BN - 1, None, ALU.bitwise_and))
            link(nc.vector.tensor_copy(K.dl[:, :], t_i[:, :]))
            link(nc.vector.tensor_tensor(mask[:, :, :], bc(buk[:, :].unsqueeze(1), [EP, NBUK, EC]),
                                         bc(K.iota[0:EP, 0:NBUK].unsqueeze(2), [EP, NBUK, EC]), ALU.is_equal))
            nc.vector.tensor_reduce(cnt[:, :], mask[:, :, :], AX.X, ALU.add).then_inc(s_cnt, 1)
            ve.wait_ge(s_pre, 1)
            link(nc.vector.tensor_copy(off[:, :], pre[0:EP, 0, 0:NBUK]))
            link(nc.vector.tensor_scalar(cmp[:, :], pre[:, 1, 0:NBUK], -float(CAP), 0.0, ALU.add, ALU.max))
            link(nc.vector.tensor_scalar(cmp[:, :], cmp[:, :], float(P - 1), None, ALU.add))
            link(nc.vector.tensor_copy(sl_i[:, :], cmp[:, :]))
            link(nc.vector.tensor_scalar(sl_i[:, :], sl_i[:, :], 7, None, ALU.arith_shift_right))
            link(nc.vector.tensor_copy(sl[:, :], sl_i[:, :]))
            link(nc.vector.tensor_tensor_scan(ends[:, :], sl[:, :], zero[:, 0:NBUK], 0.0, ALU.add, ALU.add))
            link(nc.vector.tensor_tensor(sl[:, :], ends[:, :], sl[:, :], ALU.subtract))
            link(nc.vector.tensor_scalar(sl[:, :], sl[:, :], float(P), float(OVER - CAP), ALU.mult, ALU.add))
            link(nc.vector.scalar_tensor_tensor(out=delta[:, :], in0=K.iota[0:EP, 0:NBUK], scalar=-float(CAP),
                                                in1=sl[0:EP, :], op0=ALU.mult, op1=ALU.add))
            for k in range(4):
                link(nc.vector.tensor_scalar(cmp[:, :], ends[:, :], K.slotid[:, k:k + 1], None, ALU.is_le))
                link(nc.vector.tensor_reduce(sb_f[:, k:k + 1], cmp[:, :], AX.X, ALU.add))
            link(nc.vector.tensor_scalar(sb_f[:, :], sb_f[:, :], float(NBUK - 1), None, ALU.min))
            link(nc.vector.tensor_copy(K.over[:, :], ends[0:1, NBUK - 1:NBUK]))
            nc.vector.tensor_copy(sb_i[:, :], sb_f[:, :]).then_inc(s_bk, 1)
            base = link.k
            with ve.Fori(0, NBUK // 2) as h:
                l2 = Chain(ve, s_v, h * 2 + base)
                for g in range(2):
                    m = mask[:, bass.ds(h * 2 + g, 1), :].rearrange("p a j -> p (a j)")
                    ve.wait_ge(s_add, h * 2 + g + 1)
                    l2(nc.vector.tensor_tensor_scan(cum[:, g, :], m, zero[0:EP, :], off[:, bass.ds(h * 2 + g, 1)],
                                                    ALU.add, ALU.add))
                    nc.vector.tensor_tensor(cum[:, g, :], cum[:, g, :], m, ALU.mult).then_inc(s_msk, 1)
                assert l2.k == 2
            base += NBUK
            ve.wait_ge(s_add, NBUK + 2)
            link = Chain(ve, s_v, base)
            link(nc.vector.tensor_scalar(posf[:, :], posf[:, :], -1.0, None, ALU.add))
            link(nc.vector.tensor_scalar(buk[:, :], buk[:, :], float(CAP), None, ALU.mult))
            link(nc.vector.tensor_tensor(buk[:, :], buk[:, :], posf[:, :], ALU.add))
            base += 3
            with overflowed(ve, K):
                l2 = Chain(ve, s_v, base)
                l2(nc.vector.memset(rest[:, :], 0.0))
                with ve.Fori(0, NBUK // 2) as h:
                    l3 = Chain(ve, s_v, h * 6 + (base + 1))
                    for g in range(2):
                        m = mask[:, bass.ds(h * 2 + g, 1), :].rearrange("p a j -> p (a j)")
                        l3(nc.vector.tensor_copy(c0[:, g:g + 1], delta[:, bass.ds(h * 2 + g, 1)]))
                        l3(nc.vector.tensor_scalar(cum[:, g, :], m, c0[:, g:g + 1], None, ALU.mult))
                        l3(nc.vector.tensor_tensor(rest[:, :], rest[:, :], cum[:, g, :], ALU.add))
                    assert l3.k == 6
                l2 = Chain(ve, s_v, base + 1 + 3 * NBUK)
                l2(nc.vector.tensor_scalar(posf[:, :], posf[:, :], float(CAP), None, ALU.is_ge))
                l2(nc.vector.tensor_tensor(rest[:, :], rest[:, :], posf[:, :], ALU.mult))
                l2(nc.vector.tensor_tensor(buk[:, :], buk[:, :], rest[:, :], ALU.add))
            nc.vector.tensor_copy(K.pos[:, :], buk[:, :]).then_inc(s_cp, 1)

        @block.tensor
        def _(pe):
            pe.wait_ge(s_cnt, 1)
            nc.tensor.matmul(pre[0:EP, 0, 0:NBUK], K.tri[0:EP, 0:EP], cnt[:, :], start=True, stop=True)
            nc.tensor.matmul(pre[:, 1, 0:NBUK], K.ones[0:EP, :], cnt[:, :], start=True, stop=True).then_inc(s_pre, 1)


@phase
def scatter_records(nc, B, A, K):
    W = 8
    STEPS = EC // W
    s_in, s_meta, s_free = B.sem("meta_loaded"), B.sem("meta_made"), B.sem("stage_free")
    s_attr = [B.sem("attr_staged") for _ in range(2)]
    s_stage = B.sem("meta_staged")
    s_done = [B.sem("rows_scattered") for _ in range(2)]
    s_go = B.sem("pool_go")
    with ExitStack() as ph:
        src = B.sb("src", [EP, EC], I32, ph)
        a4 = B.sb("a4", [EP, EC, 4], F32, ph)
        a16 = B.sb("a16", [EP, EC, 16], F32, ph)
        meta = B.sb("meta", [EP, EC, META], F32, ph)
        stage = B.sb("stage", [EP, 2, W, REC], F32, ph)
        idx = B.sb("idx", [EP, 2, W], I32, ph)
        block = ph.enter_context(nc.Block())
        attr = A["edge_attr_128"].rearrange("(p j) d -> p j d", p=EP)

        @block.sync
        def _(sp):
            sp.dma_start(src[:, :], A["src"].rearrange("(p j) -> p j", p=EP)).then_inc(s_in, 16)
            sp.dma_start(a4[:, :, :], A["edge_attr_4"].rearrange("(p j) k -> p j k", p=EP)).then_inc(s_in, 16)
            sp.dma_start(a16[:, :, :], A["edge_attr_16"].rearrange("(p j) k -> p j k", p=EP)).then_inc(s_in, 16)
            with sp.Fori(0, STEPS // 2) as i:
                for g in range(2):
                    sp.wait_ge(s_free, i * 2 + g + 1)
                    sp.dma_start(stage[:, g, :, 0:D], attr[:, bass.ds(i * (2 * W) + g * W, W), :]).then_inc(s_attr[g], 16)

        @block.gpsimd
        def _(po):
            with po.Fori(0, STEPS // 2) as i:
                for g in range(2):
                    po.wait_ge(s_attr[g], i * 16 + 16)
                    po.wait_ge(s_stage, i * 2 + g + 1)
                    po.sem_inc(s_go, 1)
                    for k in range(W):
                        nc.gpsimd.indirect_dma_start(
                            out=K.rec, out_offset=bass.IndirectOffsetOnAxis(ap=idx[:, g, k:k + 1], axis=0),
                            in_=stage[:, g, k, :], in_offset=None).then_inc(s_done[g], 16)

        @block.scalar
        def _(ac):
            ac.wait_ge(s_meta, 5)
            with ac.Fori(0, STEPS // 2) as i:
                for g in range(2):
                    ac.wait_ge(s_free, i * 2 + g + 1)
                    j = i * (2 * W) + g * W
                    nc.scalar.copy(stage[:, g, :, D:REC], meta[:, bass.ds(j, W), :])
                    nc.scalar.copy(idx[:, g, :], K.pos[:, bass.ds(j, W)]).then_inc(s_stage, 1)

        @block.vector
        def _(ve):
            nc.vector.memset(meta[:, :, 1:2], 1.0).then_inc(s_meta, 1)
            nc.vector.tensor_copy(meta[:, :, 0:1], K.dl[:, :].unsqueeze(2)).then_inc(s_meta, 1)
            nc.vector.memset(meta[:, :, 23:24], 0.0)
            ve.wait_ge(s_in, 48)
            nc.vector.tensor_copy(meta[:, :, 2:6], a4[:, :, :]).then_inc(s_meta, 1)
            nc.vector.tensor_copy(meta[:, :, 6:22], a16[:, :, :]).then_inc(s_meta, 1)
            nc.vector.tensor_copy(meta[:, :, 22:23].bitcast(I32), src[:, :].unsqueeze(2)).then_inc(s_meta, 1)
            ve.sem_inc(s_free, 2)
            with ve.Fori(0, STEPS // 2) as i:
                for g in range(2):
                    ve.wait_ge(s_done[g], i * (16 * W) + 16 * W)
                    ve.sem_inc(s_free, 1)


@phase
def make_operands(nc, B, A, K, reg):
    G, ng = reg.slots, reg.groups
    cols = G * P
    s_rec = [B.sem("meta_read") for _ in range(2)]
    s_tr, s_row, s_dlb, s_spr = B.sem("transposed"), B.sem("rows_copied"), B.sem("dst_rounded"), B.sem("dst_spread")
    s_t, s_tb = B.sem("onehot_rows_made"), B.sem("onehot_rows_rounded")
    s_st = [B.sem("operand_stored") for _ in range(2)]
    s_src, s_dl, s_so, s_z = B.sem("sources_kept"), B.sem("dst_kept"), B.sem("sources_stored"), B.sem("rows_zeroed")
    with ExitStack() as ph:
        rec = B.sb("rec", [P, 2, G, META], F32, ph)
        T = B.sb("T", [TR, 2, cols], F32, ph)
        Tb = B.sb("Tb", [64, 2, cols], BF16, ph)
        srcs = B.sb("srcs", [P, ng * G], I32, ph)
        dlb = B.sb("dlb", [P, 2, G], BF16, ph)
        ps_t = B.ps("ps_t", [META, -(-G // 4) * 512], ph)
        ps_d = B.ps("ps_d", [64, -(-G // 4) * 512], ph)
        block = ph.enter_context(nc.Block())
        stored = 32

        def guard(eng):
            return overflowed(eng, K) if reg.over else ExitStack()

        def past(n, back):
            return not isinstance(n, int) or n >= back

        @block.sync
        def _(sp):
            def load(n, g, r):
                if past(n, 2):
                    sp.wait_ge(s_row, n - 1)
                    sp.wait_ge(s_src, n - 1)
                    sp.wait_ge(s_dl, n - 1)
                sp.dma_start(rec[:, g, :, :], reg.rec[:, span(n, G), D:REC]).then_inc(s_rec[g], 16)

            with guard(sp):
                in_pairs(sp, ng, load)
                sp.wait_ge(s_src, ng)
                sp.dma_start(reg.src, srcs[:, :]).then_inc(s_so, 16)
                sp.wait_ge(s_so, 16)

        @block.tensor
        def _(pe):
            def step(n, g, r):
                pe.wait_ge(s_dlb, n + 1)
                if past(n, 1):
                    pe.wait_ge(s_t, n)
                for k in range(G):
                    m = nc.tensor.matmul(ps_d[:, k * P:(k + 1) * P], bc(dlb[:, g, k:k + 1], [P, 64]),
                                         K.identb[:, :], start=True, stop=True, skip_group_check=True)
                m.then_inc(s_spr, 1)
                if past(n, 1):
                    pe.wait_ge(s_row, n)
                for k in range(G):
                    m = nc.tensor.transpose(ps_t[:, k * P:(k + 1) * P], rec[:, g, k, :], K.ident[:, :])
                m.then_inc(s_tr, 1)

            with guard(pe):
                in_pairs(pe, ng, step)

        @block.scalar
        def _(ac):
            def step(n, g, r):
                if past(n, 2):
                    ac.wait_ge(s_st[g], r * stored)
                ac.wait_ge(s_tr, n + 1)
                nc.scalar.copy(T[64:64 + META, g, :], ps_t[:, 0:cols]).then_inc(s_row, 1)
                ac.wait_ge(s_t, n + 1)
                nc.scalar.copy(Tb[:, g, :], T[0:64, g, :]).then_inc(s_tb, 1)
                ac.wait_ge(s_row, n + 1)
                ac.dma_start(reg.t[span(n, 1), :, :].rearrange("a r c -> (a r) c"), T[:, g, :]).then_inc(s_st[g], 16)
                ac.wait_ge(s_tb, n + 1)
                ac.dma_start(reg.tb[span(n, 1), :, :].rearrange("a r c -> (a r) c"), Tb[:, g, :]).then_inc(s_st[g], 16)

            with guard(ac):
                ac.wait_ge(s_z, 1)
                in_pairs(ac, ng, step)
                for g in range(2):
                    ac.wait_ge(s_st[g], ng // 2 * stored)

        @block.vector
        def _(ve):
            def step(n, g, r):
                ve.wait_ge(s_rec[g], r * 16 + 16)
                nc.vector.tensor_copy(dlb[:, g, :], rec[:, g, :, 0:1].rearrange("p s a -> p (s a)")).then_inc(s_dlb, 1)
                nc.vector.tensor_copy(srcs[:, span(n, G)],
                                      rec[:, g, :, 22:23].bitcast(I32).rearrange("p s a -> p (s a)")).then_inc(s_src, 1)
                nc.vector.tensor_copy(reg.dls[:, span(n, G)],
                                      rec[:, g, :, 0:1].rearrange("p s a -> p (s a)")).then_inc(s_dl, 1)
                if past(n, 2):
                    ve.wait_ge(s_st[g], r * stored)
                ve.wait_ge(s_spr, n + 1)
                nc.vector.tensor_scalar(T[0:64, g, :], ps_d[:, 0:cols], K.eqm[:, :], K.eqc[:, :],
                                        ALU.is_equal, ALU.subtract).then_inc(s_t, 1)

            with guard(ve):
                nc.vector.memset(T[:, :, :], 0.0).then_inc(s_z, 1)
                ve.wait_ge(s_z, 1)
                in_pairs(ve, ng, step)



@phase
def load_x(nc, B, A, K):
    s_in, s_z, s_tr, s_cp = B.sem("x_loaded"), B.sem("x_padded"), B.sem("x_transposed"), B.sem("x_copied")
    with ExitStack() as ph:
        xn = B.sb("xn", [P, TILES, D], F32, ph)
        ps = [B.ps("ps", [P, P], ph) for _ in range(2)]
        block = ph.enter_context(nc.Block())
        full, rest = N // P, N % P

        @block.sync
        def _(sp):
            sp.dma_start(xn[:, 0:full, :], A["x"][0:full * P, :].rearrange("(t p) d -> p t d", p=P)).then_inc(s_in, 16)
            sp.wait_ge(s_z, 1)
            sp.dma_start(xn[0:rest, full, :], A["x"][full * P:N, :]).then_inc(s_in, 16)

        @block.tensor
        def _(pe):
            pe.wait_ge(s_in, 32)
            for t in range(TILES):
                if t >= 2:
                    pe.wait_ge(s_cp, t - 1)
                nc.tensor.transpose(ps[t % 2][:, :], xn[:, t, :], K.ident[:, :]).then_inc(s_tr, 1)

        @block.vector
        def _(ve):
            nc.vector.memset(xn[:, full, :], 0.0).then_inc(s_z, 1)
            for t in range(TILES):
                ve.wait_ge(s_tr, t + 1)
                nc.vector.tensor_copy(K.X[:, t * P:(t + 1) * P], ps[t % 2][:, :]).then_inc(s_cp, 1)


@phase
def norm_nodes(nc, B, A, K):
    s_tr, s_xc, s_v, s_sd = B.sem("x_transposed"), B.sem("x_copied"), B.sem("stat_chain"), B.sem("deviations")
    s_sq, s_h, s_hb, s_hc = B.sem("roots"), B.sem("normed"), B.sem("h_transposed"), B.sem("h_copied")
    with ExitStack() as ph:
        xn = B.sb("xn", [P, TILES, D], F32, ph)
        st = B.sb("st", [P, TILES, 6], F32, ph)
        mv = B.sb("mv", [P, TILES, 2], F32, ph)
        sd = B.sb("sd", [P, TILES], F32, ph)
        nb = B.sb("nb", [P, TILES], F32, ph)
        psx = [B.ps("psx", [P, P], ph) for _ in range(2)]
        psh = [B.ps("psh", [P, P], ph) for _ in range(2)]
        block = ph.enter_context(nc.Block())

        @block.tensor
        def _(pe):
            for t in range(TILES):
                if t >= 2:
                    pe.wait_ge(s_xc, t - 1)
                nc.tensor.transpose(psx[t % 2][:, :], K.X[:, t * P:(t + 1) * P], K.ident[:, :]).then_inc(s_tr, 1)
            for t in range(TILES):
                pe.wait_ge(s_h, t + 1)
                if t >= 2:
                    pe.wait_ge(s_hc, t - 1)
                nc.tensor.transpose(psh[t % 2][:, :], xn[:, t, :], K.ident[:, :]).then_inc(s_hb, 1)

        @block.vector
        def _(ve):
            link = Chain(ve, s_v)
            for t in range(TILES):
                ve.wait_ge(s_tr, t + 1)
                nc.vector.tensor_copy(xn[:, t, :], psx[t % 2][:, :]).then_inc(s_xc, 1)
                ve.wait_ge(s_xc, t + 1)
                link(nc.vector.bn_stats(st[:, t, :], xn[:, t, :]))
                link(nc.vector.bn_aggr(mv[:, t, :], st[:, t, :]))
            nc.vector.tensor_scalar(sd[:, :], mv[:, :, 1], EPS, None, ALU.add).then_inc(s_sd, 1)
            ve.wait_ge(s_sq, 1)
            link(nc.vector.reciprocal(sd[:, :], sd[:, :]))
            nc.vector.scalar_tensor_tensor(out=nb[:, :], in0=mv[:, :, 0], scalar=-1.0, in1=sd[:, :],
                                           op0=ALU.mult, op1=ALU.mult).then_inc(s_sd, 1)
            for t in range(TILES):
                ve.wait_ge(s_hb, t + 1)
                nc.vector.tensor_copy(K.H[:, t * P:(t + 1) * P], psh[t % 2][:, :]).then_inc(s_hc, 1)

        @block.scalar
        def _(ac):
            ac.wait_ge(s_sd, 1)
            nc.scalar.activation(sd[:, :], sd[:, :], ACT.Sqrt).then_inc(s_sq, 1)
            ac.wait_ge(s_sd, 2)
            for t in range(TILES):
                nc.scalar.activation(xn[:, t, :], xn[:, t, :], ACT.Relu, bias=nb[:, t:t + 1],
                                     scale=sd[:, t:t + 1]).then_inc(s_h, 1)


@phase
def project_nodes(nc, B, K, pairs, width, table, row=None, scale=1.0):
    s_mm, s_cp, s_st = B.sem("projected"), B.sem("row_copied"), B.sem("table_stored")
    with ExitStack() as ph:
        out = B.sb("out", [P, TILES, width], F32, ph)
        ps = [B.ps("ps", [P, 512], ph) for _ in range(2)]
        block = ph.enter_context(nc.Block())

        @block.tensor
        def _(pe):
            for t in range(TILES):
                if t >= 2:
                    pe.wait_ge(s_cp, t - 1)
                for j, (x, ws) in enumerate(pairs):
                    at = 0
                    for w in ws:
                        n = w.shape[1]
                        m = nc.tensor.matmul(ps[t % 2][:, at:at + n], x[:, t * P:(t + 1) * P], w,
                                             start=j == 0, stop=j == len(pairs) - 1, skip_group_check=True)
                        at += n
                m.then_inc(s_mm, 1)

        @block.vector
        def _(ve):
            for t in range(TILES):
                ve.wait_ge(s_mm, t + 1)
                if row is None:
                    nc.vector.tensor_copy(out[:, t, :], ps[t % 2][:, 0:width]).then_inc(s_cp, 1)
                else:
                    for j, r in enumerate(row):
                        m = nc.vector.scalar_tensor_tensor(
                            out=out[:, t, j * D:(j + 1) * D], in0=ps[t % 2][:, j * D:(j + 1) * D], scalar=scale,
                            in1=r, op0=ALU.mult, op1=ALU.add)
                    m.then_inc(s_cp, 1)

        @block.sync
        def _(sp):
            sp.wait_ge(s_cp, TILES)
            sp.dma_start(table.rearrange("(t p) w -> p t w", p=P), out[:, :, :]).then_inc(s_st, 16)
            sp.wait_ge(s_st, 16)


@phase
def feature_product(nc, B, K, pairs, consume, steps, act=None):
    s_mm, s_v = B.sem("chunk_product"), B.sem("chunk_chain")
    with ExitStack() as ph:
        ps = [B.ps("ps", [P, 512], ph) for _ in range(2)]
        block = ph.enter_context(nc.Block())

        @block.tensor
        def _(pe):
            for c in range(NCH):
                if c >= 2:
                    pe.wait_ge(s_v, steps * (c - 1))
                for j, (w, x) in enumerate(pairs):
                    m = nc.tensor.matmul(ps[c % 2][:, 0:CH], w, x[:, c * CH:(c + 1) * CH],
                                         start=j == 0, stop=j == len(pairs) - 1)
                m.then_inc(s_mm, 1)

        @block.vector
        def _(ve):
            link = Chain(ve, s_v)
            for c in range(NCH):
                ve.wait_ge(s_mm, c + 1)
                consume(slice(c * CH, (c + 1) * CH), ps[c % 2][:, 0:CH], link)
                assert link.k == steps * (c + 1)


@phase
def group_norm(nc, B, K, X, gamma, beta, func, Y):
    s_mm, s_c, s_sq = B.sem("group_mean"), B.sem("centred"), B.sem("squared")
    s_var, s_rt, s_v, s_n, s_y = B.sem("group_var"), B.sem("root"), B.sem("norm_chain"), B.sem("normed"), B.sem("written")
    with ExitStack() as ph:
        sq = B.sb("sq", [P, 2, CH], F32, ph)
        rs = B.sb("rs", [P, 2, CH], F32, ph)
        ps = [B.ps("ps", [P, 512], ph) for _ in range(2)]
        pv = [B.ps("pv", [P, 512], ph) for _ in range(2)]
        block = ph.enter_context(nc.Block())

        @block.tensor
        def _(pe):
            for c in range(NCH):
                sl = slice(c * CH, (c + 1) * CH)
                if c >= 2:
                    pe.wait_ge(s_c, c - 1)
                nc.tensor.matmul(ps[c % 2][:, 0:CH], K.gmean[:, :], X[:, sl], start=True, stop=True).then_inc(s_mm, 1)
                pe.wait_ge(s_sq, c + 1)
                nc.tensor.matmul(pv[c % 2][:, 0:CH], K.gmean[:, :], sq[:, c % 2, :], start=True, stop=True).then_inc(s_var, 1)

        @block.scalar
        def _(ac):
            for c in range(NCH):
                sl = slice(c * CH, (c + 1) * CH)
                ac.wait_ge(s_c, c + 1)
                nc.scalar.activation(sq[:, c % 2, :], X[:, sl], ACT.Square).then_inc(s_sq, 1)
                ac.wait_ge(s_v, 3 * c + 1)
                nc.scalar.activation(rs[:, c % 2, :], rs[:, c % 2, :], ACT.Sqrt).then_inc(s_rt, 1)
            for c in range(NCH):
                sl = slice(c * CH, (c + 1) * CH)
                ac.wait_ge(s_v, 3 * c + 3)
                nc.scalar.activation(Y[:, sl], X[:, sl], func, bias=beta[:, :], scale=gamma[:, :]).then_inc(s_y, 1)

        @block.vector
        def _(ve):
            link = Chain(ve, s_v)
            for c in range(NCH):
                sl = slice(c * CH, (c + 1) * CH)
                ve.wait_ge(s_mm, c + 1)
                nc.vector.tensor_tensor(X[:, sl], X[:, sl], ps[c % 2][:, 0:CH], ALU.subtract).then_inc(s_c, 1)
                ve.wait_ge(s_var, c + 1)
                link(nc.vector.tensor_scalar(rs[:, c % 2, :], pv[c % 2][:, 0:CH], EPS, None, ALU.add))
                ve.wait_ge(s_rt, c + 1)
                link(nc.vector.reciprocal(rs[:, c % 2, :], rs[:, c % 2, :]))
                link(nc.vector.tensor_tensor(X[:, sl], X[:, sl], rs[:, c % 2, :], ALU.mult))


@phase
def vector_phase(nc, B, body):
    s_v = B.sem("vector_chain")
    with ExitStack() as ph:
        block = ph.enter_context(nc.Block())

        @block.vector
        def _(ve):
            body(Chain(ve, s_v))


@phase
def load_table(nc, B, table, tab, static, first):
    s, s_st, s_z = B.sem("table_loaded"), B.sem("static_copied"), B.sem("complement_zeroed")
    half = NB // 2
    c0, c1 = (0, D) if static.shape[1] == D else (D, D + 8)
    with ExitStack() as ph:
        block = ph.enter_context(nc.Block())

        @block.sync
        def _(sp):
            sp.dma_start(tab[0:BN, :, 0:D], table.rearrange("(b p) d -> p b d", p=BN)).then_inc(s, 16)
            sp.wait_ge(s, 16)

        @block.vector
        def _(ve):
            if first:
                nc.vector.memset(tab[BN:64, :, :], 0.0).then_inc(s_z, 1)
                ve.wait_ge(s_z, 1)
            if c0:
                nc.vector.memset(tab[64:TR, :, 0:D], 0.0).then_inc(s_st, 1)
                nc.vector.memset(tab[0:BN, :, D:D + 8], 0.0).then_inc(s_st, 1)
            nc.vector.tensor_copy(tab[64:TR, 0:half, c0:c1], bc(static[64:TR, :].unsqueeze(1), [TR - 64, half, c1 - c0])).then_inc(s_st, 1)
            ve.wait_ge(s_st, (2 if c0 else 0) + 2)

        @block.scalar
        def _(ac):
            for b in range(half, NB, 10):
                o = nc.scalar.copy(tab[64:TR, b:b + 10, c0:c1], bc(static[64:TR, :].unsqueeze(1), [TR - 64, 10, c1 - c0]))
            o.then_inc(s_st, 1)



@phase
def overflow_pass(nc, B, K, kind, gather=None, gw=0, linear=None, lw=0, store=None, tab=None, tw=0, ts=0,
              static=None, gcol=None, btcol=None, MX=None, heads=0, LG=None, targets=None):
    uses_T = kind not in ("sum", "attr")
    is_max = kind in ("gatmax", "logits")
    NS = 2 if kind in ("gat", "attr", "attn") else 1
    HG = heads // 4 if heads else 0
    W = gw or lw
    s_idx = [B.sem("indices_read") for _ in range(RING)]
    s_t = [B.sem("operand_read") for _ in range(RING)]
    s_rows = [B.sem("rows_arrived") for _ in range(RING)]
    s_kept = [B.sem("rows_kept") for _ in range(RING)]
    s_lg = [B.sem("logits_moved") for _ in range(RING)]
    s_free, s_go = B.sem("group_done"), B.sem("pool_go")
    s_exp, s_v, s_val = B.sem("expanded"), B.sem("vector_chain"), B.sem("value_ready")
    s_act, s_sum, s_lk, s_z = B.sem("activated"), B.sem("summed"), B.sem("logits_kept"), B.sem("acc_zeroed")
    row_incs = 64 if gw else 16
    with ExitStack() as ph:
        rows = B.sb("rows", [P, RING, GS, W], F32, ph)
        idx = B.sb("idx", [P, RING, GS], I32, ph) if gw else None
        T = B.sb("T", [TR, RING, GS * P], F32, ph) if uses_T else None
        lg = B.sb("lg", [P, RING, GS, 8], F32, ph) if kind == "attn" else None
        oh = B.sb("oh", [P, GS, BN], F32, ph)
        m = B.sb("m", [P, GS, D], F32, ph)
        sq = B.sb("sq", [P, GS, D], F32, ph)
        w = B.sb("w", [P, GS, 8], F32, ph)
        z = B.sb("z", [P, GS, 8], F32, ph)
        y = B.sb("y", [P, 4, GS * 8], F32, ph)
        mx = B.sb("mx", [P, 2, GS], F32, ph)
        pe1 = B.ps("expanded", [P, GS, D], ph)
        pl = B.ps("edge_logits", [P, GS, 8], ph)
        pt = B.ps("logits_T", [heads, GS * P], ph) if is_max else None
        wT = B.sb("wT", [heads, GS * P], F32, ph) if is_max else None
        s_tt, s_tc = B.sem("logits_transposed"), B.sem("logits_copied")
        pm = [B.ps("spread", [P, GS, P], ph) for _ in range(2)] if is_max else None
        psum = B.ps("sums", [P, GS, 2, BN], ph)
        block = ph.enter_context(nc.Block())
        hv = {"gat": (4, 32), "attn": (8, 16)}.get(kind)

        @block.sync
        def _(sp):
            with overflowed(sp, K):
                with sp.Fori(0, TRIPS) as i:
                    for g in range(RING):
                        n = i * RING + g
                        sp.wait_ge(s_free, n + 1)
                        if gw:
                            sp.dma_start(idx[:, g, :], K.reg_o.src[:, bass.ds(n * GS, GS)]).then_inc(s_idx[g], 16)
                        else:
                            sp.dma_start(rows[:, g, :, :], linear[:, bass.ds(n * GS, GS), 0:W]).then_inc(s_rows[g], 16)
                        if kind == "attn":
                            sp.dma_start(lg[:, g, :, :], LG[:, bass.ds(n * GS, GS), :]).then_inc(s_lg[g], 16)
                        if uses_T:
                            sp.dma_start(T[:, g, :], K.reg_o.t[bass.ds(n, 1), :, :].rearrange("a r c -> (a r) c")).then_inc(s_t[g], 16)

        if gw:
            @block.gpsimd
            def _(po):
                with overflowed(po, K):
                    with po.Fori(0, TRIPS) as i:
                        for g in range(RING):
                            po.wait_ge(s_idx[g], i * 16 + 16)
                            po.sem_inc(s_go, 1)
                            for k in range(GS):
                                nc.gpsimd.indirect_dma_start(
                                    out=rows[:, g, k, :], out_offset=None, in_=gather,
                                    in_offset=bass.IndirectOffsetOnAxis(ap=idx[:, g, k:k + 1], axis=0)).then_inc(s_rows[g], 16)

        @block.tensor
        def _(pe):
            with overflowed(pe, K):
                with pe.Fori(0, TRIPS) as i:
                    for g in range(RING):
                        n = i * RING + g

                        def bucket(k):
                            return pe.value_load(K.bucket[0:1, bass.ds(n * GS + k, 1)], min_val=0, max_val=NBUK - 1)

                        if uses_T:
                            pe.wait_ge(s_t[g], i * 16 + 16)
                        if kind in ("gat", "attn", "conv", "logits"):
                            wd = tw
                            for k in range(GS):
                                v = bucket(k)
                                o = pe1[:, k, 0:wd] if wd == D else pl[:, k, 0:wd]
                                mm = nc.tensor.matmul(o, T[0:BN, g, k * P:(k + 1) * P], tab[0:BN, bass.ds(v * ts, wd)],
                                                      start=True, stop=kind != "conv", skip_group_check=True)
                                if kind == "conv":
                                    mm = nc.tensor.matmul(o, T[:, g, k * P:(k + 1) * P], static[:, :], start=False,
                                                          stop=True, skip_group_check=True)
                                if kind == "logits":
                                    mm = nc.tensor.matmul(pl[:, k, :], T[:, g, k * P:(k + 1) * P], static[:, :],
                                                          start=True, stop=True, skip_group_check=True)
                            mm.then_inc(s_exp, 1)
                        if kind == "prod":
                            for k in range(GS):
                                mm = nc.tensor.matmul(pe1[:, k, :], T[:, g, k * P:(k + 1) * P], static[:, :],
                                                      start=True, stop=True, skip_group_check=True)
                            mm.then_inc(s_exp, 1)
                        if is_max:
                            if kind == "gatmax":
                                pe.wait_ge(s_rows[g], i * row_incs + row_incs)
                                pe.wait_ge(s_free, n + RING)
                            else:
                                pe.wait_ge(s_val, n + 1)
                            for k in range(GS):
                                a = rows[:, g, k, D:D + 4] if kind == "gatmax" else w[:, k, :]
                                mm = nc.tensor.transpose(pt[:, k * P:(k + 1) * P], a, K.ident[:, :])
                            mm.then_inc(s_tt, 1)
                            pe.wait_ge(s_tc, n + 1)
                            for hg in range(HG):
                                nc.tensor.matmul(pm[hg][:, :, :].rearrange("p k e -> p (k e)"),
                                                 K.neg[:, :, :].rearrange("p h n -> p (h n)"), T[:, g, :],
                                                 start=True, stop=False)
                                mm = nc.tensor.matmul(pm[hg][:, :, :].rearrange("p k e -> p (k e)"),
                                                      K.hs32[0:heads, hg, :], wT[:, :], start=False, stop=True)
                            mm.then_inc(s_sum, 1)
                        else:
                            if kind in ("sum", "attr"):
                                pe.wait_ge(s_rows[g], i * row_incs + row_incs)
                            pe.wait_ge(s_val, n + 1)
                            for k in range(GS):
                                src = rows[:, g, k, 0:D] if kind in ("sum", "attr") else m[:, k, :]
                                mm = nc.tensor.matmul(psum[:, k, 0, :], src, oh[:, k, :], start=True, stop=True,
                                                      skip_group_check=True)
                                if NS == 2:
                                    second = K.ones[:, :] if kind == "attr" else w[:, k, 0:hv[0]]
                                    mm = nc.tensor.matmul(psum[0:second.shape[1], k, 1, :], second, oh[:, k, :], start=True, stop=True,
                                                          skip_group_check=True)
                            mm.then_inc(s_sum, 1)

        @block.scalar
        def _(ac):
            with overflowed(ac, K):
                with ac.Fori(0, TRIPS) as i:
                    for g in range(RING):
                        n = i * RING + g
                        if store is not None:
                            ac.wait_ge(s_rows[g], i * row_incs + row_incs)
                            s0, s1, dram = store
                            ac.dma_start(dram[:, bass.ds(n * GS, GS), :], rows[:, g, :, s0:s1]).then_inc(s_kept[g], 16)
                        if kind in ("gat", "attn"):
                            ac.wait_ge(s_lk, n + 1)
                            nc.scalar.activation(w[:, :, 0:hv[0]], z[:, :, 0:hv[0]], ACT.Exp).then_inc(s_act, 1)
                        if kind == "conv":
                            ac.wait_ge(s_lk, 2 * n + 1)
                            nc.scalar.activation(sq[:, :, :], m[:, :, :], ACT.Square).then_inc(s_act, 1)
                            ac.wait_ge(s_lk, 2 * n + 2)
                            nc.scalar.activation(m[:, :, :], sq[:, :, :], ACT.Silu).then_inc(s_act, 1)
                        if is_max:
                            ac.wait_ge(s_tt, n + 1)
                            nc.scalar.copy(wT[:, :], pt[:, :]).then_inc(s_tc, 1)
                        if kind == "logits":
                            ac.wait_ge(s_val, n + 1)
                            ac.dma_start(LG[:, bass.ds(n * GS, GS), :], w[:, :, :]).then_inc(s_lg[g], 16)

        per = {"gatmax": 5, "gat": 7, "sum": 4, "attr": 8, "conv": 19, "logits": 7, "attn": 4, "prod": 4}[kind]

        @block.vector
        def _(ve):
            with overflowed(ve, K):
                nc.vector.memset(psum[:, :, :, :], 0.0).then_inc(s_z, 1)
                ve.wait_ge(s_z, 1)
                ve.sem_inc(s_free, RING)
                with ve.Fori(0, TRIPS) as i:
                    link = Chain(ve, s_v, i * (per * RING))
                    for g in range(RING):
                        n = i * RING + g

                        def bucket(k):
                            return ve.value_load(K.bucket[0:1, bass.ds(n * GS + k, 1)], min_val=0, max_val=NBUK - 1)

                        if not is_max:
                            o = nc.vector.tensor_tensor(oh[:, :, :], bc(K.iota[:, 0:BN].unsqueeze(1), [P, GS, BN]),
                                                        bc(K.reg_o.dls[:, bass.ds(n * GS, GS)].unsqueeze(2), [P, GS, BN]),
                                                        ALU.is_equal)
                            if kind in ("sum", "attr"):
                                o.then_inc(s_val, 1)
                        if kind in ("gat", "attn", "conv", "prod", "logits"):
                            ve.wait_ge(s_exp, n + 1)
                        if kind not in ("sum", "attr", "gatmax"):
                            ve.wait_ge(s_rows[g], i * row_incs + row_incs)
                        r = rows[:, g, :, 0:D]
                        if kind == "gat":
                            link(nc.vector.tensor_tensor(w[:, :, 4:8], rows[:, g, :, D:D + 4], pl[:, :, 0:4], ALU.add))
                            link(nc.vector.scalar_tensor_tensor(out=z[:, :, 4:8], in0=w[:, :, 4:8], scalar=0.2,
                                                                in1=w[:, :, 4:8], op0=ALU.mult, op1=ALU.max))
                            link(nc.vector.tensor_tensor(z[:, :, 0:4], z[:, :, 4:8], pl[:, :, 4:8], ALU.subtract))
                            ve.sem_inc(s_lk, 1)
                        if kind == "attn":
                            ve.wait_ge(s_lg[g], i * 16 + 16)
                            nc.vector.tensor_tensor(z[:, :, :], lg[:, g, :, :],
                                                    pl[:, :, :], ALU.subtract).then_inc(s_lk, 1)
                        if kind in ("gat", "attn"):
                            ve.wait_ge(s_act, n + 1)
                            h, f = hv
                            for k in range(GS):
                                mm = nc.vector.tensor_tensor(m[:, k, :].rearrange("p (h f) -> p h f", h=h),
                                                             rows[:, g, k, 0:D].rearrange("p (h f) -> p h f", h=h),
                                                             bc(w[:, k, 0:h].unsqueeze(2), [P, h, f]), ALU.mult)
                            mm.then_inc(s_val, 1)
                        if kind == "prod":
                            nc.vector.tensor_tensor(m[:, :, :], r, pe1[:, :, :], ALU.mult).then_inc(s_val, 1)
                        if kind == "logits":
                            link(nc.vector.tensor_tensor(m[:, :, :], r, pe1[:, :, :], ALU.mult))
                            link(nc.vector.tensor_reduce(z[:, :, :].rearrange("p k h -> p (k h)"),
                                                         m[:, :, :].rearrange("p k (h f) -> p (k h) f", h=8), AX.X, ALU.add))
                            nc.vector.tensor_tensor(w[:, :, :], z[:, :, :], pl[:, :, :], ALU.add).then_inc(s_val, 1)
                        if kind == "conv":
                            nc.vector.tensor_tensor(m[:, :, :], r, pe1[:, :, :], ALU.add).then_inc(s_lk, 1)
                            ve.wait_ge(s_act, 2 * n + 1)
                            link(nc.vector.tensor_reduce(y[:, 0, :], sq[:, :, :].rearrange("p k (h f) -> p (k h) f", h=8),
                                                         AX.X, ALU.add))
                            link(nc.vector.tensor_scalar(y[:, 0, :], y[:, 0, :], 1.0 / 16, EPS, ALU.mult, ALU.add))
                            link(nc.vector.tensor_scalar(y[:, 1, :].bitcast(I32), y[:, 0, :].bitcast(I32), -0.5,
                                                         float(0x5f3759df), ALU.mult, ALU.add))
                            for _ in range(3):
                                link(nc.vector.scalar_tensor_tensor(out=y[:, 2, :], in0=y[:, 1, :], scalar=-0.5,
                                                                    in1=y[:, 0, :], op0=ALU.mult, op1=ALU.mult))
                                link(nc.vector.tensor_tensor(y[:, 2, :], y[:, 2, :], y[:, 1, :], ALU.mult))
                                link(nc.vector.scalar_tensor_tensor(out=y[:, 1, :], in0=y[:, 2, :], scalar=1.5,
                                                                    in1=y[:, 1, :], op0=ALU.add, op1=ALU.mult))
                            link(nc.vector.tensor_tensor(m[:, :, :].rearrange("p k (h f) -> p (k h) f", h=8),
                                                         m[:, :, :].rearrange("p k (h f) -> p (k h) f", h=8),
                                                         bc(y[:, 1, :].unsqueeze(2), [P, GS * 8, 16]), ALU.mult))
                            link(nc.vector.tensor_tensor(m[:, :, :], m[:, :, :], bc(gcol.unsqueeze(1), [P, GS, D]), ALU.mult))
                            link(nc.vector.tensor_tensor(sq[:, :, :], m[:, :, :], bc(btcol.unsqueeze(1), [P, GS, D]), ALU.add))
                            ve.sem_inc(s_lk, 1)
                            ve.wait_ge(s_act, 2 * n + 2)
                            ve.sem_inc(s_val, 1)
                        ve.wait_ge(s_sum, n + 1)
                        if is_max:
                            for hg in range(HG):
                                mm = nc.vector.tensor_reduce(mx[:, hg, :], pm[hg][:, :, :], AX.X, ALU.max)
                            link(mm)
                            for k in range(GS):
                                v = bucket(k)
                                dst = MX[:, :, bass.ds(v, 1)].rearrange("p g a -> p (g a)")
                                link(nc.vector.tensor_tensor(dst, dst, mx[:, 0:HG, k], ALU.max))
                        else:
                            for k in range(GS):
                                v = bucket(k)
                                if targets:
                                    for j, t in enumerate(targets):
                                        dst = t[:, bass.ds(v * BN, BN)]
                                        link(nc.vector.tensor_tensor(dst, dst, psum[:, k, j, :], ALU.add))
                                    continue
                                dst = K.acc[:, 0:NS, bass.ds(v * BN, BN)]
                                link(nc.vector.tensor_tensor(dst, dst, psum[:, k, 0:NS, :], ALU.add))
                        if kind == "logits":
                            ve.wait_ge(s_lg[g], i * 16 + 16)
                        if store is not None:
                            ve.wait_ge(s_kept[g], i * 16 + 16)
                        ve.sem_inc(s_free, 1)
                    assert link.k == per * RING, (kind, link.k)


@phase
def bucket_pass(nc, B, K, kind, gather=None, gw=0, linear=None, lw=0, store=None, tab=None, tw=0, ts=0,
                static=None, gcol=None, btcol=None, MX=None, heads=0, LG=None, tab3=None, attr=None):
    is_max = kind in ("gatmax", "logits")
    soft = kind in ("gat", "attn")
    uses_T = wide = kind in ("conv", "prod", "logits")
    NS = 2 if kind in ("gat", "gatmax", "attn") else 1
    adds = kind != "logits"
    HG = heads // 4 if heads else 0
    W = gw or lw
    h = {"gat": 4, "attn": 8}.get(kind, 0)
    units = [(k, min(k + 4, MG)) for k in range(0, MG, 4)]
    NU = len(units)
    NM = 2 if (NU * HG) % 3 else 3
    k3 = MG // 3 * 3
    lag = 2 if kind == "conv" else 1
    rowinc = 16 * MG if gw else 16
    s_idx = [B.sem("indices_read") for _ in range(2)]
    s_t = [B.sem("operand_read") for _ in range(2)]
    s_rows = [B.sem("rows_arrived") for _ in range(2)]
    s_at = [B.sem("attributes_read") for _ in range(2)]
    s_kept = [B.sem("rows_kept") for _ in range(2)]
    s_rfree, s_tfree, s_go = B.sem("rows_free"), B.sem("operand_free"), B.sem("pool_go")
    s_exp, s_efree = B.sem("expanded"), B.sem("expanded_free")
    s_va = B.sem("vector_chain")
    s_sq, s_pre, s_val = B.sem("squared"), B.sem("before_activation"), B.sem("values_ready")
    s_w, s_oh, s_sum, s_done = B.sem("weights_made"), B.sem("onehot_made"), B.sem("summed"), B.sem("sums_kept")
    s_tt, s_tc, s_lfree = B.sem("logits_transposed"), B.sem("logits_copied"), B.sem("complement_free")
    s_lt = [B.sem("complement_read") for _ in range(2)]
    s_spl = B.sem("logits_split")
    s_pm, s_mr, s_lk = B.sem("logits_spread"), B.sem("maxima_taken"), B.sem("logits_kept")
    with ExitStack() as ph:
        rows = B.sb("rows", [P, 2, MG, W], F32, ph)
        idx = B.sb("idx", [P, 2, MG], I32, ph) if gw else None
        T = B.sb("T", [TR, 2, MW], F32, ph) if uses_T else B.sb("Tb", [BN, 2, MW], BF16, ph) if soft else None
        oh = B.sb("oh", [P, 2, MG, BN], F32, ph) if adds else None
        at_rows = B.sb("attributes", [P, 2, MG, D], F32, ph) if attr else None
        nm = 1 if kind == "logits" else 2
        m = B.sb("m", [P, nm, MG, D], F32, ph) if kind in ("gat", "attn", "conv", "prod", "logits") else None
        sq = B.sb("sq", [P, 2, MG, D], F32, ph) if kind == "conv" else None
        y = B.sb("y", [P, 3, MG * 8], F32, ph) if kind == "conv" else None
        w = B.sb("w", [P, 2, MG, 8], F32, ph) if soft or is_max else None
        z = B.sb("z", [P, 2, MG, 8], F32, ph) if soft or kind == "logits" else None
        u = B.sb("u", [P, 2, MG, 4], F32, ph) if kind == "gat" else None
        w3 = B.sb("logit_parts", [P, 2, MG, 3 * heads], BF16, ph) if is_max else None
        rest = B.sb("rest", [P, MG, heads], F32, ph) if is_max else None
        LT = B.sb("logits_and_complement", [TR, 2, MW], BF16, ph) if is_max else None
        mx = B.sb("slot_maxima", [P, 2, HG, MG], F32, ph) if is_max else None
        oh5 = B.sb("bucket_counts", [P, 2, GB, BN], F32, ph) if attr else None
        big = [B.ps("expanded", [P, 12, D], ph) for _ in range(2)] if kind in ("conv", "prod") else None
        qe = B.ps("query_and_edge", [P, 4, 512], ph) if kind == "logits" else None
        pl = [B.ps("edge_logits", [P, MG, 8], ph) for _ in range(2)] if soft else None
        pt = B.ps("logits_T", [TR, 512], ph) if is_max else None
        pm = [B.ps("spread", [P, 4, P], ph) for _ in range(NM)] if is_max else None
        psum = [B.ps("sums", [P, NS, GB, BN], ph) for _ in range(2)] if adds else None
        block = ph.enter_context(nc.Block())
        ne = 1 if kind == "logits" else 2

        def nothing(n, g, r):
            pass

        @block.sync
        def _(sp):
            def load(n, g, r):
                if gw:
                    if not isinstance(n, int) or n >= 2:
                        sp.wait_ge(s_rows[g], r * rowinc)
                    sp.dma_start(idx[:, g, :], K.reg_m.src[:, span(n, MG)]).then_inc(s_idx[g], 16)
                else:
                    sp.wait_ge(s_rfree, n + 1)
                    sp.dma_start(rows[:, g, :, :], linear[:, span(n, MG), 0:W]).then_inc(s_rows[g], 16)
                if uses_T or soft:
                    sp.wait_ge(s_tfree, n + 1)
                    t = K.reg_m.t[span(n, 1), :, :] if uses_T else K.reg_m.tb[span(n, 1), 0:BN, :]
                    sp.dma_start(T[:, g, :], t.rearrange("a r c -> (a r) c")).then_inc(s_t[g], 16)

            def load_later(n, g, r):
                if attr:
                    sp.wait_ge(s_done, n + 1)
                    sp.dma_start(at_rows[:, g, :, :], attr[0][:, span(n, MG), 0:D]).then_inc(s_at[g], 16)
                if is_max:
                    sp.wait_ge(s_lfree, n + 1)
                    sp.dma_start(LT[0:64, g, :], K.reg_m.tb[span(n, 1), :, :].rearrange("a r c -> (a r) c")).then_inc(s_lt[g], 16)

            pipelined(sp, load, load_later)

        if gw:
            @block.gpsimd
            def _(po):
                def fetch(n, g, r):
                    po.wait_ge(s_idx[g], r * 16 + 16)
                    po.wait_ge(s_rfree, n + 1)
                    po.sem_inc(s_go, 1)
                    for k in range(MG):
                        nc.gpsimd.indirect_dma_start(
                            out=rows[:, g, k, :], out_offset=None, in_=gather,
                            in_offset=bass.IndirectOffsetOnAxis(ap=idx[:, g, k:k + 1], axis=0)).then_inc(s_rows[g], 16)

                pipelined(po, fetch, nothing)

        @block.tensor
        def _(pe):
            def expand(n, g, r, slots=(0, MG)):
                if slots[0] == 0:
                    pe.wait_ge(s_t[g], r * 16 + 16)
                    pe.wait_ge(s_efree, n + 1)
                if kind == "conv":
                    pe.wait_ge(s_rows[g], r * rowinc + rowinc)
                    for c in range(0, MG, 4):
                        c1 = min(MG, c + 4)
                        nc.tensor.matmul(big[g][:, c:c1, :].rearrange("p k d -> p (k d)"), K.ident[:, :],
                                         rows[:, g, c:c1, :].rearrange("p k d -> p (k d)"), start=True,
                                         stop=True, skip_group_check=True)
                for k in range(*slots):
                    t = T[:, g, k * P:(k + 1) * P]
                    b = n * GB + k // CAPS
                    if soft:
                        for j in range(3):
                            mm = nc.tensor.matmul(pl[g][:, k, :], t, tab3[:, j, span(b, tw)], start=j == 0,
                                                  stop=j == 2, skip_group_check=True)
                        continue
                    if kind == "prod":
                        o, a = big[g][:, k, :], static[:, :]
                    elif kind == "conv":
                        o, a = big[g][:, k, :], tab[:, at(b * ts, D)]
                    else:
                        o, a = qe[:, k // 3, (k % 3) * ts:(k % 3) * ts + ts], tab[:, at(b * ts, ts)]
                    mm = nc.tensor.matmul(o, t, a, start=kind != "conv", stop=True, skip_group_check=True)
                if slots[1] == MG:
                    mm.then_inc(s_exp, 1)

            def sums(n, g, r):
                if kind == "sum":
                    pe.wait_ge(s_rows[g], r * rowinc + rowinc)
                    pe.wait_ge(s_oh, n + 1)
                elif attr:
                    pe.wait_ge(s_at[g], r * 16 + 16)
                    pe.wait_ge(s_oh, n + 1)
                else:
                    pe.wait_ge(s_val, n + 1)
                for b in range(GB):
                    for s in range(NS):
                        for j in range(CAPS):
                            k = b * CAPS + j
                            if attr and s == 1:
                                if j == 0:
                                    mm = nc.tensor.matmul(psum[g][:, s, b, :], K.ones[:, :], oh5[:, g, b, :],
                                                          start=True, stop=True)
                                continue
                            if s == 0:
                                a = {"sum": rows, "gatmax": at_rows}.get(kind, m)[:, g, k, 0:D]
                            else:
                                a = w[:, g, k, 0:h]
                            mm = nc.tensor.matmul(psum[g][0:a.shape[1], s, b, :], a, oh[:, g, k, :],
                                                  start=j == 0, stop=j == CAPS - 1)
                mm.then_inc(s_sum, 1)

            def spread(n, g, r, expanding=None):
                pe.wait_ge(s_spl, n + 1)
                for u in range(NU + 1):
                    if u < NU:
                        pe.wait_ge(s_tc, n * NU + u + 1)
                        for k in range(*units[u]):
                            j = k - units[u][0]
                            mm = nc.tensor.matmul(pt[64:64 + 3 * heads, j * P:(j + 1) * P], w3[:, g, k, :],
                                                  K.identb[:, :], start=True, stop=True, skip_group_check=True)
                        mm.then_inc(s_tt, 1)
                    if u == 0:
                        pe.wait_ge(s_lt[g], r * 16 + 16)
                        continue
                    k0, k1 = units[u - 1]
                    pe.wait_ge(s_tc, n * NU + u + 1)
                    for hg in range(HG):
                        q = (u - 1) * HG + hg
                        if expanding and q == NM:
                            expand(*expanding, (0, CAPS))
                        pe.wait_ge(s_mr, n * (NU * HG) + q + 1)
                        nc.tensor.matmul(pm[q % NM][:, 0:k1 - k0, :].rearrange("p k e -> p (k e)"),
                                         K.spread[heads][0:64 + 3 * heads, hg * P:(hg + 1) * P],
                                         LT[0:64 + 3 * heads, g, k0 * P:k1 * P], start=True, stop=True).then_inc(s_pm, 1)
                if expanding:
                    expand(*expanding, (CAPS, MG))

            if kind == "sum":
                pipelined(pe, sums_free(pe, sums, s_done), nothing)
            elif kind == "gatmax":
                pipelined(pe, sums_free(pe, sums, s_done), spread)
            elif kind == "logits":
                expand(0, 0, 0)
                expand(1, 1, 0)
                with pe.Fori(0, MGROUPS // 2 - 1) as i:
                    spread(i * 2, 0, i, (i * 2 + 2, 0, i + 1))
                    spread(i * 2 + 1, 1, i, (i * 2 + 3, 1, i + 1))
                spread(MGROUPS - 2, 0, MGROUPS // 2 - 1)
                spread(MGROUPS - 1, 1, MGROUPS // 2 - 1)
            else:
                pipelined(pe, expand, sums_free(pe, sums, s_done), lag)

        @block.scalar
        def _(ac):
            def keep_rows(n, g, r):
                ac.wait_ge(s_rows[g], r * rowinc + rowinc)
                c0, c1, dram = store
                ac.dma_start(dram[:, span(n, MG), :], rows[:, g, :, c0:c1]).then_inc(s_kept[g], 16)

            def copy_T(n, g, r):
                for u, (k0, k1) in enumerate(units):
                    ac.wait_ge(s_tt, n * NU + u + 1)
                    nc.scalar.copy(LT[64:64 + 3 * heads, g, k0 * P:k1 * P],
                                   pt[64:64 + 3 * heads, 0:(k1 - k0) * P]).then_inc(s_tc, 1)

            def keep_sums(n, g, r):
                ac.wait_ge(s_sum, n + 1)
                if attr:
                    for j in range(2):
                        o = nc.scalar.copy(attr[1 + j][:, span(n, GB * BN)], psum[g][:, j, :, :].rearrange("p b n -> p (b n)"))
                elif kind in ("gat", "attn"):
                    nc.scalar.copy(K.acc[0:h, 1, span(n, GB * BN)], psum[g][0:h, 1, :, :].rearrange("p b n -> p (b n)"))
                    o = nc.scalar.copy(K.acc[:, 0, span(n, GB * BN)], psum[g][:, 0, :, :].rearrange("p b n -> p (b n)"))
                else:
                    o = nc.scalar.copy(K.acc[:, 0:NS, span(n, GB * BN)],
                                       psum[g][:, :, :, :].rearrange("p s b n -> p s (b n)"))
                o.then_inc(s_done, 1)

            def silu(n, g):
                ac.wait_ge(s_pre, n + 1)
                nc.scalar.activation(m[:, g, :, :], m[:, g, :, :], ACT.Silu).then_inc(s_val, 1)

            def first(n, g, r):
                if store is not None:
                    keep_rows(n, g, r)
                if kind in ("sum", "gatmax"):
                    keep_sums(n, g, r)
                if kind == "conv":
                    ac.wait_ge(s_exp, n + 1)
                    nc.scalar.activation(sq[:, g, :, :], big[g][:, 0:MG, :], ACT.Square).then_inc(s_sq, 1)
                    if not isinstance(n, int) or n > 0:
                        silu(n - 1, 1 - g)
                if soft:
                    ac.wait_ge(s_pre, n + 1)
                    nc.scalar.activation(w[:, g, :, 0:h], z[:, g, :, 0:h], ACT.Exp).then_inc(s_w, 1)

            def second(n, g, r):
                if kind == "conv" and isinstance(n, int) and n == MGROUPS - lag:
                    silu(MGROUPS - 1, (MGROUPS - 1) % 2)
                if kind == "logits":
                    ac.wait_ge(s_val, n + 1)
                    nc.scalar.copy(LG[:, span(n, MG * 8)], w[:, g, :, :].rearrange("p k h -> p (k h)"))
                    copy_T(n, g, r)
                elif kind == "gatmax":
                    copy_T(n, g, r)
                elif kind != "sum":
                    keep_sums(n, g, r)

            ac.sem_inc(s_tc, 1)
            pipelined(ac, first, second, lag)

        per_a = {"conv": 15, "gat": 4, "attn": 2, "prod": 1, "logits": 9 if MG % 3 else 7, "gatmax": 5}.get(kind, 0)

        @block.vector
        def _(ve):
            ve.sem_inc(s_rfree, 2)
            ve.sem_inc(s_tfree, 2)
            ve.sem_inc(s_lfree, 2)
            ve.sem_inc(s_done, 2)
            ve.sem_inc(s_efree, ne)
            ve.sem_inc(s_mr, NM)

            def onehot(n, g):
                ve.wait_ge(s_done, n + 1)
                return nc.vector.tensor_tensor(oh[:, g, :, :], bc(K.iota[:, 0:BN].unsqueeze(1), [P, MG, BN]),
                                               bc(K.reg_m.dls[:, span(n, MG)].unsqueeze(2), [P, MG, BN]), ALU.is_equal)

            def maxima(n, g):
                for u, (k0, k1) in enumerate(units):
                    for hg in range(HG):
                        q = u * HG + hg
                        ve.wait_ge(s_pm, n * (NU * HG) + q + 1)
                        nc.vector.tensor_reduce(mx[:, g, hg, k0:k1], pm[q % NM][:, 0:k1 - k0, :], AX.X, ALU.max).then_inc(s_mr, 1)
                ve.wait_ge(s_mr, n * (NU * HG) + NU * HG + NM)
                nc.vector.tensor_reduce(MX[:, :, span(n, GB)], mx[:, g, :, :].rearrange("p a (b j) -> p a b j", b=GB),
                                        AX.X, ALU.max)

            def split(link, a, g):
                part = lambda j: w3[:, g, :, j * heads:(j + 1) * heads]
                link(nc.vector.tensor_copy(part(0), a))
                link(nc.vector.tensor_tensor(rest[:, :, :], a, part(0), ALU.subtract))
                link(nc.vector.tensor_copy(part(1), rest[:, :, :]))
                link(nc.vector.tensor_tensor(part(2), rest[:, :, :], part(1), ALU.subtract))
                ve.sem_inc(s_spl, 1)

            def first(n, g, r):
                link = Chain(ve, s_va, n * per_a)
                groups = lambda t: t.rearrange("p k (h f) -> p (k h) f", h=8)
                if kind == "sum":
                    onehot(n, g).then_inc(s_oh, 1)
                if attr:
                    link(onehot(n, g))
                    nc.vector.tensor_reduce(oh5[:, g, :, :], oh[:, g, :, :].rearrange("p (b j) n -> p b n j", b=GB),
                                            AX.X, ALU.add).then_inc(s_oh, 1)
                if kind == "sum":
                    ve.wait_ge(s_sum, n + 1)
                    ve.sem_inc(s_rfree, 1)
                if kind == "gatmax":
                    ve.wait_ge(s_rows[g], r * rowinc + rowinc)
                    split(link, rows[:, g, :, D:D + 4], g)
                    ve.wait_ge(s_kept[g], r * 16 + 16)
                    ve.sem_inc(s_rfree, 1)
                if soft:
                    onehot(n, g)
                    ve.wait_ge(s_exp, n + 1)
                    ve.wait_ge(s_rows[g], r * rowinc + rowinc)
                    if kind == "gat":
                        link(nc.vector.tensor_tensor(u[:, g, :, :], rows[:, g, :, D:D + 4], pl[g][:, :, 0:4], ALU.add))
                        link(nc.vector.scalar_tensor_tensor(out=u[:, g, :, :], in0=u[:, g, :, :], scalar=0.2,
                                                            in1=u[:, g, :, :], op0=ALU.mult, op1=ALU.max))
                        link(nc.vector.tensor_tensor(z[:, g, :, 0:4], u[:, g, :, :], pl[g][:, :, 4:8], ALU.subtract))
                    else:
                        link(nc.vector.tensor_tensor(z[:, g, :, :],
                                                     LG[:, span(n, MG * 8)].rearrange("p (k h) -> p k h", h=8),
                                                     pl[g][:, :, :], ALU.subtract))
                    ve.sem_inc(s_pre, 1)
                    ve.sem_inc(s_efree, 1)
                    ve.sem_inc(s_tfree, 1)
                    ve.wait_ge(s_w, n + 1)
                    link(nc.vector.tensor_tensor(m[:, g, :, :].rearrange("p k (h f) -> p k h f", h=h),
                                                 rows[:, g, :, 0:D].rearrange("p k (h f) -> p k h f", h=h),
                                                 bc(w[:, g, :, 0:h].unsqueeze(3), [P, MG, h, D // h]), ALU.mult))
                    ve.sem_inc(s_val, 1)
                    ve.sem_inc(s_rfree, 1)
                if kind == "prod":
                    onehot(n, g)
                    ve.wait_ge(s_exp, n + 1)
                    ve.wait_ge(s_rows[g], r * rowinc + rowinc)
                    link(nc.vector.tensor_tensor(m[:, g, :, :], rows[:, g, :, :], big[g][:, 0:MG, :], ALU.mult))
                    for s in (s_val, s_efree, s_tfree, s_rfree):
                        ve.sem_inc(s, 1)
                if kind == "logits":
                    ve.wait_ge(s_exp, n + 1)
                    ve.sem_inc(s_tfree, 1)
                    ve.wait_ge(s_rows[g], r * rowinc + rowinc)
                    for k0, k1, c in [(0, k3, 3)] + ([(k3, MG, MG - k3)] if k3 < MG else []):
                        banks = qe[:, k0 // 3:-(-k1 // 3), 0:c * ts].rearrange("p b (s c) -> p b s c", s=c)
                        slots = lambda t: t.rearrange("p (b s) c -> p b s c", s=c)
                        link(nc.vector.tensor_tensor(slots(m[:, 0, k0:k1, :]), slots(rows[:, g, k0:k1, 0:D]),
                                                     banks[:, :, :, 0:D], ALU.mult))
                    link(nc.vector.tensor_reduce(z[:, g, :, :].rearrange("p k h -> p (k h)"), groups(m[:, 0, :, :]),
                                                 AX.X, ALU.add))
                    for k0, k1, c in [(0, k3, 3)] + ([(k3, MG, MG - k3)] if k3 < MG else []):
                        banks = qe[:, k0 // 3:-(-k1 // 3), 0:c * ts].rearrange("p b (s c) -> p b s c", s=c)
                        slots = lambda t: t.rearrange("p (b s) c -> p b s c", s=c)
                        link(nc.vector.tensor_tensor(slots(w[:, g, k0:k1, :]), slots(z[:, g, k0:k1, :]),
                                                     banks[:, :, :, D:ts], ALU.add))
                    ve.sem_inc(s_val, 1)
                    ve.sem_inc(s_efree, 1)
                    split(link, w[:, g, :, :], g)
                    ve.wait_ge(s_kept[g], r * 16 + 16)
                    ve.sem_inc(s_rfree, 1)
                if kind == "conv":
                    ve.wait_ge(s_exp, n + 1)
                    ve.sem_inc(s_rfree, 1)
                    ve.sem_inc(s_tfree, 1)
                    ve.wait_ge(s_sq, n + 1)
                    link(nc.vector.tensor_reduce(y[:, 0, :], groups(sq[:, g, :, :]), AX.X, ALU.add))
                    link(nc.vector.tensor_scalar(y[:, 0, :], y[:, 0, :], 1.0 / 16, EPS, ALU.mult, ALU.add))
                    link(nc.vector.tensor_scalar(y[:, 1, :].bitcast(I32), y[:, 0, :].bitcast(I32), -0.5,
                                                 float(0x5f3759df), ALU.mult, ALU.add))
                    for _ in range(3):
                        link(nc.vector.scalar_tensor_tensor(out=y[:, 2, :], in0=y[:, 1, :], scalar=-0.5,
                                                            in1=y[:, 0, :], op0=ALU.mult, op1=ALU.mult))
                        link(nc.vector.tensor_tensor(y[:, 2, :], y[:, 2, :], y[:, 1, :], ALU.mult))
                        link(nc.vector.scalar_tensor_tensor(out=y[:, 1, :], in0=y[:, 2, :], scalar=1.5,
                                                            in1=y[:, 1, :], op0=ALU.add, op1=ALU.mult))
                    onehot(n, g)
                    link(nc.vector.tensor_tensor(groups(m[:, g, :, :]), groups(big[g][:, 0:MG, :]),
                                                 bc(y[:, 1, :].unsqueeze(2), [P, MG * 8, 16]), ALU.mult))
                    ve.sem_inc(s_efree, 1)
                    link(nc.vector.tensor_tensor(m[:, g, :, :], m[:, g, :, :], bc(gcol.unsqueeze(1), [P, MG, D]), ALU.mult))
                    link(nc.vector.tensor_tensor(m[:, g, :, :], m[:, g, :, :], bc(btcol.unsqueeze(1), [P, MG, D]), ALU.add))
                    ve.sem_inc(s_pre, 1)
                assert link.k == per_a, (kind, link.k)

            def second(n, g, r):
                if is_max:
                    maxima(n, g)
                    ve.sem_inc(s_lfree, 1)

            pipelined(ve, first, second)


def sums_free(eng, sums, s_done):
    def step(n, g, r):
        eng.wait_ge(s_done, n + 1)
        sums(n, g, r)
    return step



def bucket_maxima(nc, B, K, MX, groups, ps, pe):
    for hg in range(groups):
        for h in range(4):
            m = nc.tensor.matmul(ps[hg][:, h * NB:(h + 1) * NB], K.ident[:, 32 * h:32 * h + 32], MX[:, hg, :],
                                 start=True, stop=True, skip_group_check=True)
    return m


def split_table(nc, link, tab8, tab3, rest):
    link(nc.vector.tensor_copy(tab3[:, 0, :], tab8[:, :]))
    link(nc.vector.tensor_tensor(rest[:, :], tab8[:, :], tab3[:, 0, :], ALU.subtract))
    link(nc.vector.tensor_copy(tab3[:, 1, :], rest[:, :]))
    link(nc.vector.tensor_tensor(tab3[:, 2, :], rest[:, :], tab3[:, 1, :], ALU.subtract))


@phase
def gat_tables(nc, B, K, T0, MX, tab8, tab3, u4):
    s_ld, s_mm, s_v, s_e = B.sem("logits_loaded"), B.sem("maxima_spread"), B.sem("table_chain"), B.sem("own_weight")
    s_ws, s_cp = B.sem("weight_spread"), B.sem("weight_copied")
    per = 512 // BN
    banks = -(-NB // per)
    with ExitStack() as ph:
        a = B.sb("a", [BN, NB, 8], F32, ph)
        t = B.sb("t", [BN, NB, 4], F32, ph)
        rest = B.sb("rest", [BN, NB * 8], F32, ph)
        u = B.sb("u", [BN, NB, 4], F32, ph)
        ps = [B.ps("ps", [BN, 512], ph)]
        pw = [B.ps("pw", [4, 512], ph) for _ in range(2)]
        block = ph.enter_context(nc.Block())
        tab = tab8[:, :].rearrange("p (b c) -> p b c", c=8)

        @block.sync
        def _(sp):
            sp.dma_start(a[:, :, :], T0.rearrange("(b p) d -> p b d", p=BN)[:, :, D:D + 8]).then_inc(s_ld, 16)

        @block.tensor
        def _(pe):
            bucket_maxima(nc, B, K, MX, 1, ps, pe).then_inc(s_mm, 1)
            pe.wait_ge(s_e, 1)
            for c in range(banks):
                if c >= 2:
                    pe.wait_ge(s_cp, c - 1)
                for b in range(c * per, min(NB, (c + 1) * per)):
                    m = nc.tensor.matmul(pw[c % 2][:, (b - c * per) * BN:(b - c * per + 1) * BN],
                                         u[:, b, :], K.ident[0:BN, 0:BN],
                                         start=True, stop=True, skip_group_check=True)
                m.then_inc(s_ws, 1)

        @block.scalar
        def _(ac):
            ac.wait_ge(s_v, 8)
            nc.scalar.activation(u[:, :, :], u[:, :, :], ACT.Exp).then_inc(s_e, 1)

        @block.vector
        def _(ve):
            link = Chain(ve, s_v)
            ve.wait_ge(s_ld, 16)
            ve.wait_ge(s_mm, 1)
            mxv = ps[0][:, 0:4 * NB].rearrange("p (h b) -> p b h", h=4)
            link(nc.vector.tensor_tensor(t[:, :, :], a[:, :, 0:4], mxv, ALU.max))
            link(nc.vector.tensor_tensor(t[:, :, :], t[:, :, :], a[:, :, 4:8], ALU.add))
            link(nc.vector.scalar_tensor_tensor(out=tab[:, :, 4:8], in0=t[:, :, :], scalar=0.2, in1=t[:, :, :],
                                                op0=ALU.mult, op1=ALU.max))
            link(nc.vector.tensor_copy(tab[:, :, 0:4], a[:, :, 4:8]))
            link(nc.vector.tensor_tensor(t[:, :, :], a[:, :, 0:4], a[:, :, 4:8], ALU.add))
            link(nc.vector.tensor_scalar(u[:, :, :], t[:, :, :], 0.2, None, ALU.mult))
            link(nc.vector.tensor_tensor(u[:, :, :], u[:, :, :], t[:, :, :], ALU.max))
            link(nc.vector.tensor_tensor(u[:, :, :], u[:, :, :], tab[:, :, 4:8], ALU.subtract))
            split_table(nc, link, tab8, tab3, rest)
            for c in range(banks):
                w = min(NP, (c + 1) * 512) - c * 512
                ve.wait_ge(s_ws, c + 1)
                nc.vector.tensor_copy(u4[:, c * 512:c * 512 + w], pw[c % 2][:, 0:w]).then_inc(s_cp, 1)


@phase
def attn_table(nc, B, K, MX, tab8, tab3):
    s_mm, s_v = B.sem("maxima_spread"), B.sem("table_chain")
    with ExitStack() as ph:
        ps = [B.ps("ps", [BN, 512], ph) for _ in range(2)]
        rest = B.sb("rest", [BN, NB * 8], F32, ph)
        block = ph.enter_context(nc.Block())

        @block.tensor
        def _(pe):
            bucket_maxima(nc, B, K, MX, 2, ps, pe).then_inc(s_mm, 1)

        @block.vector
        def _(ve):
            ve.wait_ge(s_mm, 1)
            tab = tab8[:, :].rearrange("p (b c) -> p b c", c=8)
            for hg in range(2):
                nc.vector.tensor_copy(tab[:, :, 4 * hg:4 * hg + 4],
                                      ps[hg][:, 0:4 * NB].rearrange("p (h b) -> p b h", h=4)).then_inc(s_v, 1)
            ve.wait_ge(s_v, 2)
            split_table(nc, Chain(ve, s_v, 2), tab8, tab3, rest)


@phase
def batch_norm(nc, B, K):
    s_v, s_r = B.sem("stat_chain"), B.sem("root")
    O = K.acc[:, 0, 0:N]
    with ExitStack() as ph:
        st = B.sb("st", [P, 4], F32, ph)
        block = ph.enter_context(nc.Block())

        @block.scalar
        def _(ac):
            ac.wait_ge(s_v, 6)
            nc.scalar.activation(st[:, 2:3], st[:, 1:2], ACT.Sqrt).then_inc(s_r, 1)

        @block.vector
        def _(ve):
            link = Chain(ve, s_v)
            link(nc.vector.tensor_reduce(st[:, 0:1], O, AX.X, ALU.add))
            link(nc.vector.tensor_scalar(st[:, 0:1], st[:, 0:1], 1.0 / N, None, ALU.mult))
            link(nc.vector.tensor_scalar(O, O, st[:, 0:1], None, ALU.subtract))
            link(nc.vector.tensor_tensor(K.acc[:, 1, 0:N], O, O, ALU.mult))
            link(nc.vector.tensor_reduce(st[:, 1:2], K.acc[:, 1, 0:N], AX.X, ALU.add))
            link(nc.vector.tensor_scalar(st[:, 1:2], st[:, 1:2], 1.0 / N, EPS, ALU.mult, ALU.add))
            ve.wait_ge(s_r, 1)
            link(nc.vector.reciprocal(st[:, 3:4], st[:, 2:3]))
            link(nc.vector.tensor_tensor(st[:, 3:4], st[:, 3:4], K.c["L0_gnn_gamma"][:, :], ALU.mult))
            link(nc.vector.tensor_scalar(O, O, st[:, 3:4], K.c["L0_gnn_beta"][:, :], ALU.mult, ALU.add))
            link(nc.vector.tensor_tensor(K.X[:, 0:N], K.X[:, 0:N], O, ALU.add))


@phase
def store_x(nc, B, K, out):
    s_tr, s_cp, s_st = B.sem("transposed"), B.sem("copied"), B.sem("result_stored")
    with ExitStack() as ph:
        xn = B.sb("xn", [P, TILES, D], F32, ph)
        ps = [B.ps("ps", [P, P], ph) for _ in range(2)]
        block = ph.enter_context(nc.Block())
        full, rest = N // P, N % P

        @block.tensor
        def _(pe):
            for t in range(TILES):
                if t >= 2:
                    pe.wait_ge(s_cp, t - 1)
                nc.tensor.transpose(ps[t % 2][:, :], K.X[:, t * P:(t + 1) * P], K.ident[:, :]).then_inc(s_tr, 1)

        @block.vector
        def _(ve):
            for t in range(TILES):
                ve.wait_ge(s_tr, t + 1)
                nc.vector.tensor_copy(xn[:, t, :], ps[t % 2][:, :]).then_inc(s_cp, 1)

        @block.sync
        def _(sp):
            sp.wait_ge(s_cp, TILES)
            sp.dma_start(out[0:full * P, :].rearrange("(t p) d -> p t d", p=P), xn[:, 0:full, :]).then_inc(s_st, 16)
            sp.dma_start(out[full * P:N, :], xn[0:rest, full, :]).then_inc(s_st, 16)
            sp.wait_ge(s_st, 32)


def program(nc, A, out):
    with ExitStack() as ctx:
        B = Build(nc, ctx)

        class K:
            pass

        K.rec = B.dram("records", [(MSLOTS + SLOTS) * P, REC])
        K.bucket_dram = B.dram("slot_buckets", [512], I32)
        K.X = B.sb("X", [P, NP])
        K.H = B.sb("H", [P, NP])
        K.acc = B.sb("acc", [P, 2, NP])
        K.cnt = B.sb("cnt", [P, NP])
        constants(nc, B, A, K)
        rank_edges(nc, B, A, K)
        scatter_records(nc, B, A, K)

        class Region:
            def __init__(self, over, slots, groups, rec):
                self.over, self.slots, self.groups = over, slots, groups
                self.rec = rec.rearrange("(s p) w -> p s w", p=P)
                self.src = B.dram("sources", [P, slots * groups], I32)
                self.t = B.dram("operands", [groups, TR, slots * P])
                self.tb = B.dram("onehot_operands", [groups, 64, slots * P], BF16)
                self.dls = B.sb("dst_local", [P, slots * groups])

            def rows(self, width):
                return B.dram("slot_rows", [P, self.slots * self.groups, width])

        K.reg_m = Region(False, MG, MGROUPS, K.rec[0:OVER, :])
        K.reg_o = Region(True, GS, GROUPS, K.rec[OVER:, :])
        make_operands(nc, B, A, K, K.reg_m)
        make_operands(nc, B, A, K, K.reg_o)
        load_x(nc, B, A, K)

        def edge_pass(kind, kept=None, LG=None, tab3=None, attr=None, **kw):
            for f, j in ((bucket_pass, 0), (overflow_pass, 1)):
                args = dict(kw)
                if j == 0:
                    args["tab3"], args["attr"] = tab3, attr
                if kept:
                    name, c0, c1, arrays = kept
                    args[name] = arrays[j] if name == "linear" else (c0, c1, arrays[j])
                f(nc, B, K, kind, LG=LG[j] if LG else None, **args)

        V = nc.vector
        acc0, acc1 = K.acc[:, 0, :], K.acc[:, 1, :]

        norm_nodes(nc, B, A, K)
        attributes = ExitStack()
        agg = B.sb("agg", [P, NP], F32, attributes)
        T0 = B.dram("gat_rows", [NP, 136])
        gs = [r.rows(132) for r in (K.reg_m, K.reg_o)]
        project_nodes(nc, B, K, [(K.H, [K.w0[:, :]])], 136, T0)
        with ExitStack() as l0:
            MX = B.sb("MX", [P, 1, NB], F32, l0)
            tab8 = B.sb("tab8", [BN, NB * 8], F32, l0)
            tab3 = B.sb("tab3", [BN, 3, NB * 8], BF16, l0)
            wsf = B.sb("wsf", [P, NP], F32, l0)
            u4 = B.sb("own_weights", [4, NP], F32, l0)
            r4 = B.sb("inverse_sums", [4, NP], F32, l0)
            edge_pass("gatmax", gather=T0, gw=136, kept=("store", 0, 132, gs), MX=MX, heads=4,
                      attr=(K.reg_m.rec, agg, K.cnt))
            overflow_pass(nc, B, K, "attr", linear=K.reg_o.rec, lw=D, targets=[agg, K.cnt])
            gat_tables(nc, B, K, T0, MX, tab8, tab3, u4)
            edge_pass("gat", kept=("linear", 0, 132, gs), lw=132, tab=tab8, tab3=tab3, tw=8, ts=8, heads=4)

            def inverse(link):
                link(V.scalar_tensor_tensor(out=r4[:, :], in0=acc1[0:4, :], scalar=1e-16, in1=u4[:, :],
                                            op0=ALU.add, op1=ALU.add))
                link(V.reciprocal(r4[:, :], r4[:, :]))

            def spread(sl, ps, link):
                link(V.tensor_copy(wsf[:, sl], ps))

            def own(sl, ps, link):
                link(V.tensor_tensor(wsf[:, sl], ps, wsf[:, sl], ALU.mult))
                link(V.tensor_tensor(acc0[:, sl], acc0[:, sl], wsf[:, sl], ALU.add))

            def scale(sl, ps, link):
                link(V.tensor_tensor(acc0[:, sl], acc0[:, sl], ps, ALU.mult))
                link(V.tensor_scalar(acc0[:, sl], acc0[:, sl], K.c["L0_gnn_bias"][:, :], None, ALU.add))

            vector_phase(nc, B, inverse)
            feature_product(nc, B, K, [(K.hs32[0:4, 0, :], u4)], spread, 1)
            feature_product(nc, B, K, [(K.w0[:, 0:D], K.H)], own, 2)
            feature_product(nc, B, K, [(K.hs32[0:4, 0, :], r4)], scale, 2)
        batch_norm(nc, B, K)
        norm_nodes(nc, B, A, K)
        with attributes:
            Y = B.dram("gin_rows", [NP, D])

            def embed(sl, ps, link):
                link(V.scalar_tensor_tensor(out=agg[:, sl], in0=K.cnt[:, sl], scalar=K.c["L1_gnn_be"][:, :], in1=ps,
                                            op0=ALU.mult, op1=ALU.add))

            feature_product(nc, B, K, [(K.w["L1_gnn_We"][:, :], agg)], embed, 1)
            both = [(K.H, [K.w1a[:, :]]), (agg, [K.w1b[:, :]])]
            project_nodes(nc, B, K, both, D, Y)
            edge_pass("sum", gather=Y, gw=D)

            def hidden(sl, ps, link):
                link(V.tensor_tensor(acc0[:, sl], acc0[:, sl], ps, ALU.add))
                link(V.tensor_scalar(acc0[:, sl], acc0[:, sl], K.c["L1_gnn_b1"][:, :], 0.0, ALU.add, ALU.max))

            feature_product(nc, B, K, [(K.w1a[:, :], K.H), (K.w1b[:, :], agg)], hidden, 2)

            def add_out(sl, ps, link):
                link(V.scalar_tensor_tensor(out=K.X[:, sl], in0=ps, scalar=K.c["L1_gnn_b2"][:, :], in1=K.X[:, sl],
                                            op0=ALU.add, op1=ALU.add))

            feature_product(nc, B, K, [(K.w["L1_gnn_W2"][:, :], acc0)], add_out, 1)
        norm_nodes(nc, B, A, K)
        rows_a, rows_b = B.dram("dst_rows", [NP, D]), B.dram("src_rows", [NP, D])
        TW = D + 8
        tab = B.sb("tab", [TR, NB, TW])
        flat = tab[:, :, :].rearrange("p b d -> p (b d)")
        convolutions = ExitStack()
        inv = B.sb("inverse_counts", [P, NP], F32, convolutions)

        def invert(link):
            link(V.tensor_scalar(inv[:, :], K.cnt[:, :], 1.0, None, ALU.max))
            link(V.reciprocal(inv[:, :], inv[:, :]))

        vector_phase(nc, B, invert)
        for i, c in enumerate(("c1", "c2")):
            inp = K.H if i == 0 else acc1
            project_nodes(nc, B, K, [(inp, [K.ca[i][:, :]])], D, rows_a)
            project_nodes(nc, B, K, [(inp, [K.cb[i][:, :]])], D, rows_b)
            load_table(nc, B, rows_a, tab, K.cs[i], i == 0)
            edge_pass("conv", gather=rows_b, gw=D, tab=flat, tw=D, ts=TW, static=K.cs[i], 
                      gcol=K.r[f"L2_gnn_{c}_g"][:, :], btcol=K.r[f"L2_gnn_{c}_bt"][:, :])

            def mean(sl, ps, link):
                link(V.scalar_tensor_tensor(out=acc1[:, sl], in0=K.cnt[:, sl], scalar=K.c[f"L2_gnn_{c}_b2"][:, :],
                                            in1=ps, op0=ALU.mult, op1=ALU.add))
                link(V.tensor_tensor(acc1[:, sl], acc1[:, sl], inv[:, sl], ALU.mult))

            feature_product(nc, B, K, [(K.w[f"L2_gnn_{c}_w2"][:, :], acc0)], mean, 2)
            n = f"L2_gnn_n{i + 1}_"
            group_norm(nc, B, K, acc1, K.c[n + "g"], K.c[n + "b"], ACT.Silu, acc1)
            if i == 0:
                vector_phase(nc, B, lambda link: link(
                    V.tensor_scalar(acc1, acc1, K.tvec[:, :], None, ALU.add)))
            else:
                vector_phase(nc, B, lambda link: link(V.tensor_tensor(K.H[:, :], K.H[:, :], acc1, ALU.add)))
        convolutions.close()
        KV, Q = B.dram("kv_rows", [NP, 2 * D]), rows_a
        vs = [r.rows(D) for r in (K.reg_m, K.reg_o)]
        project_nodes(nc, B, K, [(K.H, [K.w["L2_gnn_kw"][:, :], K.w["L2_gnn_vw"][:, :]])], 2 * D, KV,
                      row=[K.r["L2_gnn_kb"][:, :], K.r["L2_gnn_vb"][:, :]])
        project_nodes(nc, B, K, [(K.H, [K.w["L2_gnn_qw"][:, :]])], D, Q, row=[K.r["L2_gnn_qb"][:, :]], scale=0.25)
        MX = B.sb("MX", [P, 2, NB])
        LG = (B.sb("logits", [P, MSLOTS * 8]), K.reg_o.rows(8))
        load_table(nc, B, Q, tab, K.ew, False)
        edge_pass("logits", gather=KV, gw=2 * D, kept=("store", D, 2 * D, vs), MX=MX, heads=8, LG=LG,
                  tab=flat, tw=D, ts=TW, static=K.ew)
        tab8 = B.sb("tab8", [BN, NB * 8])
        tab3 = B.sb("tab3", [BN, 3, NB * 8], BF16)
        attn_table(nc, B, K, MX, tab8, tab3)
        edge_pass("attn", kept=("linear", 0, D, vs), lw=D, tab=tab8, tab3=tab3, tw=8, ts=8, heads=8, LG=LG)

        def divide(link):
            link(V.tensor_scalar(acc1[0:8, :], acc1[0:8, :], 1e-6, None, ALU.max))
            link(V.reciprocal(acc1[0:8, :], acc1[0:8, :]))

        vector_phase(nc, B, divide)

        def scale8(sl, ps, link):
            link(V.tensor_tensor(acc0[:, sl], acc0[:, sl], ps, ALU.mult))

        feature_product(nc, B, K, [(K.hs16[:, :], acc1[0:8, :])], scale8, 1)

        def attn_out(sl, ps, link):
            link(V.tensor_scalar(acc1[:, sl], ps, K.c["L2_gnn_ob"][:, :], None, ALU.add))

        feature_product(nc, B, K, [(K.w["L2_gnn_ow"][:, :], acc0)], attn_out, 1)
        group_norm(nc, B, K, acc1, K.c["L2_gnn_an_g"], K.c["L2_gnn_an_b"], ACT.Identity, acc1)

        def add_layer(link):
            link(V.tensor_tensor(K.X[:, :], K.X[:, :], K.H[:, :], ALU.add))
            link(V.tensor_tensor(K.X[:, :], K.X[:, :], acc1, ALU.add))

        vector_phase(nc, B, add_layer)
        norm_nodes(nc, B, A, K)
        project_nodes(nc, B, K, [(K.H, [K.w["L3_gnn_W"][:, :]])], D, rows_a)
        edge_pass("prod", gather=rows_a, gw=D, static=K.w3)
        vector_phase(nc, B, lambda link: link(V.scalar_tensor_tensor(
            out=K.X[:, :], in0=acc0, scalar=K.c["L3_gnn_b"][:, :], in1=K.X[:, :], op0=ALU.add, op1=ALU.add)))
        store_x(nc, B, K, out)


def kernel(**inputs):
    import numpy as _np
    import concourse.bacc as _bacc
    from concourse import mybir as _mybir
    from concourse.bass_utils import run_bass_kernel_spmd as _run

    nc = _bacc.Bacc("TRN2", target_bir_lowering=False, num_devices=1)
    arrays, args = {}, {}
    for name, a in inputs.items():
        a = _np.ascontiguousarray(a)
        arrays[f"in_{name}"] = a
        args[name] = nc.dram_tensor(f"in_{name}", a.shape, _mybir.dt.from_np(a.dtype), kind="ExternalInput").ap()
    out = nc.dram_tensor("out_0", (N, D), _mybir.dt.float32, kind="ExternalOutput").ap()
    program(nc, args, out)
    r = _run(nc, [arrays], core_ids=[0])
    return r.results[0]["out_0"]
```
